# Optimizing a Trainium2 kernel written in Bass

```python
import numpy as np
import jax
import jax.numpy as jnp

def _softmax(x, axis=-1):
    return jax.nn.softmax(x, axis=axis)

def _gelu(x):
    return jax.nn.gelu(x, approximate=True)

def _silu(x):
    return jax.nn.silu(x)

def _sigmoid(x):
    return jax.nn.sigmoid(x)

def _layernorm(x, axis=-1, eps=1e-05):
    m = jnp.mean(x, axis=axis, keepdims=True)
    v = jnp.var(x, axis=axis, keepdims=True)
    return (x - m) / jnp.sqrt(v + eps)

def _scatter_add(tgt, idx, src, axis=0):
    return tgt.at[idx].add(src)

def _segment_sum(src, seg, n):
    return jax.ops.segment_sum(src, seg, n)
kernel_name = 'mk_perceiver_d2_seqx_r4_9c1bb4'

def setup_inputs(seed: int=0):
    np.random.seed(seed)
    _w = jnp.asarray

    def _rec_inputs():
        import jax
        import jax.numpy as jnp
        _rk = jax.random.key(seed)
        x = -0.0002928 + 1 * jax.random.normal(jax.random.fold_in(_rk, 1), (1, 256, 512), jnp.float32)
        _lenS = 256 - jax.random.randint(jax.random.fold_in(_rk, 7), (1,), 0, max(1, 256 // 4) + 1, jnp.int32)
        _lenS2 = 4096 - jax.random.randint(jax.random.fold_in(_rk, 8), (1,), 0, max(1, 4096 // 4) + 1, jnp.int32)
        _ctx_2048P = jax.random.normal(jax.random.fold_in(_rk, 11), (1, 16, 512), jnp.float32)
        _ctx_2048c = jax.random.dirichlet(jax.random.fold_in(_rk, 511), 0.3 * jnp.ones((16,), jnp.float32), (1, 4096))
        _ctx_2048t = jnp.einsum('bsk,bkd->bsd', _ctx_2048c, _ctx_2048P)
        _ctx_2048t = _ctx_2048t * jax.lax.rsqrt(jnp.mean(jnp.square(_ctx_2048t)) + 1e-12) * 0.953939
        ctx_2048 = -1.39393e-06 + 0.999914 * (_ctx_2048t + 0.3 * jax.random.normal(jax.random.fold_in(_rk, 611), (1, 4096, 512), jnp.float32))
        _validS = jnp.arange(256)[None, :] < _lenS[:, None]
        _validS2 = jnp.arange(4096)[None, :] < _lenS2[:, None]
        _causal = jnp.tril(jnp.ones((256, 256), dtype=bool))
        mask_BxS2_bk0 = jnp.logical_not(jnp.broadcast_to(_validS2[:, :], (1, 4096)))
        return (x, ctx_2048, mask_BxS2_bk0)
    x, ctx_2048, mask_BxS2_bk0 = _rec_inputs()

    def _L0_xattn_setup():
        import math
        import jax, jax.numpy as jnp
        import numpy as np
        N_HEADS = 16
        key = jax.random.key(seed)
        k1, k2 = jax.random.split(key)
        qkv = jax.random.normal(k1, (2, 256, 512), dtype=jnp.float32)
        y = jax.random.normal(k2, (2, 256, 512), dtype=jnp.float32)
        return {'qkv': qkv, 'y': y}
    _L0_xattn_all = _L0_xattn_setup()
    _L0_xattn_in = {k: v for k, v in _L0_xattn_all.items() if k in ()}
    del _L0_xattn_all

    def _L0_attn_setup():
        import jax, jax.numpy as jnp
        import numpy as np
        D_MODEL = 512
        NUM_HEADS = 16
        THETA = 10000.0

        def _rope(t, cos, sin):
            x_even = t[..., 0::2]
            x_odd = t[..., 1::2]
            rot = jnp.stack((-x_odd, x_even), axis=-1).reshape(t.shape)
            return t * cos + rot * sin
        key = jax.random.key(seed)
        ks = jax.random.split(key, 5)
        bs, S, d = (4, 512, D_MODEL)
        std = (2.0 / (d + d)) ** 0.5
        x = jax.random.normal(ks[0], (bs, S, d), dtype=jnp.float32)
        wq = jax.random.normal(ks[1], (d, d), dtype=jnp.float32) * std
        wk = jax.random.normal(ks[2], (d, d), dtype=jnp.float32) * std
        wv = jax.random.normal(ks[3], (d, d), dtype=jnp.float32) * std
        wo = jax.random.normal(ks[4], (d, d), dtype=jnp.float32) * std
        return {'x': x, 'wq': wq, 'wk': wk, 'wv': wv, 'wo': wo}
    _L0_attn_all = _L0_attn_setup()
    _L0_attn_in = {k: v for k, v in _L0_attn_all.items() if k in ('wq', 'wk', 'wv', 'wo')}
    del _L0_attn_all

    def _L0_ffn_setup():
        import jax, jax.numpy as jnp
        import numpy as np
        B, S, DIM = (4, 128, 512)
        E, INTER = (32, 256)
        G, TOPK_G, TOPK = (8, 4, 6)
        ROUTE_SCALE = 2.5
        SHARED_INTER = 2 * INTER

        def _gate(xf, gate_w):
            scores = jax.nn.sigmoid(xf @ gate_w.T)
            gs = scores.reshape(-1, G, E // G)
            group_scores = gs.max(axis=-1)
            _, gidx = jax.lax.top_k(group_scores, TOPK_G)
            gmask = jnp.any(jnp.arange(G)[None, None, :] == gidx[:, :, None], axis=1)
            masked = jnp.where(gmask[:, :, None], gs, -jnp.inf).reshape(-1, E)
            _, idx = jax.lax.top_k(masked, TOPK)
            w = jnp.take_along_axis(scores, idx, axis=1)
            w = w / jnp.sum(w, axis=-1, keepdims=True) * ROUTE_SCALE
            return (w, idx)
        key = jax.random.key(seed)
        ks = jax.random.split(key, 8)
        sd = 0.02
        return {'x': jax.random.normal(ks[0], (B, S, DIM), jnp.float32), 'gate_w': jax.random.normal(ks[1], (E, DIM), jnp.float32) * sd, 'w11': jax.random.normal(ks[2], (E, INTER, DIM), jnp.float32) * sd, 'w33': jax.random.normal(ks[3], (E, INTER, DIM), jnp.float32) * sd, 'w22': jax.random.normal(ks[4], (E, DIM, INTER), jnp.float32) * sd, 'sw1': jax.random.normal(ks[5], (SHARED_INTER, DIM), jnp.float32) * sd, 'sw2': jax.random.normal(ks[6], (DIM, SHARED_INTER), jnp.float32) * sd, 'sw3': jax.random.normal(ks[7], (SHARED_INTER, DIM), jnp.float32) * sd}
    _L0_ffn_all = _L0_ffn_setup()
    _L0_ffn_in = {k: v for k, v in _L0_ffn_all.items() if k in ('gate_w', 'w11', 'w33', 'w22', 'sw1', 'sw2', 'sw3')}
    del _L0_ffn_all

    def _L1_xattn_setup():
        import jax, jax.numpy as jnp
        import numpy as np
        key = jax.random.key(seed)
        k1, k2, k3 = jax.random.split(key, 3)
        B, S, D, M = (8, 512, 512, 128)
        hidden_states = jax.random.normal(k1, (B, S, D), dtype=jnp.float32)
        memory_tokens = jax.random.normal(k2, (B, M, D), dtype=jnp.float32)
        memory_mask = jax.random.randint(k3, (B, M), 0, 2).astype(jnp.bool_)
        return {'hidden_states': hidden_states, 'memory_tokens': memory_tokens, 'memory_mask': memory_mask}
    _L1_xattn_all = _L1_xattn_setup()
    _L1_xattn_in = {k: v for k, v in _L1_xattn_all.items() if k in ()}
    del _L1_xattn_all

    def _L1_attn_setup():
        import jax, jax.numpy as jnp
        import numpy as np
        HIDDEN = 512
        NUM_HEADS = 32
        HEAD_DIM = 64
        NUM_KV = 8
        GROUP = NUM_HEADS // NUM_KV
        SCALE = HEAD_DIM ** (-0.5)
        ROPE_BASE = 10000.0

        def apply_rope(t):
            S, D = (t.shape[-2], t.shape[-1])
            inv_freq = 1.0 / ROPE_BASE ** (jnp.arange(0, D, 2, dtype=jnp.float32) / D)
            ang = jnp.arange(S, dtype=jnp.float32)[:, None] * inv_freq[None, :]
            cos, sin = (jnp.cos(ang), jnp.sin(ang))
            x1, x2 = (t[..., :D // 2], t[..., D // 2:])
            return jnp.concatenate([x1 * cos - x2 * sin, x2 * cos + x1 * sin], axis=-1)
        key = jax.random.key(seed)
        ks = jax.random.split(key, 10)
        B, S = (2, 512)
        s_in = HIDDEN ** (-0.5)
        s_o = (NUM_HEADS * HEAD_DIM) ** (-0.5)
        return {'x': jax.random.normal(ks[0], (B, S, HIDDEN), jnp.float32), 'Wq': jax.random.normal(ks[1], (NUM_HEADS * HEAD_DIM, HIDDEN), jnp.float32) * s_in, 'bq': jnp.zeros((NUM_HEADS * HEAD_DIM,), jnp.float32), 'Wk': jax.random.normal(ks[2], (NUM_KV * HEAD_DIM, HIDDEN), jnp.float32) * s_in, 'bk': jnp.zeros((NUM_KV * HEAD_DIM,), jnp.float32), 'Wv': jax.random.normal(ks[3], (NUM_KV * HEAD_DIM, HIDDEN), jnp.float32) * s_in, 'bv': jnp.zeros((NUM_KV * HEAD_DIM,), jnp.float32), 'Wo': jax.random.normal(ks[4], (HIDDEN, NUM_HEADS * HEAD_DIM), jnp.float32) * s_o, 'bo': jnp.zeros((HIDDEN,), jnp.float32), 'key_weights': jax.random.normal(ks[5], (NUM_HEADS,), jnp.float32)}
    _L1_attn_all = _L1_attn_setup()
    _L1_attn_in = {k: v for k, v in _L1_attn_all.items() if k in ('Wq', 'bq', 'Wk', 'bk', 'Wv', 'bv', 'Wo', 'bo', 'key_weights')}
    del _L1_attn_all

    def _L1_ffn_setup():
        import jax, jax.numpy as jnp
        import numpy as np
        B, S, D = (4, 128, 512)
        E, K, H = (8, 2, 352)
        HS = 2 * 352
        ALPHA = 0.001
        W_SCALE = 0.02

        def _moe_forward(hidden_states, gate_w, w_gate, w_up, w_down, sw_gate, sw_up, sw_down):
            b, s, d = hidden_states.shape
            x = hidden_states.reshape(-1, d)
            T = x.shape[0]
            logits = x @ gate_w
            scores = jax.nn.softmax(logits, axis=-1)
            topk_w, topk_idx = jax.lax.top_k(scores, K)
            mask = jax.nn.one_hot(topk_idx, E, dtype=scores.dtype).sum(axis=1)
            ce = mask.mean(axis=0)
            Pi = scores.mean(axis=0)
            aux_loss = (Pi * ce * E).sum() * ALPHA
            comb = jnp.zeros((T, E), dtype=x.dtype)
            comb = comb.at[jnp.arange(T)[:, None], topk_idx].add(topk_w)
            g = jax.nn.silu(jnp.einsum('td,edh->teh', x, w_gate)) * jnp.einsum('td,edh->teh', x, w_up)
            routed = jnp.einsum('teh,ehd,te->td', g, w_down, comb)
            shared = jax.nn.silu(x @ sw_gate) * (x @ sw_up) @ sw_down
            out = (routed + shared).reshape(b, s, d)
            return (out, aux_loss)
        key = jax.random.key(seed)
        ks = jax.random.split(key, 8)
        rn = lambda k, sh: jax.random.normal(k, sh, dtype=jnp.float32)
        return {'hidden_states': rn(ks[0], (B, S, D)), 'gate_w': rn(ks[1], (D, E)) * W_SCALE, 'w_gate': rn(ks[2], (E, D, H)) * W_SCALE, 'w_up': rn(ks[3], (E, D, H)) * W_SCALE, 'w_down': rn(ks[4], (E, H, D)) * W_SCALE, 'sw_gate': rn(ks[5], (D, HS)) * W_SCALE, 'sw_up': rn(ks[6], (D, HS)) * W_SCALE, 'sw_down': rn(ks[7], (HS, D)) * W_SCALE}
    _L1_ffn_all = _L1_ffn_setup()
    _L1_ffn_in = {k: v for k, v in _L1_ffn_all.items() if k in ('gate_w', 'w_gate', 'w_up', 'w_down', 'sw_gate', 'sw_up', 'sw_down')}
    del _L1_ffn_all
    return {'x': x, 'ctx_2048': ctx_2048, 'mask_BxS2_bk0': mask_BxS2_bk0, 'L0_attn_wq': _L0_attn_in['wq'], 'L0_attn_wk': _L0_attn_in['wk'], 'L0_attn_wv': _L0_attn_in['wv'], 'L0_attn_wo': _L0_attn_in['wo'], 'L0_ffn_gate_w': _L0_ffn_in['gate_w'], 'L0_ffn_w11': _L0_ffn_in['w11'], 'L0_ffn_w33': _L0_ffn_in['w33'], 'L0_ffn_w22': _L0_ffn_in['w22'], 'L0_ffn_sw1': _L0_ffn_in['sw1'], 'L0_ffn_sw2': _L0_ffn_in['sw2'], 'L0_ffn_sw3': _L0_ffn_in['sw3'], 'L1_attn_Wq': _L1_attn_in['Wq'], 'L1_attn_bq': _L1_attn_in['bq'], 'L1_attn_Wk': _L1_attn_in['Wk'], 'L1_attn_bk': _L1_attn_in['bk'], 'L1_attn_Wv': _L1_attn_in['Wv'], 'L1_attn_bv': _L1_attn_in['bv'], 'L1_attn_Wo': _L1_attn_in['Wo'], 'L1_attn_bo': _L1_attn_in['bo'], 'L1_attn_key_weights': _L1_attn_in['key_weights'], 'L1_ffn_gate_w': _L1_ffn_in['gate_w'], 'L1_ffn_w_gate': _L1_ffn_in['w_gate'], 'L1_ffn_w_up': _L1_ffn_in['w_up'], 'L1_ffn_w_down': _L1_ffn_in['w_down'], 'L1_ffn_sw_gate': _L1_ffn_in['sw_gate'], 'L1_ffn_sw_up': _L1_ffn_in['sw_up'], 'L1_ffn_sw_down': _L1_ffn_in['sw_down']}

def reference(x, ctx_2048, mask_BxS2_bk0, L0_attn_wq, L0_attn_wk, L0_attn_wv, L0_attn_wo, L0_ffn_gate_w, L0_ffn_w11, L0_ffn_w33, L0_ffn_w22, L0_ffn_sw1, L0_ffn_sw2, L0_ffn_sw3, L1_attn_Wq, L1_attn_bq, L1_attn_Wk, L1_attn_bk, L1_attn_Wv, L1_attn_bv, L1_attn_Wo, L1_attn_bo, L1_attn_key_weights, L1_ffn_gate_w, L1_ffn_w_gate, L1_ffn_w_up, L1_ffn_w_down, L1_ffn_sw_gate, L1_ffn_sw_up, L1_ffn_sw_down):
    import jax
    import jax.numpy as jnp

    def _L0_xattn_ref(qkv, y):
        import math
        import jax, jax.numpy as jnp
        import numpy as np
        N_HEADS = 16
        bs, width, length = qkv.shape
        ch = width // N_HEADS
        q = qkv.reshape(bs * N_HEADS, ch, length)
        k = v = y.reshape(bs * N_HEADS, ch, -1)
        scale = 1.0 / math.sqrt(math.sqrt(ch))
        weight = jnp.einsum('bct,bcs->bts', q * scale, k * scale)
        weight = jax.nn.softmax(weight.astype(jnp.float32), axis=-1).astype(weight.dtype)
        a = jnp.einsum('bts,bcs->bct', weight, v)
        return a.reshape(bs, -1, length)

    def _L0_attn_ref(x, wq, wk, wv, wo):
        import jax, jax.numpy as jnp
        import numpy as np
        D_MODEL = 512
        NUM_HEADS = 16
        THETA = 10000.0

        def _rope(t, cos, sin):
            x_even = t[..., 0::2]
            x_odd = t[..., 1::2]
            rot = jnp.stack((-x_odd, x_even), axis=-1).reshape(t.shape)
            return t * cos + rot * sin
        bs, S, d = x.shape
        H = NUM_HEADS
        dk = d // H
        q = (x @ wq.T).reshape(bs, S, H, dk).transpose(0, 2, 1, 3)
        k = (x @ wk.T).reshape(bs, S, H, dk).transpose(0, 2, 1, 3)
        v = (x @ wv.T).reshape(bs, S, H, dk).transpose(0, 2, 1, 3)
        half = dk // 2
        inv_freq = THETA ** (-2.0 * jnp.arange(half, dtype=jnp.float32) / dk)
        pos = jnp.arange(S, dtype=jnp.float32)
        ang = pos[:, None] * inv_freq[None, :]
        cos = jnp.repeat(jnp.cos(ang), 2, axis=-1)
        sin = jnp.repeat(jnp.sin(ang), 2, axis=-1)
        q = _rope(q, cos, sin)
        k = _rope(k, cos, sin)
        scale = 1.0 / jnp.sqrt(jnp.asarray(dk, dtype=x.dtype))
        attn = jnp.einsum('bhqd,bhkd->bhqk', q, k) * scale
        causal = jnp.tril(jnp.ones((S, S), dtype=bool))
        attn = jnp.where(causal, attn, -jnp.inf)
        probs = jax.nn.softmax(attn, axis=-1)
        out = jnp.einsum('bhqk,bhkd->bhqd', probs, v)
        out = out.transpose(0, 2, 1, 3).reshape(bs, S, d)
        return out @ wo.T

    def _L0_ffn_ref(x, gate_w, w11, w33, w22, sw1, sw2, sw3):
        import jax, jax.numpy as jnp
        import numpy as np
        B, S, DIM = (4, 128, 512)
        E, INTER = (32, 256)
        G, TOPK_G, TOPK = (8, 4, 6)
        ROUTE_SCALE = 2.5
        SHARED_INTER = 2 * INTER

        def _gate(xf, gate_w):
            scores = jax.nn.sigmoid(xf @ gate_w.T)
            gs = scores.reshape(-1, G, E // G)
            group_scores = gs.max(axis=-1)
            _, gidx = jax.lax.top_k(group_scores, TOPK_G)
            gmask = jnp.any(jnp.arange(G)[None, None, :] == gidx[:, :, None], axis=1)
            masked = jnp.where(gmask[:, :, None], gs, -jnp.inf).reshape(-1, E)
            _, idx = jax.lax.top_k(masked, TOPK)
            w = jnp.take_along_axis(scores, idx, axis=1)
            w = w / jnp.sum(w, axis=-1, keepdims=True) * ROUTE_SCALE
            return (w, idx)
        xf = x.reshape(-1, DIM)
        T = xf.shape[0]
        w, idx = _gate(xf, gate_w)
        c = jnp.zeros((T, E), xf.dtype).at[jnp.arange(T)[:, None], idx].add(w)
        g = jnp.einsum('td,eid->tei', xf, w11)
        u = jnp.einsum('td,eid->tei', xf, w33)
        act = jax.nn.silu(g) * u
        y = jnp.einsum('tei,te,edi->td', act, c, w22)
        shared = jax.nn.silu(xf @ sw1.T) * (xf @ sw3.T) @ sw2.T
        return (y + shared).reshape(x.shape)

    def _L1_xattn_ref(hidden_states, memory_tokens, memory_mask):
        import jax, jax.numpy as jnp
        import numpy as np
        B, S, D = hidden_states.shape
        scale = 1.0 / jnp.sqrt(jnp.asarray(D, hidden_states.dtype))
        scores = jnp.einsum('bsd,bmd->bsm', hidden_states, memory_tokens) * scale
        neg_inf = jnp.asarray(-1e+30, scores.dtype)
        scores = jnp.where(memory_mask[:, None, :], scores, neg_inf)
        attn = jax.nn.softmax(scores, axis=-1)
        readout = jnp.einsum('bsm,bmd->bsd', attn, memory_tokens)
        valid_b = jnp.any(memory_mask, axis=-1)
        out = jnp.where(valid_b[:, None, None], readout, jnp.zeros_like(readout))
        return out

    def _L1_attn_ref(x, Wq, bq, Wk, bk, Wv, bv, Wo, bo, key_weights):
        import jax, jax.numpy as jnp
        import numpy as np
        HIDDEN = 512
        NUM_HEADS = 32
        HEAD_DIM = 64
        NUM_KV = 8
        GROUP = NUM_HEADS // NUM_KV
        SCALE = HEAD_DIM ** (-0.5)
        ROPE_BASE = 10000.0

        def apply_rope(t):
            S, D = (t.shape[-2], t.shape[-1])
            inv_freq = 1.0 / ROPE_BASE ** (jnp.arange(0, D, 2, dtype=jnp.float32) / D)
            ang = jnp.arange(S, dtype=jnp.float32)[:, None] * inv_freq[None, :]
            cos, sin = (jnp.cos(ang), jnp.sin(ang))
            x1, x2 = (t[..., :D // 2], t[..., D // 2:])
            return jnp.concatenate([x1 * cos - x2 * sin, x2 * cos + x1 * sin], axis=-1)
        B, S, _ = x.shape
        q = (x @ Wq.T + bq).reshape(B, S, NUM_HEADS, HEAD_DIM).transpose(0, 2, 1, 3)
        k = (x @ Wk.T + bk).reshape(B, S, NUM_KV, HEAD_DIM).transpose(0, 2, 1, 3)
        v = (x @ Wv.T + bv).reshape(B, S, NUM_KV, HEAD_DIM).transpose(0, 2, 1, 3)
        q = apply_rope(q)
        k = apply_rope(k)
        qg = q.reshape(B, NUM_KV, GROUP, S, HEAD_DIM)
        scores = jnp.einsum('bkgsd,bktd->bkgst', qg, k) * SCALE
        scores = scores * key_weights.reshape(1, NUM_KV, GROUP, 1, 1)
        causal = jnp.tril(jnp.ones((S, S), bool))
        scores = jnp.where(causal, scores, -jnp.inf)
        a = jax.nn.softmax(scores, axis=-1)
        o = jnp.einsum('bkgst,bktd->bkgsd', a, v)
        o = o.reshape(B, NUM_HEADS, S, HEAD_DIM).transpose(0, 2, 1, 3).reshape(B, S, NUM_HEADS * HEAD_DIM)
        return o @ Wo.T + bo

    def _L1_ffn_ref(hidden_states, gate_w, w_gate, w_up, w_down, sw_gate, sw_up, sw_down):
        import jax, jax.numpy as jnp
        import numpy as np
        B, S, D = (4, 128, 512)
        E, K, H = (8, 2, 352)
        HS = 2 * 352
        ALPHA = 0.001
        W_SCALE = 0.02

        def _moe_forward(hidden_states, gate_w, w_gate, w_up, w_down, sw_gate, sw_up, sw_down):
            b, s, d = hidden_states.shape
            x = hidden_states.reshape(-1, d)
            T = x.shape[0]
            logits = x @ gate_w
            scores = jax.nn.softmax(logits, axis=-1)
            topk_w, topk_idx = jax.lax.top_k(scores, K)
            mask = jax.nn.one_hot(topk_idx, E, dtype=scores.dtype).sum(axis=1)
            ce = mask.mean(axis=0)
            Pi = scores.mean(axis=0)
            aux_loss = (Pi * ce * E).sum() * ALPHA
            comb = jnp.zeros((T, E), dtype=x.dtype)
            comb = comb.at[jnp.arange(T)[:, None], topk_idx].add(topk_w)
            g = jax.nn.silu(jnp.einsum('td,edh->teh', x, w_gate)) * jnp.einsum('td,edh->teh', x, w_up)
            routed = jnp.einsum('teh,ehd,te->td', g, w_down, comb)
            shared = jax.nn.silu(x @ sw_gate) * (x @ sw_up) @ sw_down
            out = (routed + shared).reshape(b, s, d)
            return (out, aux_loss)
        out, _aux = _moe_forward(hidden_states, gate_w, w_gate, w_up, w_down, sw_gate, sw_up, sw_down)
        return out
    x = x + _L0_xattn_ref(_layernorm(x, axis=-1), ctx_2048)
    x = x + _L0_attn_ref(_layernorm(x, axis=-1), L0_attn_wq, L0_attn_wk, L0_attn_wv, L0_attn_wo)
    x = x + _L0_ffn_ref(_layernorm(x, axis=-1), L0_ffn_gate_w, L0_ffn_w11, L0_ffn_w33, L0_ffn_w22, L0_ffn_sw1, L0_ffn_sw2, L0_ffn_sw3)
    x = x + _L1_xattn_ref(_layernorm(x, axis=-1), ctx_2048, mask_BxS2_bk0)
    x = x + _L1_attn_ref(_layernorm(x, axis=-1), L1_attn_Wq, L1_attn_bq, L1_attn_Wk, L1_attn_bk, L1_attn_Wv, L1_attn_bv, L1_attn_Wo, L1_attn_bo, L1_attn_key_weights)
    x = x + _L1_ffn_ref(_layernorm(x, axis=-1), L1_ffn_gate_w, L1_ffn_w_gate, L1_ffn_w_up, L1_ffn_w_down, L1_ffn_sw_gate, L1_ffn_sw_up, L1_ffn_sw_down)
    return x

_drawn_inputs = setup_inputs


def setup_inputs(seed=0):
    import zlib

    import numpy as np

    out = dict(_drawn_inputs(seed))
    spreads = {'L1_attn_bq': (0.0, 0.626),
     'L1_attn_bk': (0.0, 0.8),
     'L1_attn_bv': (0.0, 0.1),
     'L1_attn_bo': (0.0, 0.1)}
    factors = {'L1_ffn_gate_w': 8.0,
     'L1_ffn_w_gate': 7.625,
     'L1_ffn_w_up': 7.547,
     'L1_ffn_w_down': 7.494,
     'L1_ffn_sw_gate': 8.0,
     'L1_ffn_sw_up': 8.0,
     'L1_ffn_sw_down': 8.0}
    for name, (base, spread) in spreads.items():
        noise = np.random.default_rng([zlib.crc32(name.encode()), seed]).standard_normal(out[name].shape)
        drawn = base * np.exp(spread * noise) if base else spread * noise
        out[name] = jnp.asarray(drawn.astype(out[name].dtype))
    for name, factor in factors.items():
        out[name] = (out[name] * factor).astype(out[name].dtype)
    return out
```

```python
from contextlib import ExitStack

import concourse.bass as bass
from concourse import mybir

F32 = mybir.dt.float32
BF16 = mybir.dt.bfloat16
ALU = mybir.AluOpType
ACT = mybir.ActivationFunctionType
AX = mybir.AxisListType

P = 128
T = 256
TA = T // P
D = 512
DC = D // P
S2 = 4096
EPS = 1e-5

XH = 16
XC = T // XH
XS = S2 * D // T
XT = XS // P
XHA = P // XC
XSCALE = 0.25
TERMS = [0, 1, 0, 1, 2, 0]
QTERMS = [0, 0, 1, 1, 0, 2]
KR = 6 * XC
LAG = 8


class Count:

    def __init__(self, sem):
        self.sem, self.n = sem, 0

    def inc(self, ins, by=1):
        ins.then_inc(self.sem, by)
        self.n += by
        return self.n



SLOTS = 4


def size(dt):
    return 2 if dt == BF16 else 1 if dt == mybir.dt.uint8 else 4


class Area:

    def __init__(self, nc, lo, hi):
        self.nc, self.base, self.hi = nc, lo, hi

    def at(self, kib, name, shape, dt=F32):
        n = size(dt)
        for d in shape[1:]:
            n *= d
        assert self.base + kib * 1024 + n <= self.hi, (name, kib, n)
        self.end = kib + n / 1024
        return self.nc.alloc_sbuf_tensor_at(name, shape, dt, offset=self.base + int(kib * 1024))


class Shared:
    pass


class Gates:
    pass


def setup(nc, ctx):
    g = Shared()
    g.nc = nc

    def sb(name, shape, dt=F32):
        return ctx.enter_context(nc.sbuf_tensor(name, shape, dt))

    def sem(name):
        return ctx.enter_context(nc.semaphore(name))

    g.sem = sem
    g.bank = ctx.enter_context(nc.psum_tensor("bank", [P, 8, 512], F32))
    g.ident = sb("ident", [P, P])
    g.identb = sb("identb", [P, P], BF16)
    g.X = sb("X", [P, TA, D])
    g.xn = sb("xn", [P, TA, D])
    g.xnT = sb("xnT", [P, DC, T])
    g.stats = sb("stats", [P, TA, 6])
    g.mv = sb("mv", [P, TA, 2])
    g.rstd = sb("rstd", [P, TA, 1])
    g.var = sb("var", [P, TA, 1])
    g.std = sb("std", [P, TA, 1])
    g.arena_size = 180 * 1024
    slab = ctx.enter_context(nc.sbuf_tensor("slab", [P, g.arena_size // 4], F32))
    g.slab = slab
    base = nc.sbuf_base - g.arena_size
    g.area = Area(nc, base, base + g.arena_size)
    g.ident_ready = sem("ident_ready")
    g.dve_step = Count(sem("dve_step"))
    g.var_ready = sem("var_ready")
    g.std_ready = sem("std_ready")
    g.xn_ready = sem("xn_ready")
    g.xn_turned = sem("xn_turned")
    g.xnT_ready = sem("xnT_ready")
    g.stage = 0
    return g


def norm_dve(g, dve, k, link):
    nc = g.nc
    for a in range(TA):
        link(nc.vector.bn_stats(g.stats[:, a, :], g.X[:, a, :]))
        link(nc.vector.bn_aggr(g.mv[:, a, :], g.stats[:, a, :]))
    nc.vector.tensor_scalar(g.var[:, :, :], g.mv[:, :, 1:2], EPS, None, ALU.add).then_inc(g.var_ready, 1)
    dve.wait_ge(g.std_ready, k + 1)
    link(nc.vector.reciprocal(g.rstd[:, :, :], g.std[:, :, :]))
    link(nc.vector.tensor_tensor(g.std[:, :, :], g.rstd[:, :, :], g.rstd[:, :, :], ALU.mult))
    link(nc.vector.tensor_tensor(g.std[:, :, :], g.std[:, :, :], g.var[:, :, :], ALU.mult))
    link(nc.vector.tensor_scalar(g.std[:, :, :], g.std[:, :, :], -0.5, 1.5, ALU.mult, ALU.add))
    link(nc.vector.tensor_tensor(g.rstd[:, :, :], g.rstd[:, :, :], g.std[:, :, :], ALU.mult))
    for a in range(TA):
        nc.vector.tensor_scalar(g.xn[:, a, :], g.X[:, a, :], g.mv[:, a, 0:1], g.rstd[:, a, :],
                                ALU.subtract, ALU.mult).then_inc(g.xn_ready, 1)


def norm_act(g, act, k):
    act.wait_ge(g.var_ready, k + 1)
    g.nc.scalar.activation(g.std[:, :, :], g.var[:, :, :], ACT.Sqrt).then_inc(g.std_ready, 1)


def norm_turn_act(g, act, k):
    for a in range(TA):
        act.wait_ge(g.xn_turned, TA * (k - 1) + a + 1)
        g.nc.scalar.copy(g.xnT[:, :, a * P:a * P + P],
                         g.bank[:, 6 + a, :].rearrange("p (d t) -> p d t", d=DC)).then_inc(g.xnT_ready, 1)


def norm_turn_pe(g, pe, k):
    for a in range(TA):
        pe.wait_ge(g.xn_ready, TA * k + a + 1)
        for d in range(DC):
            ins = g.nc.tensor.transpose(g.bank[:, 6 + a, d * P:d * P + P], g.xn[:, a, d * P:d * P + P], g.ident[:, :])
        ins.then_inc(g.xn_turned, 1)


def cross_attention_0(g, x, ctx_rows, ctx_vt, first_loads):
    nc, sem, bank, ident, identb, X, xn = g.nc, g.sem, g.bank, g.ident, g.identb, g.X, g.xn
    dve_step = g.dve_step
    at = g.area.at
    kraw = at(32, "kraw", [P, 2, 1024])
    kres = at(40, "kres", [P, 1024])
    ksplit = at(44, "ksplit", [P, 3, 1024], BF16)
    kstack = at(50, "kstack", [P, 2, XS], BF16)
    qsplit = at(82, "qsplit", [P, 3, TA, D], BF16)
    qstack = at(88, "qstack", [P, XH, D], BF16)
    vraw = at(104, "vraw", [P, 2, XT, XC])
    vext = at(112, "vext", [P, 2, XT, 2 * XC])
    probs = at(128, "probs", [P, 4, 512])
    osb = at(136, "osb", [P, 2, D])
    nd = at(140, "nd", [P, TA, 4, 2, D])
    pm = at(172, "pm", [P, 2, 4, 8])
    negmax = at(172.25, "negmax", [P, 2, 4])
    nres = at(172.5, "nres", [P, 4])
    nsplit = at(172.75, "nsplit", [P, 4, 3], BF16)
    kscratch = nc.dram_tensor("kscratch", [XH, 3, P, 1024], BF16, kind="Internal").ap()
    qscratch = nc.dram_tensor("qscratch", [3, T, D], BF16, kind="Internal").ap()
    oscratch = nc.dram_tensor("oscratch", [XH, P, D], F32, kind="Internal").ap()
    x_loaded = sem("x_loaded")
    kraw_loaded = [sem("kraw_loaded0"), sem("kraw_loaded1")]
    vraw_loaded = [sem("vraw_loaded0"), sem("vraw_loaded1")]
    split_step = sem("split_step")
    split_stored = sem("split_stored")
    stack_lo = [sem("stack_lo0"), sem("stack_lo1")]
    stack_hi = [sem("stack_hi0"), sem("stack_hi1")]
    const_ready = sem("const_ready")
    v_ready = sem("v_ready")
    qsplit_ready = sem("qsplit_ready")
    qsplit_stored = sem("qsplit_stored")
    q_stacked = sem("q_stacked")
    pre_scores = sem("pre_scores")
    pre_reduced = sem("pre_reduced")
    negmax_ready = sem("negmax_ready")
    nsplit_step = sem("nsplit_step")
    negmax_turned = sem("negmax_turned")
    negmax_stacked = sem("negmax_stacked")
    scores = sem("scores")
    probs_ready = sem("probs_ready")
    pv_done = sem("pv_done")
    o_copied = sem("o_copied")
    o_stored = [sem("o_stored0"), sem("o_stored1")]
    nd_loaded = sem("nd_loaded")
    x_final = sem("x_final")

    with nc.Block() as block:

        def over_heads(eng, phase):
            phase(0, 0, True, False)
            phase(1, 1, False, False)
            with eng.Fori(1, XH // 2 - 1) as i:
                phase(i * 2, 0, False, False)
                phase(i * 2 + 1, 1, False, False)
            phase(XH - 2, 0, False, False)
            phase(XH - 1, 1, False, True)

        @block.sync
        def _(sp):
            sp.dma_start(X[:, :, :], x.rearrange("(a p) d -> p a d", p=P)).then_inc(x_loaded, 16)

            def load_raw(h, b):
                sp.dma_start(kraw[:, b, :], ctx_rows[bass.ds(h, 1)].rearrange("h p n -> (h p) n")).then_inc(kraw_loaded[b], 16)

            def load_v(h, b):
                sp.dma_start(vraw[:, b], ctx_vt[bass.ds(h, 1)].rearrange("h p t c -> (h p) t c")).then_inc(vraw_loaded[b], 16)

            def store_split(h):
                sp.wait_ge(split_step, 4 * h + 4)
                sp.dma_start(kscratch[bass.ds(h, 1)].rearrange("h k p n -> (h p) k n") if isinstance(h, int) else
                             kscratch[bass.ds(h, 1)].rearrange("h k p n -> p (h k) n"), ksplit[:, :, :]).then_inc(split_stored, 16)

            def load_stack(h, b, half, reused):
                if half == 0:
                    sp.wait_ge(split_stored, 16 * h + 16)
                if reused:
                    sp.wait_ge(scores, XT * (h - 2) + XT // 2 * (half + 1))
                lo = half * XS // 2
                for j, part in enumerate(TERMS):
                    src = kscratch[bass.ds(h, 1), part].rearrange("h (c s) n -> (h c) (s n)", c=XC)
                    sp.dma_start(kstack[XC * j:XC * j + XC, b, lo:lo + XS // 2],
                                 src[:, lo:lo + XS // 2]).then_inc([stack_lo, stack_hi][half][b], 16)

            load_raw(0, 0)
            load_raw(1, 1)
            load_v(0, 0)
            load_v(1, 1)
            first_loads(sp)
            store_split(0)
            load_stack(0, 0, 0, False)
            load_stack(0, 0, 1, False)
            sp.wait_ge(qsplit_ready, 4)
            sp.dma_start(qscratch.rearrange("k (a p) t -> p k a t", p=P), qsplit[:, :, :, :]).then_inc(qsplit_stored, 16)
            sp.wait_ge(qsplit_stored, 16)
            for j, part in enumerate(QTERMS):
                sp.dma_start(qstack[XC * j:XC * j + XC, :, :],
                             qscratch[part].rearrange("(h c) t -> c h t", c=XC)).then_inc(q_stacked, 16)

            def phase(h, b, first, last):
                if not last:
                    store_split(h + 1)
                    load_stack(h + 1, 1 - b, 0, not first)
                    load_stack(h + 1, 1 - b, 1, not first)
                if not first:
                    sp.wait_ge(o_copied, h)
                    sp.dma_start(oscratch[bass.ds(h - 1, 1)].rearrange("h p t -> (h p) t"), osb[:, 1 - b, :]).then_inc(o_stored[1 - b], 16)
                if not last and not (isinstance(h, int) and h == XH - 2):
                    sp.wait_ge(split_step, 4 * h + 4)
                    load_raw(h + 2, b)
                    sp.wait_ge(v_ready, h + 1)
                    load_v(h + 2, b)

            over_heads(sp, phase)

            def load_nd(h):
                r = XC * (h % XHA)
                sp.dma_start(nd[r:r + XC, h // XHA].rearrange("c g k t -> c (g k) t"),
                             oscratch[h].rearrange("(q c) t -> c q t", c=XC)).then_inc(nd_loaded, 16)

            sp.wait_ge(o_stored[0], 16 * XH // 2)
            sp.wait_ge(o_stored[1], 16 * (XH // 2 - 1))
            for h in range(XH - 1):
                load_nd(h)
            sp.wait_ge(o_copied, XH)
            sp.dma_start(oscratch[XH - 1], osb[:, 1, :]).then_inc(o_stored[1], 16)
            sp.wait_ge(o_stored[1], 16 * XH // 2)
            load_nd(XH - 1)

        @block.gpsimd
        def _(pool):
            nc.gpsimd.memset(ident[:, :], 0.0).then_inc(g.ident_ready, 1)
            nc.gpsimd.memset(identb[:, :], 0.0).then_inc(g.ident_ready, 1)
            pool.wait_ge(g.ident_ready, 2)
            for m in (ident, identb):
                nc.gpsimd.affine_select(out=m[:, :], in_=m[:, :], compare_op=ALU.not_equal, fill=1.0, base=0,
                                        pattern=[[-1, P]], channel_multiplier=1).then_inc(g.ident_ready, 1)

            def split(h, b, first):
                if first:
                    pool.wait_ge(kraw_loaded[b], 16)
                else:
                    pool.wait_ge(kraw_loaded[b], (h - b) * 8 + 16)
                if not (isinstance(h, int) and h == 0):
                    pool.wait_ge(split_stored, 16 * h)
                nc.gpsimd.tensor_copy(ksplit[:, 0, :], kraw[:, b, :]).then_inc(split_step, 1)
                pool.wait_ge(split_step, 4 * h + 1)
                nc.gpsimd.tensor_tensor(kres[:, :], kraw[:, b, :], ksplit[:, 0, :], ALU.subtract).then_inc(split_step, 1)
                pool.wait_ge(split_step, 4 * h + 2)
                nc.gpsimd.tensor_copy(ksplit[:, 1, :], kres[:, :]).then_inc(split_step, 1)
                pool.wait_ge(split_step, 4 * h + 3)
                nc.gpsimd.tensor_tensor(ksplit[:, 2, :], kres[:, :], ksplit[:, 1, :], ALU.subtract).then_inc(split_step, 1)

            def values(h, b, reused):
                pool.wait_ge(vraw_loaded[b], (h - b) * 8 + 16)
                if reused:
                    pool.wait_ge(pv_done, XT * (h - 1))
                nc.gpsimd.tensor_copy(vext[:, b, :, 0:XC], vraw[:, b]).then_inc(v_ready, 1)

            split(0, 0, True)
            split(1, 1, True)
            values(0, 0, False)

            def phase(h, b, first, last):
                pool.wait_ge(negmax_ready, h + 1)
                if not first:
                    pool.wait_ge(negmax_turned, h)
                nc.gpsimd.tensor_copy(nsplit[:, :, 0], negmax[:, b, :]).then_inc(nsplit_step, 1)
                pool.wait_ge(nsplit_step, 4 * h + 1)
                nc.gpsimd.tensor_tensor(nres[:, :], negmax[:, b, :], nsplit[:, :, 0], ALU.subtract).then_inc(nsplit_step, 1)
                pool.wait_ge(nsplit_step, 4 * h + 2)
                nc.gpsimd.tensor_copy(nsplit[:, :, 1], nres[:, :]).then_inc(nsplit_step, 1)
                pool.wait_ge(nsplit_step, 4 * h + 3)
                nc.gpsimd.tensor_tensor(nsplit[:, :, 2], nres[:, :], nsplit[:, :, 1], ALU.subtract).then_inc(nsplit_step, 1)
                if not last:
                    values(h + 1, 1 - b, not first)
                if not last and not (isinstance(h, int) and h == XH - 2):
                    split(h + 2, b, False)

            for h in range(XH):
                phase(h, h % 2, h == 0, h == XH - 1)

        @block.vector
        def _(dve):
            def link(ins):
                dve.wait_ge(dve_step.sem, dve_step.inc(ins))

            nc.vector.memset(kstack[96:99, :, :], 1.0).then_inc(const_ready, 1)
            nc.vector.memset(vext[:, :, :, XC:], 1.0).then_inc(const_ready, 1)
            dve.wait_ge(x_loaded, 16)
            norm_dve(g, dve, 0, link)
            dve.wait_ge(g.xn_ready, TA)
            nc.vector.tensor_copy(qsplit[:, 0], xn[:, :, :]).then_inc(qsplit_ready, 1)
            dve.wait_ge(qsplit_ready, 1)
            link(nc.vector.tensor_tensor(xn[:, :, :], xn[:, :, :], qsplit[:, 0], ALU.subtract))
            nc.vector.tensor_copy(qsplit[:, 1], xn[:, :, :]).then_inc(qsplit_ready, 1)
            dve.wait_ge(qsplit_ready, 2)
            nc.vector.tensor_tensor(qsplit[:, 2], xn[:, :, :], qsplit[:, 1], ALU.subtract).then_inc(qsplit_ready, 2)

            def reduces(h, b, rs):
                for r in rs:
                    dve.wait_ge(pre_scores, 32 * h + r + 1)
                    nc.vector.tensor_reduce(pm[:, b, r % 4, r // 4:r // 4 + 1], bank[:, 2 * (r % 2):2 * (r % 2) + 2, :],
                                            AX.XY, ALU.max).then_inc(pre_reduced, 1)

            reduces(0, 0, range(32))

            def phase(h, b, first, last):
                dve.wait_ge(pre_reduced, 32 * h + 32)
                nc.vector.tensor_reduce(negmax[:, b, :], pm[:, b], AX.X, ALU.max, negate=True).then_inc(negmax_ready, 1)
                if not last:
                    reduces(h + 1, 1 - b, range(3))
                dve.wait_ge(negmax_turned, h + 1)
                nc.vector.tensor_copy(qstack[96:99, bass.ds(h, 1), :], bank[96:99, 7:8, :]).then_inc(negmax_stacked, 1)
                if not last:
                    reduces(h + 1, 1 - b, range(3, 32))

            over_heads(dve, phase)
            dve.wait_ge(nd_loaded, 16 * XH)
            for q in range(1, 4):
                link(nc.vector.tensor_tensor(nd[:, :, 0], nd[:, :, 0], nd[:, :, q], ALU.add))
            link(nc.vector.reciprocal(nd[:, :, 1, 1, :], nd[:, :, 0, 1, :]))
            link(nc.vector.tensor_tensor(nd[:, :, 0, 0, :], nd[:, :, 0, 0, :], nd[:, :, 1, 1, :], ALU.mult))
            nc.vector.tensor_tensor(X[:, :, :], X[:, :, :], nd[:, :, 0, 0, :], ALU.add).then_inc(x_final, 1)
            dve.wait_ge(x_final, 1)

        @block.scalar
        def _(act):
            def exps(h, b, n, first):
                m = XT * b + n
                act.wait_ge(scores, XT * h + n + 1)
                if not (first and n < 4):
                    act.wait_ge(pv_done, XT * h + n - 3)
                nc.scalar.activation(probs[:, m % 4, :], bank[:, 4 + m % 2, :], ACT.Exp, scale=XSCALE).then_inc(probs_ready, 1)

            def copy_o(h, b, first):
                act.wait_ge(pv_done, XT * h + XT)
                if not first:
                    act.wait_ge(o_stored[b], (h - b) * 8)
                nc.scalar.copy(osb[:, b, :], bank[:, 6, :]).then_inc(o_copied, 1)

            def phase(h, b, first, last):
                for n in range(XT):
                    exps(h, b, n, first)
                    if n == 1 and not first:
                        copy_o(h - 1, 1 - b, isinstance(h, int) and h <= 2)

            norm_act(g, act, 0)
            over_heads(act, phase)
            copy_o(XH - 1, 1, False)

        @block.tensor
        def _(pe):
            def pre(h, b, n):
                r = n // 2
                c, tt = r // 4, r % 4
                if n % 2 == 0 and not (isinstance(h, int) and h == 0 and r < 2):
                    pe.wait_ge(pre_reduced, 32 * h + r - 1)
                if n == 0:
                    pe.wait_ge(stack_lo[b], (h - b) * 48 + 96)
                if n == 32:
                    pe.wait_ge(stack_hi[b], (h - b) * 48 + 96)
                k = c * 1024 + 512 * (n % 2)
                ins = nc.tensor.matmul(bank[:, 2 * (r % 2) + n % 2, :], qof(h, slice(0, KR))[:, tt * P:tt * P + P],
                                       kstack[0:KR, b, k:k + 512], start=True, stop=True)
                if n % 2:
                    ins.then_inc(pre_scores, 1)

            def qof(h, rows):
                if isinstance(h, int):
                    return qstack[rows, h, :]
                return qstack[rows, bass.ds(h, 1), :].rearrange("p h t -> p (h t)")

            def score(h, b, n, first):
                m = XT * b + n
                if n == 0:
                    pe.wait_ge(negmax_stacked, h + 1)
                if not (first and n < 2):
                    pe.wait_ge(probs_ready, XT * h + n - 1)
                nc.tensor.matmul(bank[:, 4 + m % 2, :], kstack[0:KR + 3, b, n * P:n * P + P], qof(h, slice(0, KR + 3)),
                                 start=True, stop=True).then_inc(scores, 1)

            def pv(h, b, n, first):
                m = XT * b + n
                pe.wait_ge(probs_ready, XT * h + n + 1)
                if n == 0:
                    pe.wait_ge(v_ready, h + 1)
                    if not first:
                        pe.wait_ge(o_copied, h)
                q = n % 4
                nc.tensor.matmul(bank[32 * q:32 * q + 32, 6, :], vext[:, b, n, :], probs[:, m % 4, :],
                                 start=n < 4, stop=n >= XT - 4).then_inc(pv_done, 1)

            pe.wait_ge(const_ready, 2)
            pe.wait_ge(g.ident_ready, 4)
            pe.wait_ge(q_stacked, 96)
            for n in range(64):
                pre(0, 0, n)

            def main_step(h, b, s, first):
                for fn, lag in ((score, LAG), (pv, LAG + 2)):
                    if s >= lag:
                        fn(h, b, s - lag, first)
                    elif not first:
                        fn(h - 1, 1 - b, XT + s - lag, False)

            def phase(h, b, first, last):
                for s in range(XT):
                    if s == 4:
                        pe.wait_ge(nsplit_step, 4 * h + 4)
                        if not first:
                            pe.wait_ge(negmax_stacked, h)
                        for tt in range(4):
                            ins = nc.tensor.matmul(bank[96:99, 7, tt * P:tt * P + P], nsplit[:, tt, :], identb[:, :],
                                                   start=True, stop=True)
                        ins.then_inc(negmax_turned, 1)
                    if not last:
                        pre(h + 1, 1 - b, s)
                    main_step(h, b, s, first)

            over_heads(pe, phase)
            for s in range(LAG):
                score(XH - 1, 1, XT + s - LAG, False)
                pv(XH - 1, 1, XT + s - LAG - 2, False)
            pv(XH - 1, 1, XT - 2, False)
            pv(XH - 1, 1, XT - 1, False)




def self_attention(g, k, name, heads, dk, q_tiles, kv_tile_of, v_col_of, pairs, w, table, kw, bias, area_at, loaded,
                   first_loads, later_loads):
    nc, sem, bank, X = g.nc, g.sem, g.bank, g.X
    per = P // dk
    NQ = q_tiles * P
    jobs = [("k", 0, a) for a in range(TA)] + [("v", 0, a) for a in range(TA)]
    jobs += [("q", c, a) for c in range(NQ // 512) for a in range(TA)]

    at = lambda kib, what, shape: area_at(kib, f"{name}_{what}", shape)
    qtok = at(0, "qtok", [P, TA, NQ])
    kib = TA * NQ * 4 / 1024
    ktok = at(kib, "ktok", [P, TA, 512])
    vtok = at(kib + 4, "vtok", [P, TA, 512])
    rot = at(kib + 8, "rot", [P, 3, 2, 512])
    qT = at(kib + 20, "qT", [P, q_tiles, T])
    kT = at(2 * kib + 20, "kT", [P, 4, T])
    soft = at(2 * kib + 24, "soft", [P, 3, 3 * P])
    turned_sb = rot[:, 0:2].rearrange("p a b n -> p (a b n)")[:, 0:2 * 3 * P].rearrange("p (r n) -> p r n", r=2)
    aoT = at(0, "aoT", [P, q_tiles, T])
    small = at(2 * kib + 28.5, "small", [P, 4, 2])
    nmax = small[:, 0:2]
    denom = small[:, 2:4]
    rden = at(2 * kib + 28.75, "rden", [P, 2, 2])

    proj_done = sem(name + "_proj_done")
    rot_step = Count(sem(name + "_rot_step"))
    rotated = sem(name + "_rotated")
    v_copied = sem(name + "_v_copied")
    turned = sem(name + "_turned")
    turn_copied = sem(name + "_turn_copied")
    s_ready = sem(name + "_s_ready")
    masked = sem(name + "_masked")
    maxed = sem(name + "_maxed")
    exp_done = sem(name + "_exp_done")
    inverted = sem(name + "_inverted")
    normed = sem(name + "_normed")
    p_turned = sem(name + "_p_turned")
    pt_copied = sem(name + "_pt_copied")
    pv_done = sem(name + "_pv_done")
    ao_copied = sem(name + "_ao_copied")
    out_done = sem(name + "_out_done")

    rot_jobs = [j for j, (kind, c, a) in enumerate(jobs) if kind != "v"]
    v_jobs = [j for j, (kind, c, a) in enumerate(jobs) if kind == "v"]

    with nc.Block() as block:

        @block.sync
        def _(sp):
            first_loads(sp)
            if later_loads:
                sp.wait_ge(proj_done, len(jobs))
                later_loads(sp)

        @block.tensor
        def _(pe):
            norm_turn_pe(g, pe, k)
            pe.wait_ge(g.xnT_ready, TA * k)
            for s, n in loaded:
                pe.wait_ge(s, n)

            def project(j):
                kind, c, a = jobs[j]
                if j >= 4:
                    if jobs[j - 4][0] == "v":
                        pe.wait_ge(v_copied, v_jobs.index(j - 4) + 1)
                    else:
                        pe.wait_ge(rotated, rot_jobs.index(j - 4) + 1)
                for d in range(DC):
                    ins = nc.tensor.matmul(bank[:, j % 4, :], g.xnT[:, d, a * P:a * P + P],
                                           w[kind][:, d, 512 * c:512 * c + 512], start=d == 0, stop=d == DC - 1)
                ins.then_inc(proj_done, 1)

            def turn(r):
                kind, c, a = jobs[rot_jobs[r]]
                pe.wait_ge(rotated, r + 1)
                if r >= 2:
                    pe.wait_ge(turn_copied, r - 1)
                src = (ktok if kind == "k" else qtok)[:, a, 512 * c:512 * c + 512]
                for f in range(4):
                    ins = nc.tensor.transpose(bank[:, 4 + r % 2, f * P:f * P + P], src[:, f * P:f * P + P], g.ident[:, :])
                ins.then_inc(turned, 1)

            r = 0
            for j in range(len(jobs)):
                project(j)
                while r < len(rot_jobs) and rot_jobs[r] <= j - 2:
                    turn(r)
                    r += 1
            for r in range(r, len(rot_jobs)):
                turn(r)
            pe.wait_ge(turn_copied, len(rot_jobs))
            pe.wait_ge(v_copied, TA)

            def scores(n):
                if n >= 2:
                    pe.wait_ge(masked, n - 1)
                b, r0, q, kt = bank[:, n % 2, :], dk * (n % per), n // per, kv_tile_of(n)
                nc.tensor.matmul(b[:, 0:P], qT[r0:r0 + dk, q, 0:P], kT[r0:r0 + dk, kt, 0:P], start=True, stop=True)
                nc.tensor.matmul(b[:, P:3 * P], qT[r0:r0 + dk, q, P:T], kT[r0:r0 + dk, kt, :],
                                 start=True, stop=True).then_inc(s_ready, 1)

            def turn_probs(n):
                pe.wait_ge(normed, n + 1)
                if n >= 2:
                    pe.wait_ge(pt_copied, n - 1)
                for f in range(3):
                    ins = nc.tensor.transpose(bank[:, 2 + n % 2, f * P:f * P + P], soft[:, n % 3, f * P:f * P + P], g.ident[:, :])
                ins.then_inc(p_turned, 1)

            def values(n):
                pe.wait_ge(pt_copied, n + 1)
                q, r0, v0 = n // per, dk * (n % per), v_col_of(n)
                if n % per == 0 and q >= 2:
                    pe.wait_ge(ao_copied, q - 1)
                b = bank[r0:r0 + dk, 4 + q % 2, :]
                nc.tensor.matmul(b[:, 0:T], vtok[:, 0, v0:v0 + dk], turned_sb[:, n % 2, 0:T], start=True, stop=False)
                nc.tensor.matmul(b[:, P:T], vtok[:, 1, v0:v0 + dk], turned_sb[:, n % 2, T:3 * P],
                                 start=False, stop=True).then_inc(pv_done, 1)

            for n in range(heads + 3):
                if n < heads:
                    scores(n)
                if 0 <= n - 2 < heads:
                    turn_probs(n - 2)
                if 0 <= n - 3 < heads:
                    values(n - 3)
            for q in range(q_tiles):
                if q == q_tiles - 1 or q == 0:
                    pe.wait_ge(ao_copied, q_tiles if q else q_tiles - 1)
                for a in range(TA):
                    ins = nc.tensor.matmul(bank[:, 6 + a, :], aoT[:, q, a * P:a * P + P], w["o"][:, q, :],
                                           start=q == 0, stop=q == q_tiles - 1)
            ins.then_inc(out_done, 1)

        @block.vector
        def _(dve):
            def link(ins):
                dve.wait_ge(g.dve_step.sem, g.dve_step.inc(ins))

            norm_dve(g, dve, k, link)

            def rotate(r):
                kind, c, a = jobs[rot_jobs[r]]
                j = rot_jobs[r]
                dve.wait_ge(proj_done, j + 1)
                src = bank[:, j % 4, :]
                if bias is not None:
                    row = bias[kind][:, 512 * c:512 * c + 512]
                    dve.wait_ge(rot_step.sem, rot_step.inc(nc.vector.tensor_tensor(rot[:, 2, r % 2, :], src, row, ALU.add)))
                    src = rot[:, 2, r % 2, :]
                tab = table[kind]
                cos = tab[:, a, 0, :].unsqueeze(1).to_broadcast([P, 512 // dk, dk])
                fold = "p (h i two) -> p h i two" if pairs else "p (h two i) -> p h i two"
                tfold = "p (i two) -> p i two" if pairs else "p (two i) -> p i two"
                sin = tab[:, a, 1, :].rearrange(tfold, two=2)
                x4 = src.rearrange(fold, i=dk // 2, two=2)
                o4 = rot[:, 1, r % 2, :].rearrange(fold, i=dk // 2, two=2)
                rot_step.inc(nc.vector.tensor_tensor(rot[:, 0, r % 2, :].rearrange("p (h i) -> p h i", i=dk),
                                                     src.rearrange("p (h i) -> p h i", i=dk), cos, ALU.mult))
                for t in range(2):
                    s1 = sin[:, :, t].unsqueeze(1).to_broadcast([P, 512 // dk, dk // 2])
                    n = rot_step.inc(nc.vector.tensor_tensor(o4[:, :, :, t], x4[:, :, :, 1 - t], s1, ALU.mult))
                dve.wait_ge(rot_step.sem, n)
                dst = (ktok if kind == "k" else qtok)[:, a, 512 * c:512 * c + 512]
                if kind == "q" and kw is not None:
                    n = rot_step.inc(nc.vector.tensor_tensor(rot[:, 0, r % 2, :], rot[:, 0, r % 2, :], rot[:, 1, r % 2, :], ALU.add))
                    dve.wait_ge(rot_step.sem, n)
                    f = kw[:, 512 // dk * c:512 // dk * (c + 1)].unsqueeze(2).to_broadcast([P, 512 // dk, dk])
                    nc.vector.tensor_tensor(dst.rearrange("p (h i) -> p h i", i=dk),
                                            rot[:, 0, r % 2, :].rearrange("p (h i) -> p h i", i=dk), f, ALU.mult).then_inc(rotated, 1)
                else:
                    nc.vector.tensor_tensor(dst, rot[:, 0, r % 2, :], rot[:, 1, r % 2, :], ALU.add).then_inc(rotated, 1)

            for s, n in loaded:
                dve.wait_ge(s, n)
            for r in range(len(rot_jobs)):
                rotate(r)
                if r == 1:
                    for a in range(TA):
                        j = v_jobs[a]
                        dve.wait_ge(proj_done, j + 1)
                        if bias is not None:
                            nc.vector.tensor_tensor(vtok[:, a, :], bank[:, j % 4, :], bias["v"], ALU.add).then_inc(v_copied, 1)
                        else:
                            nc.vector.tensor_copy(vtok[:, a, :], bank[:, j % 4, :]).then_inc(v_copied, 1)

            def mask_max(n):
                dve.wait_ge(s_ready, n + 1)
                if n >= 3:
                    dve.wait_ge(p_turned, n - 2)
                nc.vector.tensor_tensor(soft[:, n % 3, :], bank[:, n % 2, 0:3 * P], g.causal[:, :], ALU.add).then_inc(masked, 1)
                dve.wait_ge(masked, n + 1)
                if n >= 2:
                    dve.wait_ge(exp_done, 2 * n - 2)
                nc.vector.tensor_reduce(nmax[:, n % 2, 0:1], soft[:, n % 3, 0:P], AX.X, ALU.max, negate=True).then_inc(maxed, 1)
                nc.vector.tensor_reduce(nmax[:, n % 2, 1:2], soft[:, n % 3, P:3 * P], AX.X, ALU.max, negate=True).then_inc(maxed, 1)

            def invert(n):
                dve.wait_ge(exp_done, 2 * n + 2)
                if n >= 2:
                    dve.wait_ge(normed, n - 1)
                nc.vector.reciprocal(rden[:, n % 2, :], denom[:, n % 2, :]).then_inc(inverted, 1)

            def copy_ao(q):
                dve.wait_ge(pv_done, per * q + per)
                nc.vector.tensor_copy(aoT[:, q, :], bank[:, 4 + q % 2, 0:T]).then_inc(ao_copied, 1)

            for n in range(heads + 5):
                if n < heads:
                    mask_max(n)
                if 0 <= n - 1 < heads:
                    invert(n - 1)
                if 0 <= n - 4 < heads and (n - 4) % per == per - 1:
                    copy_ao((n - 4) // per)
            dve.wait_ge(out_done, 1)
            for a in range(TA):
                link(nc.vector.tensor_tensor(X[:, a, :], X[:, a, :], bank[:, 6 + a, :], ALU.add))
                if bias is not None:
                    link(nc.vector.tensor_tensor(X[:, a, :], X[:, a, :], bias["o"], ALU.add))

        @block.gpsimd
        def _(pool):
            for n in range(heads):
                pool.wait_ge(inverted, n + 1)
                nc.gpsimd.tensor_scalar(soft[:, n % 3, 0:P], soft[:, n % 3, 0:P], rden[:, n % 2, 0:1], None, ALU.mult)
                nc.gpsimd.tensor_scalar(soft[:, n % 3, P:3 * P], soft[:, n % 3, P:3 * P], rden[:, n % 2, 1:2], None,
                                        ALU.mult).then_inc(normed, 1)

        @block.scalar
        def _(act):
            norm_act(g, act, k)
            norm_turn_act(g, act, k)
            for r in range(len(rot_jobs)):
                kind, c, a = jobs[rot_jobs[r]]
                act.wait_ge(turned, r + 1)
                dst = kT if kind == "k" else qT
                nc.scalar.copy(dst[:, 4 * c:4 * c + 4, a * P:a * P + P],
                               bank[:, 4 + r % 2, :].rearrange("p (f t) -> p f t", f=4)).then_inc(turn_copied, 1)

            def exps(n):
                act.wait_ge(maxed, 2 * n + 2)
                if n >= 2:
                    act.wait_ge(inverted, n - 1)
                for a, cols in enumerate((slice(0, P), slice(P, 3 * P))):
                    nc.scalar.activation(soft[:, n % 3, cols], soft[:, n % 3, cols], ACT.Exp, bias=nmax[:, n % 2, a:a + 1],
                                         accum_out=denom[:, n % 2, a:a + 1]).then_inc(exp_done, 1)

            def copy_turned(n):
                act.wait_ge(p_turned, n + 1)
                if n >= 2:
                    act.wait_ge(pv_done, n - 1)
                nc.scalar.copy(turned_sb[:, n % 2, :], bank[:, 2 + n % 2, 0:3 * P]).then_inc(pt_copied, 1)

            for n in range(heads + 2):
                if n < heads:
                    exps(n)
                if n >= 2:
                    copy_turned(n - 2)


def experts(g, k, name, E, width, choose, gate_w, gate_loaded, slots, slot_loaded, wall, area_at, cb, first_loads, later_loads):
    nc, sem, bank, X = g.nc, g.sem, g.bank, g.X
    rows = [min(P, width - u * P) for u in range(-(-width // P))]
    U = len(rows)
    N = E + 2
    slot_of = lambda n: (n + 2) % SLOTS

    at = lambda kib, what, shape: area_at(kib, f"{name}_{what}", shape)
    silu = at(0, "silu", [P, 4, T])
    acts = at(4, "acts", [P, 4, T])
    early = lambda kib, what, shape: g.area.at(kib, f"{name}_{what}", shape)
    gates = Gates()
    gates.z = at(8, "z", [P, TA, E])
    gates.s = at(8.25, "s", [P, TA, E])
    gates.c = at(8.5, "c", [P, TA, E])
    gates.t = at(8.75, "t", [P, TA, E])
    gates.cmp = early(0, "cmp", [P, TA, E, E])
    gates.eq = early(8, "eq", [P, TA, E, E])
    gates.r = at(9, "r", [P, TA, E])
    gates.g8 = at(9.25, "g8", [P, TA, 8])
    gates.m = at(9.5, "m", [P, TA, 8])
    gates.one = at(9.75, "one", [P, TA, 1])
    gates.cmp8 = at(10, "cmp8", [P, TA, 8, 8])
    gates.eq8 = at(10.5, "eq8", [P, TA, 8, 8])
    cT = at(11, "cT", [E, T])
    cscratch = nc.dram_tensor(name + "_cscratch", [E, T], F32, kind="Internal").ap()

    z_ready = sem(name + "_z_ready")
    gate_exp = sem(name + "_gate_exp")
    gate_in = sem(name + "_gate_in")
    c_ready = sem(name + "_c_ready")
    c_turned = sem(name + "_c_turned")
    c_copied = sem(name + "_c_copied")
    c_stored = sem(name + "_c_stored")
    c_spread = sem(name + "_c_spread")
    gu_ready = sem(name + "_gu_ready")
    silu_ready = sem(name + "_silu_ready")
    weighted = sem(name + "_weighted")
    act_ready = sem(name + "_act_ready")
    down_done = sem(name + "_down_done")

    def over_experts(eng, expert):
        expert(0, 2)
        expert(1, 3)
        with eng.Fori(0, E // SLOTS) as i:
            for s in range(SLOTS):
                expert(i * SLOTS + (s + 2), s)

    with nc.Block() as block:

        @block.sync
        def _(sp):
            first_loads(sp)
            sp.wait_ge(c_copied, 1)
            sp.dma_start(cscratch, cT[:, :]).then_inc(c_stored, 16)
            sp.wait_ge(c_stored, 16)
            sp.dma_start(cb[:, :, :].rearrange("p e t -> p (e t)"),
                         cscratch.rearrange("e t -> (e t)").partition_broadcast(P)).then_inc(c_spread, 16)
            for n in range(SLOTS, N):
                sp.wait_ge(down_done, U * (n - SLOTS + 1))
                sp.dma_start(slots[slot_of(n)], wall[n]).then_inc(slot_loaded[slot_of(n)], 16)
            if later_loads:
                later_loads(sp)

        @block.tensor
        def _(pe):
            norm_turn_pe(g, pe, k)
            pe.wait_ge(g.xnT_ready, TA * k)
            for s, n in gate_loaded:
                pe.wait_ge(s, n)
            for a in range(TA):
                for d in range(DC):
                    ins = nc.tensor.matmul(bank[:, 6, a * E:a * E + E], g.xnT[:, d, a * P:a * P + P], gate_w[:, d, :],
                                           start=d == 0, stop=d == DC - 1)
            ins.then_inc(z_ready, 1)

            def turn_c():
                pe.wait_ge(c_ready, 1)
                for a in range(TA):
                    ins = nc.tensor.transpose(bank[0:E, 7, a * P:a * P + P], gates.c[:, a, :], g.ident[:, :])
                ins.then_inc(c_turned, 1)

            def down(u0, j, last=False):
                slot, jj, b = j
                pe.wait_ge(act_ready, u0 + 1)
                r = rows[jj]
                wd = slots[slot][:, 2 * DC * width:].rearrange("p (u n) -> p u n", n=D)
                for a in range(TA):
                    ins = nc.tensor.matmul(bank[:, 4 + a, :], acts[0:r, b, a * P:a * P + P], wd[0:r, jj, :],
                                           start=isinstance(u0, int) and u0 == 0, stop=last, skip_group_check=True)
                ins.then_inc(down_done, 1)

            before = [None]

            def expert(n, slot):
                wg = slots[slot][:, 0:2 * DC * width].rearrange("p (m d i) -> p m d i", m=2, d=DC)
                if isinstance(n, int):
                    pe.wait_ge(slot_loaded[slot], 16)
                else:
                    pe.wait_ge(slot_loaded[slot], (n - (slot + 2)) * (16 // SLOTS) + (16 if slot < 2 else 32))
                for j, r in enumerate(rows):
                    b = (U * (slot + 2) + j) % 4
                    u = n * U + j
                    if not (isinstance(n, int) and u < 4):
                        pe.wait_ge(act_ready, u - 3)
                    for m in range(2):
                        for d in range(DC):
                            ins = nc.tensor.matmul(bank[0:r, b, m * T:m * T + T], wg[:, m, d, j * P:j * P + r],
                                                   g.xnT[:, d, :], start=d == 0, stop=d == DC - 1)
                    ins.then_inc(gu_ready, 1)
                    if before[0] is not None:
                        down(u - 1, before[0])
                    before[0] = (slot, j, b)
                if isinstance(n, int) and n == 1:
                    turn_c()

            over_experts(pe, expert)
            down(U * N - 1, before[0], last=True)

        @block.scalar
        def _(act):
            norm_act(g, act, k)
            norm_turn_act(g, act, k)
            if choose == "softmax":
                act.wait_ge(gate_in, 1)
                nc.scalar.activation(gates.s[:, :, :], gates.t[:, :, :], ACT.Exp).then_inc(gate_exp, 1)
            else:
                act.wait_ge(z_ready, 1)
                nc.scalar.activation(gates.s[:, :, :], bank[:, 6, 0:TA * E].rearrange("p (a e) -> p a e", a=TA), ACT.Exp,
                                     scale=-1.0).then_inc(gate_exp, 1)

            def expert(n, slot):
                for j, r in enumerate(rows):
                    b = (U * (slot + 2) + j) % 4
                    u = n * U + j
                    act.wait_ge(gu_ready, u + 1)
                    if not (isinstance(n, int) and u < 4):
                        act.wait_ge(act_ready, u - 3)
                    nc.scalar.activation(silu[0:r, b, :], bank[0:r, b, 0:T], ACT.Silu).then_inc(silu_ready, 1)

            over_experts(act, expert)

        @block.vector
        def _(dve):
            def link(ins):
                dve.wait_ge(g.dve_step.sem, g.dve_step.inc(ins))

            norm_dve(g, dve, k, link)
            G = gates
            dve.wait_ge(z_ready, 1)
            if choose == "softmax":
                link(nc.vector.tensor_copy(G.z[:, :, :], bank[:, 6, 0:TA * E].rearrange("p (a e) -> p a e", a=TA)))
                link(nc.vector.tensor_reduce(G.one[:, :, :], G.z[:, :, :], AX.X, ALU.max))
                nc.vector.tensor_tensor(G.t[:, :, :], G.z[:, :, :], G.one[:, :, :].to_broadcast([P, TA, E]),
                                        ALU.subtract).then_inc(gate_in, 1)
                dve.wait_ge(gate_exp, 1)
                link(nc.vector.tensor_reduce(G.one[:, :, :], G.s[:, :, :], AX.X, ALU.add))
                link(nc.vector.reciprocal(G.one[:, :, :], G.one[:, :, :]))
                link(nc.vector.tensor_tensor(G.s[:, :, :], G.s[:, :, :], G.one[:, :, :].to_broadcast([P, TA, E]), ALU.mult))
            else:
                dve.wait_ge(gate_exp, 1)
                link(nc.vector.tensor_copy(G.z[:, :, :], bank[:, 6, 0:TA * E].rearrange("p (a e) -> p a e", a=TA)))
                link(nc.vector.tensor_scalar(G.s[:, :, :], G.s[:, :, :], 1.0, None, ALU.add))
                link(nc.vector.reciprocal(G.s[:, :, :], G.s[:, :, :]))

            def keep_top(out, val, n, top, cmp, eq):
                for a in range(TA):
                    mine = val[:, a, :].unsqueeze(2).to_broadcast([P, n, n])
                    other = val[:, a, :].unsqueeze(1).to_broadcast([P, n, n])
                    left = g.left[:, 0:n, 0:n]
                    nc.vector.tensor_tensor(cmp[:, a], other, mine, ALU.is_gt).then_inc(g.dve_step.sem, 1)
                    g.dve_step.n += 1
                    link(nc.vector.tensor_tensor(eq[:, a], other, mine, ALU.is_equal))
                    link(nc.vector.tensor_tensor(eq[:, a], eq[:, a], left, ALU.mult))
                    link(nc.vector.tensor_tensor(cmp[:, a], cmp[:, a], eq[:, a], ALU.add))
                link(nc.vector.tensor_reduce(out, cmp[:, :, :, :], AX.X, ALU.add))
                link(nc.vector.tensor_scalar(out, out, top - 0.5, None, ALU.is_lt))

            if choose == "softmax":
                keep_top(G.r[:, :, :], G.z, E, 2, G.cmp, G.eq)
                nc.vector.tensor_tensor(G.c[:, :, :], G.s[:, :, :], G.r[:, :, :], ALU.mult).then_inc(c_ready, 1)
            else:
                link(nc.vector.tensor_reduce(G.g8[:, :, :], G.z[:, :, :].rearrange("p a (g e) -> p a g e", g=8), AX.X, ALU.max))
                keep_top(G.m[:, :, :], G.g8, 8, 4, G.cmp8, G.eq8)
                z4 = G.z[:, :, :].rearrange("p a (g e) -> p a g e", g=8)
                link(nc.vector.tensor_scalar(G.g8[:, :, :], G.m[:, :, :], 1.0, 1e30, ALU.subtract, ALU.mult))
                for op, row in ((ALU.mult, G.m), (ALU.add, G.g8)):
                    for a in range(TA):
                        link(nc.vector.tensor_tensor(z4[:, a], z4[:, a], row[:, a, :].unsqueeze(2).to_broadcast([P, 8, 4]), op))
                keep_top(G.r[:, :, :], G.z, E, 6, G.cmp, G.eq)
                link(nc.vector.tensor_tensor(G.c[:, :, :], G.s[:, :, :], G.r[:, :, :], ALU.mult))
                link(nc.vector.tensor_reduce(G.one[:, :, :], G.c[:, :, :], AX.X, ALU.add))
                link(nc.vector.reciprocal(G.one[:, :, :], G.one[:, :, :]))
                link(nc.vector.tensor_tensor(G.c[:, :, :], G.c[:, :, :], G.one[:, :, :].to_broadcast([P, TA, E]), ALU.mult))
                nc.vector.tensor_scalar(G.c[:, :, :], G.c[:, :, :], 2.5, None, ALU.mult).then_inc(c_ready, 1)

            def expert(n, slot):
                shared = isinstance(n, int)
                for j, r in enumerate(rows):
                    b = (U * (slot + 2) + j) % 4
                    u = n * U + j
                    dve.wait_ge(silu_ready, u + 1)
                    if not shared:
                        c = cb[0:r, bass.ds(n - 2, 1), :].rearrange("p e t -> p (e t)")
                        nc.vector.tensor_tensor(silu[0:r, b, :], silu[0:r, b, :], c, ALU.mult).then_inc(weighted, 1)
                        dve.wait_ge(weighted, u - (2 * U - 1))
                    if not (shared and u < 4):
                        dve.wait_ge(down_done, u - 3)
                    nc.vector.tensor_tensor(acts[0:r, b, :], silu[0:r, b, :], bank[0:r, b, T:2 * T], ALU.mult).then_inc(act_ready, 1)
                if shared and n == 1:
                    dve.wait_ge(c_turned, 1)
                    nc.vector.tensor_copy(cT[:, :], bank[0:E, 7, 0:T]).then_inc(c_copied, 1)
                    dve.wait_ge(c_spread, 16)

            over_experts(dve, expert)
            dve.wait_ge(down_done, U * N)
            for a in range(TA):
                link(nc.vector.tensor_tensor(X[:, a, :], X[:, a, :], bank[:, 4 + a, :], ALU.add))


def cross_attention_1(g, k, ctxT, ctxT_loaded, ctx_chunks, mask, first_loads, later_loads):
    nc, sem, bank, X = g.nc, g.sem, g.bank, g.X
    at = g.area.at
    M = S2
    MC = M // 512
    MT = M // P
    pr = at(0, "pr", [P, TA, M])
    mb = at(32, "mb", [P, M])
    mask8 = at(48, "mask8", [P, M], mybir.dt.uint8)
    pT = at(52, "pT", [P, 4, 2, T])
    nat = [at(124 + 8 * c, f"nat{c}", [P, 4, D]) for c in range(6)]
    nat += [ctxT[0], ctxT[1]]
    pmx = at(172, "pmx", [P, TA, MC])
    nmx = at(172.25, "nmx", [P, TA])
    den = at(172.5, "cden", [P, TA])
    okay = at(172.75, "okay", [P, 1])
    SC = float(D) ** -0.5
    mask_loaded = sem("mask_loaded")
    nat_loaded = [sem(f"nat_loaded{c}") for c in range(MC)]
    s_ready = sem("x1_s_ready")
    s_masked = sem("x1_s_masked")
    maxed = sem("x1_maxed")
    exp_done = sem("x1_exp_done")
    p_turned = sem("x1_p_turned")
    pt_copied = [sem("x1_pt_copied0"), sem("x1_pt_copied1")]
    pv_done = sem("x1_pv_done")

    with nc.Block() as block:

        @block.sync
        def _(sp):
            sp.dma_start(mask8[:, :], mask.partition_broadcast(P)).then_inc(mask_loaded, 16)
            first_loads(sp)
            for c in range(MC):
                if c >= 6:
                    sp.wait_ge(s_ready, MC + c - 6 + 1)
                sp.dma_start(nat[c][:, :, :], ctx_chunks[c]).then_inc(nat_loaded[c], 16)
            sp.wait_ge(s_ready, 2 * MC)
            later_loads(sp)

        @block.tensor
        def _(pe):
            norm_turn_pe(g, pe, k)
            pe.wait_ge(g.xnT_ready, TA * k)
            for a in range(TA):
                for c in range(MC):
                    i = a * MC + c
                    if a == 0:
                        pe.wait_ge(ctxT_loaded[c], 16)
                    if i >= 4:
                        pe.wait_ge(s_masked, i - 3)
                    for d in range(DC):
                        ins = nc.tensor.matmul(bank[:, i % 4, :], g.xnT[:, d, a * P:a * P + P], ctxT[c][:, d, :],
                                               start=d == 0, stop=d == DC - 1)
                    ins.then_inc(s_ready, 1)

            def turn(i):
                if i >= 2:
                    pe.wait_ge(pt_copied[i % 2], i // 2)
                for t in range(2):
                    for a in range(TA):
                        ins = nc.tensor.transpose(bank[:, 4 + i % 2, t * T + a * P:t * T + a * P + P],
                                                  pr[:, a, (2 * i + t) * P:(2 * i + t + 1) * P], g.ident[:, :])
                ins.then_inc(p_turned, 1)

            def read(i):
                pe.wait_ge(pt_copied[i % 2], i // 2 + 1)
                if i % 2 == 0:
                    pe.wait_ge(nat_loaded[i // 2], 16)
                for t in range(2):
                    m = 2 * i + t
                    for a in range(TA):
                        ins = nc.tensor.matmul(bank[:, 6 + a, :], pT[:, i % 4, t, a * P:a * P + P], nat[m // 4][:, m % 4, :],
                                               start=m == 0, stop=m == MT - 1)
                ins.then_inc(pv_done, 1)

            pe.wait_ge(exp_done, TA)
            for i in range(MT // 2 + 1):
                if i < MT // 2:
                    turn(i)
                if i >= 1:
                    read(i - 1)

        @block.vector
        def _(dve):
            def link(ins):
                dve.wait_ge(g.dve_step.sem, g.dve_step.inc(ins))

            norm_dve(g, dve, k, link)
            dve.wait_ge(mask_loaded, 16)
            link(nc.vector.tensor_scalar(mb[:, :], mask8[:, :], 1.0, 1e30, ALU.subtract, ALU.mult))
            link(nc.vector.tensor_reduce(okay[:, :], mb[:, :], AX.X, ALU.max))
            link(nc.vector.tensor_scalar(okay[:, :], okay[:, :], -1.0, None, ALU.is_ge))
            for a in range(TA):
                for c in range(MC):
                    i = a * MC + c
                    dve.wait_ge(s_ready, i + 1)
                    nc.vector.tensor_tensor(pr[:, a, c * 512:c * 512 + 512], bank[:, i % 4, :], mb[:, c * 512:c * 512 + 512],
                                            ALU.add).then_inc(s_masked, 1)
                    dve.wait_ge(s_masked, i + 1)
                    n = nc.vector.tensor_reduce(pmx[:, a, c:c + 1], pr[:, a, c * 512:c * 512 + 512], AX.X, ALU.max)
                    if c == MC - 1:
                        link(n)
                link(nc.vector.tensor_reduce(nmx[:, a:a + 1], pmx[:, a, :], AX.X, ALU.max))
                nc.vector.tensor_scalar(nmx[:, a:a + 1], nmx[:, a:a + 1], -SC, None, ALU.mult).then_inc(maxed, 1)
            for i in range(1, MT // 2, 2):
                dve.wait_ge(p_turned, i + 1)
                if i >= 4:
                    dve.wait_ge(pv_done, i - 3)
                nc.vector.tensor_copy(pT[:, i % 4].rearrange("p t n -> p (t n)"), bank[:, 4 + i % 2, :]).then_inc(pt_copied[1], 1)
            link(nc.vector.reciprocal(den[:, :], den[:, :]))
            link(nc.vector.tensor_scalar(den[:, :], den[:, :], okay[:, 0:1], None, ALU.mult))
            dve.wait_ge(pv_done, MT // 2)
            for a in range(TA):
                link(nc.vector.scalar_tensor_tensor(out=X[:, a, :], in0=bank[:, 6 + a, :], scalar=den[:, a:a + 1],
                                                    in1=X[:, a, :], op0=ALU.mult, op1=ALU.add))

        @block.scalar
        def _(act):
            norm_act(g, act, k)
            norm_turn_act(g, act, k)
            for a in range(TA):
                act.wait_ge(maxed, a + 1)
                nc.scalar.activation(pr[:, a, :], pr[:, a, :], ACT.Exp, scale=SC, bias=nmx[:, a:a + 1],
                                     accum_out=den[:, a:a + 1]).then_inc(exp_done, 1)
            for i in range(0, MT // 2, 2):
                act.wait_ge(p_turned, i + 1)
                if i >= 4:
                    act.wait_ge(pv_done, i - 3)
                nc.scalar.copy(pT[:, i % 4].rearrange("p t n -> p (t n)"), bank[:, 4 + i % 2, :]).then_inc(pt_copied[0], 1)


H0, K0 = 16, 32
H1, K1, KV1 = 32, 64, 8
E0, I0 = 32, 256
E1, I1 = 8, 352
W0 = 2 * DC * I0 + 2 * D
W1 = 2 * DC * I1 + 3 * D
BIAS = 512 + 512 + 2048 + D


def perceiver(nc, ins, out, stages=6):
    with ExitStack() as ctx:
        g = setup(nc, ctx)
        sem, at = g.sem, g.area.at

        def sb(name, shape, dt=F32):
            return ctx.enter_context(nc.sbuf_tensor(name, shape, dt))

        g.causal = sb("causal_mask", [P, 3 * P])
        g.left = sb("left_of", [P, E0, E0])
        table0 = sb("rope0", [P, 2, TA, 2, K0])
        table1 = sb("rope1", [P, 2, TA, 2, K1])
        gate0 = sb("gate0_w", [P, DC, E0])
        gate1 = sb("gate1_w", [P, DC, E1])
        kw1 = sb("kw1_row", [P, H1])
        small_loaded = sem("small_loaded")
        w_attn0 = at(0, "w_attn0_sb", [P, 4, DC, D])
        w_attn0_loaded = sem("w_attn0_loaded")
        slots0 = [at(130 + 12 * s, f"slot0_{s}", [P, W0])[:, :] for s in range(SLOTS)]
        slot0_loaded = [sem(f"slot0_loaded{s}") for s in range(SLOTS)]
        cb0 = at(0, "cb0", [P, E0, T])
        ctxT = [at(60 + 8 * c, f"ctxT{c}", [P, DC, 512]) for c in range(8)]
        ctxT_loaded = [sem(f"ctxT_loaded{c}") for c in range(8)]
        wq1 = at(76, "wq1_sb", [P, DC, 2048])
        wk1 = at(108, "wk1_sb", [P, DC, 512])
        wv1 = at(116, "wv1_sb", [P, DC, 512])
        wo1 = at(130, "wo1_sb", [P, 16, D])
        qkv1_loaded = sem("qkv1_loaded")
        wo1_loaded = sem("wo1_loaded")
        bias1_loaded = sem("bias1_loaded")
        bias1 = at(61, "bias1_row", [P, BIAS])
        slots1 = [at(kib, f"slot1_{s}", [P, W1])[:, :] for s, kib in enumerate((76, 93, 162, 110))]
        slot1_loaded = [sem(f"slot1_loaded{s}") for s in range(SLOTS)]
        cb1 = at(0, "cb1", [P, E1, T])

        def loads_a(sp):
            for dst, src in ((g.causal[:, :], ins["causal"]), (g.left[:, :, :].rearrange("p a b -> p (a b)"), ins["left"].partition_broadcast(P)),
                             (table0[:, :, :, :, :], ins["table0"]), (table1[:, :, :, :, :], ins["table1"]), (gate0[:, :, :], ins["gate0"]),
                             (gate1[:, :, :], ins["gate1"]), (kw1[:, :], ins["kw1"].partition_broadcast(P))):
                sp.dma_start(dst, src).then_inc(small_loaded, 16)
            sp.dma_start(w_attn0[:, :, :, :], ins["w_attn0"]).then_inc(w_attn0_loaded, 16)

        def loads_b(sp):
            for n in range(SLOTS):
                s = (n + 2) % SLOTS
                sp.dma_start(slots0[s], ins["wall0"][n]).then_inc(slot0_loaded[s], 16)

        def loads_c(sp):
            for c in range(8):
                sp.dma_start(ctxT[c][:, :, :], ins["ctxT"][c]).then_inc(ctxT_loaded[c], 16)

        def loads_d(sp):
            sp.dma_start(wk1[:, :, :], ins["wk1"]).then_inc(qkv1_loaded, 16)
            sp.dma_start(wv1[:, :, :], ins["wv1"]).then_inc(qkv1_loaded, 16)
            sp.dma_start(wq1[:, :, :], ins["wq1"]).then_inc(qkv1_loaded, 16)

        def load_slot1(sp, n):
            s = (n + 2) % SLOTS
            sp.dma_start(slots1[s], ins["wall1"][n]).then_inc(slot1_loaded[s], 16)

        def loads_e(sp):
            sp.dma_start(bias1[:, :], ins["bias1"].partition_broadcast(P)).then_inc(bias1_loaded, 16)
            sp.dma_start(wo1[:, :, :], ins["wo1"]).then_inc(wo1_loaded, 16)
            load_slot1(sp, 0)

        def later_e(sp):
            for n in range(1, SLOTS):
                load_slot1(sp, n)

        smalls = (small_loaded, 16 * 7)
        cross_attention_0(g, ins["x"], ins["ctx_rows"], ins["ctx_vt"], loads_a)
        if stages > 1:
            self_attention(g, 1, "a0", H0, K0, 4, lambda n: n // 4, lambda n: K0 * n, True,
                       {"q": w_attn0[:, 0], "k": w_attn0[:, 1], "v": w_attn0[:, 2], "o": w_attn0[:, 3]},
                       {"q": table0[:, 0], "k": table0[:, 1]}, None, None, lambda kib, n, s: at(32 + kib, n, s),
                       [smalls, (w_attn0_loaded, 16)], loads_b, None)
        if stages > 2:
            experts(g, 2, "e0", E0, I0, "sigmoid", gate0, [smalls], slots0, slot0_loaded, ins["wall0"],
                lambda kib, n, s: at(32 + kib, n, s), cb0, lambda sp: None, loads_c)
        if stages > 3:
            cross_attention_1(g, 3, ctxT, ctxT_loaded, ins["ctx_chunks"], ins["mask"], lambda sp: None, loads_d)
        if stages > 4:
            b = bias1[:, :]
            self_attention(g, 4, "a1", H1, K1, 16, lambda n: n // 8, lambda n: K1 * (2 * (n // 8) + n % 2), False,
                       {"q": wq1, "k": wk1, "v": wv1, "o": wo1}, {"q": table1[:, 0], "k": table1[:, 1]}, kw1,
                       {"k": b[:, 0:512], "v": b[:, 512:1024], "q": b[:, 1024:3072], "o": b[:, 3072:]},
                       lambda kib, n, s: at(kib, n, s), [smalls, (bias1_loaded, 16), (qkv1_loaded, 48), (wo1_loaded, 16)], loads_e, later_e)
        if stages > 5:
            experts(g, 5, "e1", E1, I1, "softmax", gate1, [smalls], slots1, slot1_loaded, ins["wall1"],
                lambda kib, n, s: at(32 + kib, n, s), cb1, lambda sp: None, None)
        out_stored = sem("out_stored")
        with nc.Block() as block:
            @block.sync
            def _(sp):
                sp.dma_start(out.rearrange("(a p) d -> p a d", p=P), g.X[:, :, :]).then_inc(out_stored, 16)
                sp.wait_ge(out_stored, 16)


def kernel(**inputs):
    import numpy as np
    import concourse.bacc as bacc
    from concourse.bass_utils import run_bass_kernel_spmd

    nc = bacc.Bacc("TRN2", target_bir_lowering=False, num_devices=1)
    c = np.ascontiguousarray
    v = {n: c(a) for n, a in inputs.items()}

    def inner_first(wT, n):
        s = wT.shape
        return c(np.moveaxis(wT.reshape(s[:-2] + (n, P, s[-1])), -3, -2))

    def rope(dim, base, repeat, scale):
        f32 = np.float32
        i = np.arange(dim // 2)
        inv = (base ** (-2.0 * i / dim)).astype(f32) if repeat else (1.0 / (base ** (2.0 * i / dim)).astype(f32)).astype(f32)
        ang = (np.arange(T, dtype=f32)[:, None] * inv[None, :]).astype(np.float64)
        cos, sin = np.cos(ang), np.sin(ang)
        if repeat:
            cs, sn = np.repeat(cos, 2, axis=-1), np.stack([-sin, sin], axis=-1).reshape(T, dim)
        else:
            cs, sn = np.concatenate([cos, cos], -1), np.concatenate([-sin, sin], -1)
        t = np.stack([cs, sn], 1)
        t = np.stack([t * scale, t], 0).astype(f32)
        return c(t.reshape(2, TA, P, 2, dim).transpose(2, 0, 1, 3, 4))

    def all_experts(gate, up, down, width):
        n = gate.shape[0]
        U = -(-width // P)
        dn = np.zeros((n, U * P, D), down.dtype)
        dn[:, :width] = down
        parts = [inner_first(gate, DC), inner_first(up, DC), inner_first(dn, U)]
        return c(np.concatenate([p.reshape(n, P, -1) for p in parts], axis=-1))

    halves = lambda w: w.reshape(D, 2, -1).transpose(1, 0, 2)
    order = [4 * (2 * p + r) + m for p in range(KV1 // 2) for m in range(4) for r in range(2)]
    ctx = v["ctx_2048"]
    tri = np.where(np.tril(np.ones((P, P), bool)), np.float32(0), np.float32(-1e30)).astype(np.float32)
    Wq = v["L1_attn_Wq"].reshape(H1, K1, D)[order].reshape(H1 * K1, D)
    Wo = v["L1_attn_Wo"].reshape(D, H1, K1)[:, order].reshape(D, H1 * K1)
    arrays = {
        "x": v["x"].reshape(T, D),
        "ctx_rows": ctx.reshape(XH, P, 1024),
        "ctx_vt": c(ctx.reshape(XH, XC, XT, P).transpose(0, 3, 2, 1)),
        "ctxT": c(ctx.reshape(8, 512, DC, P).transpose(0, 3, 2, 1)),
        "ctx_chunks": c(ctx.reshape(8, 4, P, D).transpose(0, 2, 1, 3)),
        "mask": v["mask_BxS2_bk0"].reshape(S2),
        "causal": np.concatenate([tri, np.zeros((P, P), np.float32), tri], axis=1),
        "left": np.tril(np.ones((E0, E0), np.float32), -1).reshape(-1),
        "table0": rope(K0, 10000.0, True, float(K0) ** -0.5),
        "table1": rope(K1, 10000.0, False, float(K1) ** -0.5),
        "gate0": inner_first(v["L0_ffn_gate_w"].T, DC),
        "gate1": inner_first(v["L1_ffn_gate_w"], DC),
        "kw1": c(v["L1_attn_key_weights"][order]),
        "bias1": c(np.concatenate([v["L1_attn_bk"], v["L1_attn_bv"], v["L1_attn_bq"].reshape(H1, K1)[order].reshape(-1),
                                   v["L1_attn_bo"]])),
        "w_attn0": c(np.stack([inner_first(v["L0_attn_" + n].T, DC) for n in ("wq", "wk", "wv", "wo")], axis=1)),
        "wk1": inner_first(v["L1_attn_Wk"].T, DC),
        "wv1": inner_first(v["L1_attn_Wv"].T, DC),
        "wq1": inner_first(Wq.T, DC),
        "wo1": inner_first(Wo.T, 16),
        "wall0": all_experts(np.concatenate([halves(v["L0_ffn_sw1"].T), v["L0_ffn_w11"].transpose(0, 2, 1)]),
                             np.concatenate([halves(v["L0_ffn_sw3"].T), v["L0_ffn_w33"].transpose(0, 2, 1)]),
                             np.concatenate([v["L0_ffn_sw2"].T.reshape(2, I0, D), v["L0_ffn_w22"].transpose(0, 2, 1)]), I0),
        "wall1": all_experts(np.concatenate([halves(v["L1_ffn_sw_gate"]), v["L1_ffn_w_gate"]]),
                             np.concatenate([halves(v["L1_ffn_sw_up"]), v["L1_ffn_w_up"]]),
                             np.concatenate([v["L1_ffn_sw_down"].reshape(2, I1, D), v["L1_ffn_w_down"]]), I1),
    }
    ins = {n: nc.dram_tensor(n, a.shape, mybir.dt.from_np(a.dtype), kind="ExternalInput").ap() for n, a in arrays.items()}
    out = nc.dram_tensor("out", (T, D), F32, kind="ExternalOutput").ap()
    perceiver(nc, ins, out, stages=6)
    r = run_bass_kernel_spmd(nc, [arrays], core_ids=[0])
    return r.results[0]["out"].reshape(1, T, D)
```

```python
from contextlib import ExitStack

import concourse.bass as bass
from concourse import mybir

F32 = mybir.dt.float32
BF16 = mybir.dt.bfloat16
F32R = mybir.dt.float32r
ALU = mybir.AluOpType
ACT = mybir.ActivationFunctionType
AX = mybir.AxisListType

P = 128
T = 256
TA = T // P
D = 512
DC = D // P
S2 = 4096
EPS = 1e-5

XH = 16
XC = T // XH
XS = S2 * D // T
XT = XS // P
XHA = P // XC
XSCALE = 0.25
TERMS = [0, 1, 0, 1, 2, 0]
QTERMS = [0, 0, 1, 1, 0, 2]
KR = 6 * XC
LAG = 8


class Count:

    def __init__(self, sem):
        self.sem, self.n = sem, 0

    def inc(self, ins, by=1):
        ins.then_inc(self.sem, by)
        self.n += by
        return self.n




def size(dt):
    return 2 if dt == BF16 else 1 if dt == mybir.dt.uint8 else 4


class Area:

    def __init__(self, nc, lo, hi):
        self.nc, self.base, self.hi = nc, lo, hi

    def at(self, kib, name, shape, dt=F32):
        n = size(dt)
        for d in shape[1:]:
            n *= d
        assert self.base + kib * 1024 + n <= self.hi, (name, kib, n)
        self.end = kib + n / 1024
        return self.nc.alloc_sbuf_tensor_at(name, shape, dt, offset=self.base + int(kib * 1024))


class Shared:
    pass


class Gates:
    pass


def setup(nc, ctx):
    g = Shared()
    g.nc = nc

    def sb(name, shape, dt=F32):
        return ctx.enter_context(nc.sbuf_tensor(name, shape, dt))

    def sem(name):
        return ctx.enter_context(nc.semaphore(name))

    g.sem = sem
    g.bank = ctx.enter_context(nc.psum_tensor("bank", [P, 8, 512], F32))
    g.ident = sb("ident", [P, P])
    g.identb = sb("identb", [P, P], BF16)
    g.X = sb("X", [P, TA, D])
    g.xn = sb("xn", [P, TA, D])
    g.xnT = sb("xnT", [P, DC, T])
    g.stats = sb("stats", [P, TA, 6])
    g.mv = sb("mv", [P, TA, 2])
    g.rstd = sb("rstd", [P, TA, 1])
    g.var = sb("var", [P, TA, 1])
    g.std = sb("std", [P, TA, 1])
    g.arena_size = 184 * 1024
    slab = ctx.enter_context(nc.sbuf_tensor("slab", [P, g.arena_size // 4], F32))
    g.slab = slab
    base = nc.sbuf_base - g.arena_size
    g.area = Area(nc, base, base + g.arena_size)
    g.ident_ready = sem("ident_ready")
    g.dve_step = Count(sem("dve_step"))
    g.var_ready = sem("var_ready")
    g.std_ready = sem("std_ready")
    g.xn_ready = sem("xn_ready")
    g.xn_turned = sem("xn_turned")
    g.xnT_ready = sem("xnT_ready")
    g.stage = 0
    return g


def norm_dve(g, dve, k, link):
    nc = g.nc
    for a in range(TA):
        link(nc.vector.bn_stats(g.stats[:, a, :], g.X[:, a, :]))
        link(nc.vector.bn_aggr(g.mv[:, a, :], g.stats[:, a, :]))
    nc.vector.tensor_scalar(g.var[:, :, :], g.mv[:, :, 1:2], EPS, None, ALU.add).then_inc(g.var_ready, 1)
    dve.wait_ge(g.std_ready, k + 1)
    link(nc.vector.reciprocal(g.rstd[:, :, :], g.std[:, :, :]))
    link(nc.vector.tensor_tensor(g.std[:, :, :], g.rstd[:, :, :], g.rstd[:, :, :], ALU.mult))
    link(nc.vector.tensor_tensor(g.std[:, :, :], g.std[:, :, :], g.var[:, :, :], ALU.mult))
    link(nc.vector.tensor_scalar(g.std[:, :, :], g.std[:, :, :], -0.5, 1.5, ALU.mult, ALU.add))
    link(nc.vector.tensor_tensor(g.rstd[:, :, :], g.rstd[:, :, :], g.std[:, :, :], ALU.mult))
    for a in range(TA):
        nc.vector.tensor_scalar(g.xn[:, a, :], g.X[:, a, :], g.mv[:, a, 0:1], g.rstd[:, a, :],
                                ALU.subtract, ALU.mult).then_inc(g.xn_ready, 1)


def norm_act(g, act, k):
    act.wait_ge(g.var_ready, k + 1)
    g.nc.scalar.activation(g.std[:, :, :], g.var[:, :, :], ACT.Sqrt).then_inc(g.std_ready, 1)


def norm_turn_act(g, act, k):
    for a in range(TA):
        act.wait_ge(g.xn_turned, TA * (k - 1) + a + 1)
        g.nc.scalar.copy(g.xnT[:, :, a * P:a * P + P],
                         g.bank[:, 6 + a, :].rearrange("p (d t) -> p d t", d=DC)).then_inc(g.xnT_ready, 1)


def norm_turn_pe(g, pe, k):
    for a in range(TA):
        pe.wait_ge(g.xn_ready, TA * k + a + 1)
        for d in range(DC):
            ins = g.nc.tensor.transpose(g.bank[:, 6 + a, d * P:d * P + P], g.xn[:, a, d * P:d * P + P], g.ident[:, :])
        ins.then_inc(g.xn_turned, 1)


def cross_attention_0(g, x, ctx_rows, ctx_vt, first_loads):
    nc, sem, bank, ident, identb, X, xn = g.nc, g.sem, g.bank, g.ident, g.identb, g.X, g.xn
    dve_step = g.dve_step
    at = g.area.at
    kraw = at(32, "kraw", [P, 2, 1024])
    kres = at(40, "kres", [P, 1024])
    ksplit = at(44, "ksplit", [P, 3, 1024], BF16)
    kstack = at(50, "kstack", [P, 2, XS], BF16)
    qsplit = at(82, "qsplit", [P, 3, TA, D], BF16)
    qstack = at(88, "qstack", [P, XH, D], BF16)
    vraw = at(104, "vraw", [P, 2, XT, XC])
    vext = at(112, "vext", [P, 2, XT, 2 * XC])
    probs = at(128, "probs", [P, 4, 512])
    osb = at(136, "osb", [P, 2, D])
    nd = at(140, "nd", [P, TA, 4, 2, D])
    pm = at(172, "pm", [P, 2, 4, 8])
    negmax = at(172.25, "negmax", [P, 2, 4])
    nres = at(172.5, "nres", [P, 4])
    nsplit = at(172.75, "nsplit", [P, 4, 3], BF16)
    kscratch = nc.dram_tensor("kscratch", [XH, 3, P, 1024], BF16, kind="Internal").ap()
    qscratch = nc.dram_tensor("qscratch", [3, T, D], BF16, kind="Internal").ap()
    oscratch = nc.dram_tensor("oscratch", [XH, P, D], F32, kind="Internal").ap()
    x_loaded = sem("x_loaded")
    kraw_loaded = [sem("kraw_loaded0"), sem("kraw_loaded1")]
    vraw_loaded = [sem("vraw_loaded0"), sem("vraw_loaded1")]
    split_step = sem("split_step")
    split_stored = sem("split_stored")
    stack_lo = [sem("stack_lo0"), sem("stack_lo1")]
    stack_hi = [sem("stack_hi0"), sem("stack_hi1")]
    const_ready = sem("const_ready")
    v_ready = sem("v_ready")
    qsplit_ready = sem("qsplit_ready")
    qsplit_stored = sem("qsplit_stored")
    q_stacked = sem("q_stacked")
    pre_scores = sem("pre_scores")
    pre_reduced = sem("pre_reduced")
    negmax_ready = sem("negmax_ready")
    nsplit_step = sem("nsplit_step")
    negmax_turned = sem("negmax_turned")
    negmax_stacked = sem("negmax_stacked")
    scores = sem("scores")
    probs_ready = sem("probs_ready")
    pv_done = sem("pv_done")
    o_copied = sem("o_copied")
    o_stored = [sem("o_stored0"), sem("o_stored1")]
    nd_loaded = sem("nd_loaded")
    x_final = sem("x_final")

    with nc.Block() as block:

        def over_heads(eng, phase):
            phase(0, 0, True, False)
            phase(1, 1, False, False)
            with eng.Fori(1, XH // 2 - 1) as i:
                phase(i * 2, 0, False, False)
                phase(i * 2 + 1, 1, False, False)
            phase(XH - 2, 0, False, False)
            phase(XH - 1, 1, False, True)

        @block.sync
        def _(sp):
            sp.dma_start(X[:, :, :], x.rearrange("(a p) d -> p a d", p=P)).then_inc(x_loaded, 16)

            def load_raw(h, b):
                sp.dma_start(kraw[:, b, :], ctx_rows[bass.ds(h, 1)].rearrange("h p n -> (h p) n")).then_inc(kraw_loaded[b], 16)

            def load_v(h, b):
                sp.dma_start(vraw[:, b], ctx_vt[bass.ds(h, 1)].rearrange("h p t c -> (h p) t c")).then_inc(vraw_loaded[b], 16)

            def store_split(h):
                sp.wait_ge(split_step, 4 * h + 4)
                sp.dma_start(kscratch[bass.ds(h, 1)].rearrange("h k p n -> (h p) k n") if isinstance(h, int) else
                             kscratch[bass.ds(h, 1)].rearrange("h k p n -> p (h k) n"), ksplit[:, :, :]).then_inc(split_stored, 16)

            def load_stack(h, b, half, reused):
                if half == 0:
                    sp.wait_ge(split_stored, 16 * h + 16)
                if reused:
                    sp.wait_ge(scores, XT * (h - 2) + XT // 2 * (half + 1))
                lo = half * XS // 2
                for j, part in enumerate(TERMS):
                    src = kscratch[bass.ds(h, 1), part].rearrange("h (c s) n -> (h c) (s n)", c=XC)
                    sp.dma_start(kstack[XC * j:XC * j + XC, b, lo:lo + XS // 2],
                                 src[:, lo:lo + XS // 2]).then_inc([stack_lo, stack_hi][half][b], 16)

            load_raw(0, 0)
            load_raw(1, 1)
            load_v(0, 0)
            load_v(1, 1)
            first_loads(sp)
            store_split(0)
            load_stack(0, 0, 0, False)
            load_stack(0, 0, 1, False)
            sp.wait_ge(qsplit_ready, 4)
            sp.dma_start(qscratch.rearrange("k (a p) t -> p k a t", p=P), qsplit[:, :, :, :]).then_inc(qsplit_stored, 16)
            sp.wait_ge(qsplit_stored, 16)
            for j, part in enumerate(QTERMS):
                sp.dma_start(qstack[XC * j:XC * j + XC, :, :],
                             qscratch[part].rearrange("(h c) t -> c h t", c=XC)).then_inc(q_stacked, 16)

            def phase(h, b, first, last):
                if not last:
                    store_split(h + 1)
                    load_stack(h + 1, 1 - b, 0, not first)
                    load_stack(h + 1, 1 - b, 1, not first)
                if not first:
                    sp.wait_ge(o_copied, h)
                    sp.dma_start(oscratch[bass.ds(h - 1, 1)].rearrange("h p t -> (h p) t"), osb[:, 1 - b, :]).then_inc(o_stored[1 - b], 16)
                if not last and not (isinstance(h, int) and h == XH - 2):
                    sp.wait_ge(split_step, 4 * h + 4)
                    load_raw(h + 2, b)
                    sp.wait_ge(v_ready, h + 1)
                    load_v(h + 2, b)

            over_heads(sp, phase)

            def load_nd(h):
                r = XC * (h % XHA)
                sp.dma_start(nd[r:r + XC, h // XHA].rearrange("c g k t -> c (g k) t"),
                             oscratch[h].rearrange("(q c) t -> c q t", c=XC)).then_inc(nd_loaded, 16)

            sp.wait_ge(o_stored[0], 16 * XH // 2)
            sp.wait_ge(o_stored[1], 16 * (XH // 2 - 1))
            for h in range(XH - 1):
                load_nd(h)
            sp.wait_ge(o_copied, XH)
            sp.dma_start(oscratch[XH - 1], osb[:, 1, :]).then_inc(o_stored[1], 16)
            sp.wait_ge(o_stored[1], 16 * XH // 2)
            load_nd(XH - 1)

        @block.gpsimd
        def _(pool):
            nc.gpsimd.memset(ident[:, :], 0.0).then_inc(g.ident_ready, 1)
            nc.gpsimd.memset(identb[:, :], 0.0).then_inc(g.ident_ready, 1)
            pool.wait_ge(g.ident_ready, 2)
            for m in (ident, identb):
                nc.gpsimd.affine_select(out=m[:, :], in_=m[:, :], compare_op=ALU.not_equal, fill=1.0, base=0,
                                        pattern=[[-1, P]], channel_multiplier=1).then_inc(g.ident_ready, 1)

            def split(h, b, first):
                if first:
                    pool.wait_ge(kraw_loaded[b], 16)
                else:
                    pool.wait_ge(kraw_loaded[b], (h - b) * 8 + 16)
                if not (isinstance(h, int) and h == 0):
                    pool.wait_ge(split_stored, 16 * h)
                nc.gpsimd.tensor_copy(ksplit[:, 0, :], kraw[:, b, :]).then_inc(split_step, 1)
                pool.wait_ge(split_step, 4 * h + 1)
                nc.gpsimd.tensor_tensor(kres[:, :], kraw[:, b, :], ksplit[:, 0, :], ALU.subtract).then_inc(split_step, 1)
                pool.wait_ge(split_step, 4 * h + 2)
                nc.gpsimd.tensor_copy(ksplit[:, 1, :], kres[:, :]).then_inc(split_step, 1)
                pool.wait_ge(split_step, 4 * h + 3)
                nc.gpsimd.tensor_tensor(ksplit[:, 2, :], kres[:, :], ksplit[:, 1, :], ALU.subtract).then_inc(split_step, 1)

            def values(h, b, reused):
                pool.wait_ge(vraw_loaded[b], (h - b) * 8 + 16)
                if reused:
                    pool.wait_ge(pv_done, XT * (h - 1))
                nc.gpsimd.tensor_copy(vext[:, b, :, 0:XC], vraw[:, b]).then_inc(v_ready, 1)

            split(0, 0, True)
            split(1, 1, True)
            values(0, 0, False)

            def phase(h, b, first, last):
                pool.wait_ge(negmax_ready, h + 1)
                if not first:
                    pool.wait_ge(negmax_turned, h)
                nc.gpsimd.tensor_copy(nsplit[:, :, 0], negmax[:, b, :]).then_inc(nsplit_step, 1)
                pool.wait_ge(nsplit_step, 4 * h + 1)
                nc.gpsimd.tensor_tensor(nres[:, :], negmax[:, b, :], nsplit[:, :, 0], ALU.subtract).then_inc(nsplit_step, 1)
                pool.wait_ge(nsplit_step, 4 * h + 2)
                nc.gpsimd.tensor_copy(nsplit[:, :, 1], nres[:, :]).then_inc(nsplit_step, 1)
                pool.wait_ge(nsplit_step, 4 * h + 3)
                nc.gpsimd.tensor_tensor(nsplit[:, :, 2], nres[:, :], nsplit[:, :, 1], ALU.subtract).then_inc(nsplit_step, 1)
                if not last:
                    values(h + 1, 1 - b, not first)
                if not last and not (isinstance(h, int) and h == XH - 2):
                    split(h + 2, b, False)

            for h in range(XH):
                phase(h, h % 2, h == 0, h == XH - 1)

        @block.vector
        def _(dve):
            def link(ins):
                dve.wait_ge(dve_step.sem, dve_step.inc(ins))

            nc.vector.memset(kstack[96:99, :, :], 1.0).then_inc(const_ready, 1)
            nc.vector.memset(vext[:, :, :, XC:], 1.0).then_inc(const_ready, 1)
            dve.wait_ge(x_loaded, 16)
            norm_dve(g, dve, 0, link)
            dve.wait_ge(g.xn_ready, TA)
            nc.vector.tensor_copy(qsplit[:, 0], xn[:, :, :]).then_inc(qsplit_ready, 1)
            dve.wait_ge(qsplit_ready, 1)
            link(nc.vector.tensor_tensor(xn[:, :, :], xn[:, :, :], qsplit[:, 0], ALU.subtract))
            nc.vector.tensor_copy(qsplit[:, 1], xn[:, :, :]).then_inc(qsplit_ready, 1)
            dve.wait_ge(qsplit_ready, 2)
            nc.vector.tensor_tensor(qsplit[:, 2], xn[:, :, :], qsplit[:, 1], ALU.subtract).then_inc(qsplit_ready, 2)

            def reduces(h, b, rs):
                for r in rs:
                    dve.wait_ge(pre_scores, 32 * h + r + 1)
                    nc.vector.tensor_reduce(pm[:, b, r % 4, r // 4:r // 4 + 1], bank[:, 2 * (r % 2):2 * (r % 2) + 2, :],
                                            AX.XY, ALU.max).then_inc(pre_reduced, 1)

            reduces(0, 0, range(32))

            def phase(h, b, first, last):
                dve.wait_ge(pre_reduced, 32 * h + 32)
                nc.vector.tensor_reduce(negmax[:, b, :], pm[:, b], AX.X, ALU.max, negate=True).then_inc(negmax_ready, 1)
                if not last:
                    reduces(h + 1, 1 - b, range(3))
                dve.wait_ge(negmax_turned, h + 1)
                nc.vector.tensor_copy(qstack[96:99, bass.ds(h, 1), :], bank[96:99, 7:8, :]).then_inc(negmax_stacked, 1)
                if not last:
                    reduces(h + 1, 1 - b, range(3, 32))

            over_heads(dve, phase)
            dve.wait_ge(nd_loaded, 16 * XH)
            for q in range(1, 4):
                link(nc.vector.tensor_tensor(nd[:, :, 0], nd[:, :, 0], nd[:, :, q], ALU.add))
            link(nc.vector.reciprocal(nd[:, :, 1, 1, :], nd[:, :, 0, 1, :]))
            link(nc.vector.tensor_tensor(nd[:, :, 0, 0, :], nd[:, :, 0, 0, :], nd[:, :, 1, 1, :], ALU.mult))
            nc.vector.tensor_tensor(X[:, :, :], X[:, :, :], nd[:, :, 0, 0, :], ALU.add).then_inc(x_final, 1)
            dve.wait_ge(x_final, 1)

        @block.scalar
        def _(act):
            def exps(h, b, n, first):
                m = XT * b + n
                act.wait_ge(scores, XT * h + n + 1)
                if not (first and n < 4):
                    act.wait_ge(pv_done, XT * h + n - 3)
                nc.scalar.activation(probs[:, m % 4, :], bank[:, 4 + m % 2, :], ACT.Exp, scale=XSCALE).then_inc(probs_ready, 1)

            def copy_o(h, b, first):
                act.wait_ge(pv_done, XT * h + XT)
                if not first:
                    act.wait_ge(o_stored[b], (h - b) * 8)
                nc.scalar.copy(osb[:, b, :], bank[:, 6, :]).then_inc(o_copied, 1)

            def phase(h, b, first, last):
                for n in range(XT):
                    exps(h, b, n, first)
                    if n == 1 and not first:
                        copy_o(h - 1, 1 - b, isinstance(h, int) and h <= 2)

            norm_act(g, act, 0)
            over_heads(act, phase)
            copy_o(XH - 1, 1, False)

        @block.tensor
        def _(pe):
            def pre(h, b, n):
                r = n // 2
                c, tt = r // 4, r % 4
                if n % 2 == 0 and not (isinstance(h, int) and h == 0 and r < 2):
                    pe.wait_ge(pre_reduced, 32 * h + r - 1)
                if n == 0:
                    pe.wait_ge(stack_lo[b], (h - b) * 48 + 96)
                if n == 32:
                    pe.wait_ge(stack_hi[b], (h - b) * 48 + 96)
                k = c * 1024 + 512 * (n % 2)
                ins = nc.tensor.matmul(bank[:, 2 * (r % 2) + n % 2, :], qof(h, slice(0, KR))[:, tt * P:tt * P + P],
                                       kstack[0:KR, b, k:k + 512], start=True, stop=True)
                if n % 2:
                    ins.then_inc(pre_scores, 1)

            def qof(h, rows):
                if isinstance(h, int):
                    return qstack[rows, h, :]
                return qstack[rows, bass.ds(h, 1), :].rearrange("p h t -> p (h t)")

            def score(h, b, n, first):
                m = XT * b + n
                if n == 0:
                    pe.wait_ge(negmax_stacked, h + 1)
                if not (first and n < 2):
                    pe.wait_ge(probs_ready, XT * h + n - 1)
                nc.tensor.matmul(bank[:, 4 + m % 2, :], kstack[0:KR + 3, b, n * P:n * P + P], qof(h, slice(0, KR + 3)),
                                 start=True, stop=True).then_inc(scores, 1)

            def pv(h, b, n, first):
                m = XT * b + n
                pe.wait_ge(probs_ready, XT * h + n + 1)
                if n == 0:
                    pe.wait_ge(v_ready, h + 1)
                    if not first:
                        pe.wait_ge(o_copied, h)
                q = n % 4
                nc.tensor.matmul(bank[32 * q:32 * q + 32, 6, :], vext[:, b, n, :], probs[:, m % 4, :],
                                 start=n < 4, stop=n >= XT - 4).then_inc(pv_done, 1)

            pe.wait_ge(const_ready, 2)
            pe.wait_ge(g.ident_ready, 4)
            pe.wait_ge(q_stacked, 96)
            for n in range(64):
                pre(0, 0, n)

            def main_step(h, b, s, first):
                for fn, lag in ((score, LAG), (pv, LAG + 2)):
                    if s >= lag:
                        fn(h, b, s - lag, first)
                    elif not first:
                        fn(h - 1, 1 - b, XT + s - lag, False)

            def phase(h, b, first, last):
                for s in range(XT):
                    if s == 4:
                        pe.wait_ge(nsplit_step, 4 * h + 4)
                        if not first:
                            pe.wait_ge(negmax_stacked, h)
                        for tt in range(4):
                            ins = nc.tensor.matmul(bank[96:99, 7, tt * P:tt * P + P], nsplit[:, tt, :], identb[:, :],
                                                   start=True, stop=True)
                        ins.then_inc(negmax_turned, 1)
                    if not last:
                        pre(h + 1, 1 - b, s)
                    main_step(h, b, s, first)

            over_heads(pe, phase)
            for s in range(LAG):
                score(XH - 1, 1, XT + s - LAG, False)
                pv(XH - 1, 1, XT + s - LAG - 2, False)
            pv(XH - 1, 1, XT - 2, False)
            pv(XH - 1, 1, XT - 1, False)




def self_attention(g, k, name, heads, dk, q_tiles, kv_tile_of, v_col_of, pairs, w, table, kw, bias, area_at, loaded,
                   first_loads, later_loads):
    nc, sem, bank, X = g.nc, g.sem, g.bank, g.X
    per = P // dk
    NQ = q_tiles * P
    jobs = [("k", 0, a) for a in range(TA)] + [("v", 0, a) for a in range(TA)]
    jobs += [("q", c, a) for c in range(NQ // 512) for a in range(TA)]

    at = lambda kib, what, shape: area_at(kib, f"{name}_{what}", shape)
    qtok = at(0, "qtok", [P, TA, NQ])
    kib = TA * NQ * 4 / 1024
    ktok = at(kib, "ktok", [P, TA, 512])
    vtok = at(kib + 4, "vtok", [P, TA, 512])
    rot = at(kib + 8, "rot", [P, 3, 2, 512])
    qT = at(kib + 20, "qT", [P, q_tiles, T])
    kT = at(2 * kib + 20, "kT", [P, 4, T])
    soft = at(2 * kib + 24, "soft", [P, 3, 3 * P])
    turned_sb = rot[:, 0:2].rearrange("p a b n -> p (a b n)")[:, 0:2 * 3 * P].rearrange("p (r n) -> p r n", r=2)
    aoT = at(0, "aoT", [P, q_tiles, T])
    small = at(2 * kib + 28.5, "small", [P, 4, 2])
    nmax = small[:, 0:2]
    denom = small[:, 2:4]
    rden = at(2 * kib + 28.75, "rden", [P, 2, 2])

    proj_done = sem(name + "_proj_done")
    rot_step = Count(sem(name + "_rot_step"))
    rotated = sem(name + "_rotated")
    v_copied = sem(name + "_v_copied")
    turned = sem(name + "_turned")
    turn_copied = sem(name + "_turn_copied")
    s_ready = sem(name + "_s_ready")
    masked = sem(name + "_masked")
    maxed = sem(name + "_maxed")
    exp_done = sem(name + "_exp_done")
    inverted = sem(name + "_inverted")
    normed = sem(name + "_normed")
    p_turned = sem(name + "_p_turned")
    pt_copied = sem(name + "_pt_copied")
    pv_done = sem(name + "_pv_done")
    ao_copied = sem(name + "_ao_copied")
    out_done = sem(name + "_out_done")

    rot_jobs = [j for j, (kind, c, a) in enumerate(jobs) if kind != "v"]
    v_jobs = [j for j, (kind, c, a) in enumerate(jobs) if kind == "v"]

    with nc.Block() as block:

        @block.sync
        def _(sp):
            first_loads(sp)
            if later_loads:
                sp.wait_ge(proj_done, len(jobs))
                later_loads(sp)

        @block.tensor
        def _(pe):
            norm_turn_pe(g, pe, k)
            pe.wait_ge(g.xnT_ready, TA * k)
            for s, n in loaded:
                pe.wait_ge(s, n)

            def project(j):
                kind, c, a = jobs[j]
                if j >= 4:
                    if jobs[j - 4][0] == "v":
                        pe.wait_ge(v_copied, v_jobs.index(j - 4) + 1)
                    else:
                        pe.wait_ge(rotated, rot_jobs.index(j - 4) + 1)
                for d in range(DC):
                    ins = nc.tensor.matmul(bank[:, j % 4, :], g.xnT[:, d, a * P:a * P + P],
                                           w[kind][:, d, 512 * c:512 * c + 512], start=d == 0, stop=d == DC - 1)
                ins.then_inc(proj_done, 1)

            def turn(r):
                kind, c, a = jobs[rot_jobs[r]]
                pe.wait_ge(rotated, r + 1)
                if r >= 2:
                    pe.wait_ge(turn_copied, r - 1)
                src = (ktok if kind == "k" else qtok)[:, a, 512 * c:512 * c + 512]
                for f in range(4):
                    ins = nc.tensor.transpose(bank[:, 4 + r % 2, f * P:f * P + P], src[:, f * P:f * P + P], g.ident[:, :])
                ins.then_inc(turned, 1)

            r = 0
            for j in range(len(jobs)):
                project(j)
                while r < len(rot_jobs) and rot_jobs[r] <= j - 2:
                    turn(r)
                    r += 1
            for r in range(r, len(rot_jobs)):
                turn(r)
            pe.wait_ge(turn_copied, len(rot_jobs))
            pe.wait_ge(v_copied, TA)

            def scores(n):
                if n >= 2:
                    pe.wait_ge(masked, n - 1)
                b, r0, q, kt = bank[:, n % 2, :], dk * (n % per), n // per, kv_tile_of(n)
                nc.tensor.matmul(b[:, 0:P], qT[r0:r0 + dk, q, 0:P], kT[r0:r0 + dk, kt, 0:P], start=True, stop=True)
                nc.tensor.matmul(b[:, P:3 * P], qT[r0:r0 + dk, q, P:T], kT[r0:r0 + dk, kt, :],
                                 start=True, stop=True).then_inc(s_ready, 1)

            def turn_probs(n):
                pe.wait_ge(normed, n + 1)
                if n >= 2:
                    pe.wait_ge(pt_copied, n - 1)
                for f in range(3):
                    ins = nc.tensor.transpose(bank[:, 2 + n % 2, f * P:f * P + P], soft[:, n % 3, f * P:f * P + P], g.ident[:, :])
                ins.then_inc(p_turned, 1)

            def values(n):
                pe.wait_ge(pt_copied, n + 1)
                q, r0, v0 = n // per, dk * (n % per), v_col_of(n)
                if n % per == 0 and q >= 2:
                    pe.wait_ge(ao_copied, q - 1)
                b = bank[r0:r0 + dk, 4 + q % 2, :]
                nc.tensor.matmul(b[:, 0:T], vtok[:, 0, v0:v0 + dk], turned_sb[:, n % 2, 0:T], start=True, stop=False)
                nc.tensor.matmul(b[:, P:T], vtok[:, 1, v0:v0 + dk], turned_sb[:, n % 2, T:3 * P],
                                 start=False, stop=True).then_inc(pv_done, 1)

            for n in range(heads + 3):
                if n < heads:
                    scores(n)
                if 0 <= n - 2 < heads:
                    turn_probs(n - 2)
                if 0 <= n - 3 < heads:
                    values(n - 3)
            for q in range(q_tiles):
                if q == q_tiles - 1 or q == 0:
                    pe.wait_ge(ao_copied, q_tiles if q else q_tiles - 1)
                for a in range(TA):
                    ins = nc.tensor.matmul(bank[:, 6 + a, :], aoT[:, q, a * P:a * P + P], w["o"][:, q, :],
                                           start=q == 0, stop=q == q_tiles - 1)
            ins.then_inc(out_done, 1)

        @block.vector
        def _(dve):
            def link(ins):
                dve.wait_ge(g.dve_step.sem, g.dve_step.inc(ins))

            norm_dve(g, dve, k, link)

            def rotate(r):
                kind, c, a = jobs[rot_jobs[r]]
                j = rot_jobs[r]
                dve.wait_ge(proj_done, j + 1)
                src = bank[:, j % 4, :]
                if bias is not None:
                    row = bias[kind][:, 512 * c:512 * c + 512]
                    dve.wait_ge(rot_step.sem, rot_step.inc(nc.vector.tensor_tensor(rot[:, 2, r % 2, :], src, row, ALU.add)))
                    src = rot[:, 2, r % 2, :]
                tab = table[kind]
                cos = tab[:, a, 0, :].unsqueeze(1).to_broadcast([P, 512 // dk, dk])
                fold = "p (h i two) -> p h i two" if pairs else "p (h two i) -> p h i two"
                tfold = "p (i two) -> p i two" if pairs else "p (two i) -> p i two"
                sin = tab[:, a, 1, :].rearrange(tfold, two=2)
                x4 = src.rearrange(fold, i=dk // 2, two=2)
                o4 = rot[:, 1, r % 2, :].rearrange(fold, i=dk // 2, two=2)
                rot_step.inc(nc.vector.tensor_tensor(rot[:, 0, r % 2, :].rearrange("p (h i) -> p h i", i=dk),
                                                     src.rearrange("p (h i) -> p h i", i=dk), cos, ALU.mult))
                for t in range(2):
                    s1 = sin[:, :, t].unsqueeze(1).to_broadcast([P, 512 // dk, dk // 2])
                    n = rot_step.inc(nc.vector.tensor_tensor(o4[:, :, :, t], x4[:, :, :, 1 - t], s1, ALU.mult))
                dve.wait_ge(rot_step.sem, n)
                dst = (ktok if kind == "k" else qtok)[:, a, 512 * c:512 * c + 512]
                if kind == "q" and kw is not None:
                    n = rot_step.inc(nc.vector.tensor_tensor(rot[:, 0, r % 2, :], rot[:, 0, r % 2, :], rot[:, 1, r % 2, :], ALU.add))
                    dve.wait_ge(rot_step.sem, n)
                    f = kw[:, 512 // dk * c:512 // dk * (c + 1)].unsqueeze(2).to_broadcast([P, 512 // dk, dk])
                    nc.vector.tensor_tensor(dst.rearrange("p (h i) -> p h i", i=dk),
                                            rot[:, 0, r % 2, :].rearrange("p (h i) -> p h i", i=dk), f, ALU.mult).then_inc(rotated, 1)
                else:
                    nc.vector.tensor_tensor(dst, rot[:, 0, r % 2, :], rot[:, 1, r % 2, :], ALU.add).then_inc(rotated, 1)

            for s, n in loaded:
                dve.wait_ge(s, n)
            for r in range(len(rot_jobs)):
                rotate(r)
                if r == 1:
                    for a in range(TA):
                        j = v_jobs[a]
                        dve.wait_ge(proj_done, j + 1)
                        if bias is not None:
                            nc.vector.tensor_tensor(vtok[:, a, :], bank[:, j % 4, :], bias["v"], ALU.add).then_inc(v_copied, 1)
                        else:
                            nc.vector.tensor_copy(vtok[:, a, :], bank[:, j % 4, :]).then_inc(v_copied, 1)

            def mask_max(n):
                dve.wait_ge(s_ready, n + 1)
                if n >= 3:
                    dve.wait_ge(p_turned, n - 2)
                nc.vector.tensor_tensor(soft[:, n % 3, :], bank[:, n % 2, 0:3 * P], g.causal[:, :], ALU.add).then_inc(masked, 1)
                dve.wait_ge(masked, n + 1)
                if n >= 2:
                    dve.wait_ge(exp_done, 2 * n - 2)
                nc.vector.tensor_reduce(nmax[:, n % 2, 0:1], soft[:, n % 3, 0:P], AX.X, ALU.max, negate=True).then_inc(maxed, 1)
                nc.vector.tensor_reduce(nmax[:, n % 2, 1:2], soft[:, n % 3, P:3 * P], AX.X, ALU.max, negate=True).then_inc(maxed, 1)

            def invert(n):
                dve.wait_ge(exp_done, 2 * n + 2)
                if n >= 2:
                    dve.wait_ge(normed, n - 1)
                nc.vector.reciprocal(rden[:, n % 2, :], denom[:, n % 2, :]).then_inc(inverted, 1)

            def copy_ao(q):
                dve.wait_ge(pv_done, per * q + per)
                nc.vector.tensor_copy(aoT[:, q, :], bank[:, 4 + q % 2, 0:T]).then_inc(ao_copied, 1)

            for n in range(heads + 5):
                if n < heads:
                    mask_max(n)
                if 0 <= n - 1 < heads:
                    invert(n - 1)
                if 0 <= n - 4 < heads and (n - 4) % per == per - 1:
                    copy_ao((n - 4) // per)
            dve.wait_ge(out_done, 1)
            for a in range(TA):
                link(nc.vector.tensor_tensor(X[:, a, :], X[:, a, :], bank[:, 6 + a, :], ALU.add))
                if bias is not None:
                    link(nc.vector.tensor_tensor(X[:, a, :], X[:, a, :], bias["o"], ALU.add))

        @block.gpsimd
        def _(pool):
            for n in range(heads):
                pool.wait_ge(inverted, n + 1)
                nc.gpsimd.tensor_scalar(soft[:, n % 3, 0:P], soft[:, n % 3, 0:P], rden[:, n % 2, 0:1], None, ALU.mult)
                nc.gpsimd.tensor_scalar(soft[:, n % 3, P:3 * P], soft[:, n % 3, P:3 * P], rden[:, n % 2, 1:2], None,
                                        ALU.mult).then_inc(normed, 1)

        @block.scalar
        def _(act):
            norm_act(g, act, k)
            norm_turn_act(g, act, k)
            for r in range(len(rot_jobs)):
                kind, c, a = jobs[rot_jobs[r]]
                act.wait_ge(turned, r + 1)
                dst = kT if kind == "k" else qT
                nc.scalar.copy(dst[:, 4 * c:4 * c + 4, a * P:a * P + P],
                               bank[:, 4 + r % 2, :].rearrange("p (f t) -> p f t", f=4)).then_inc(turn_copied, 1)

            def exps(n):
                act.wait_ge(maxed, 2 * n + 2)
                if n >= 2:
                    act.wait_ge(inverted, n - 1)
                for a, cols in enumerate((slice(0, P), slice(P, 3 * P))):
                    nc.scalar.activation(soft[:, n % 3, cols], soft[:, n % 3, cols], ACT.Exp, bias=nmax[:, n % 2, a:a + 1],
                                         accum_out=denom[:, n % 2, a:a + 1]).then_inc(exp_done, 1)

            def copy_turned(n):
                act.wait_ge(p_turned, n + 1)
                if n >= 2:
                    act.wait_ge(pv_done, n - 1)
                nc.scalar.copy(turned_sb[:, n % 2, :], bank[:, 2 + n % 2, 0:3 * P]).then_inc(pt_copied, 1)

            for n in range(heads + 2):
                if n < heads:
                    exps(n)
                if n >= 2:
                    copy_turned(n - 2)


def experts(g, k, name, E, width, choose, gate_w, gate_loaded, raw, raw_loaded, wall, cb, parts_at, hi_at, lo_at, AHEAD,
            first_loads, later_loads):
    nc, sem, bank, X = g.nc, g.sem, g.bank, g.X
    rows = [min(P, width - u * P) for u in range(-(-width // P))]
    U = len(rows)
    N = E + 2
    WU = 2 * DC * P + D

    at = lambda kib, what, shape, dt=F32: g.area.at(kib, f"{name}_{what}", shape, dt)
    hi = [at(s, f"hi{n}", [P, U, WU], F32R) for n, s in enumerate(hi_at)]
    lo = [at(s, f"lo{n}", [P, U, WU], F32R) for n, s in enumerate(lo_at)]
    R = len(hi)
    silu = at(parts_at, "silu", [P, 4, T])
    acts = at(parts_at + 4, "acts", [P, 2, T])
    ahi = at(parts_at + 6, "ahi", [P, 4, T], F32R)
    alo = at(parts_at + 10, "alo", [P, 4, T], F32R)
    xhi = at(parts_at + 14, "xhi", [P, DC, T], F32R)
    xlo = at(parts_at + 18, "xlo", [P, DC, T], F32R)
    gates = Gates()
    gates.z = at(parts_at + 22, "z", [P, TA, E])
    gates.s = at(parts_at + 22.25, "s", [P, TA, E])
    gates.c = at(parts_at + 22.5, "c", [P, TA, E])
    gates.t = at(parts_at + 22.75, "t", [P, TA, E])
    gates.r = at(parts_at + 23, "r", [P, TA, E])
    gates.g8 = at(parts_at + 23.25, "g8", [P, TA, 8])
    gates.m = at(parts_at + 23.375, "m", [P, TA, 8])
    gates.one = at(parts_at + 23.5, "one", [P, TA, 1])
    gates.gt = at(0, "gt", [P, TA, E])
    gates.eq = at(0.25, "eq", [P, TA, E])
    gates.pre = at(0.5, "pre", [P, TA, E])
    gates.m8 = at(0.75, "m8", [P, TA, 8])
    cT = at(parts_at + 23.625, "cT", [E, T])
    cscratch = nc.dram_tensor(name + "_cscratch", [E, T], F32, kind="Internal").ap()

    z_ready = sem(name + "_z_ready")
    gate_exp = sem(name + "_gate_exp")
    gate_in = sem(name + "_gate_in")
    c_ready = sem(name + "_c_ready")
    c_turned = sem(name + "_c_turned")
    c_copied = sem(name + "_c_copied")
    c_stored = sem(name + "_c_stored")
    c_first = sem(name + "_c_first")
    c_spread = sem(name + "_c_spread")
    x_hi = sem(name + "_x_hi")
    x_lo = sem(name + "_x_lo")
    w_hi = sem(name + "_w_hi")
    w_lo = sem(name + "_w_lo")
    gu_ready = sem(name + "_gu_ready")
    silu_ready = sem(name + "_silu_ready")
    weighted = sem(name + "_weighted")
    act_made = sem(name + "_act_made")
    act_hi = sem(name + "_act_hi")
    act_ready = sem(name + "_act_ready")
    down_done = sem(name + "_down_done")

    def over_units(eng, step):
        for n in range(2):
            for j in range(U):
                step(n, n, j)
        for n in range(2, 6):
            for j in range(U):
                step(n, n % 4, j)
        if E > 8:
            with eng.Fori(1, E // 4 - 1) as i:
                for s in range(2, 6):
                    for j in range(U):
                        step(i * 4 + s, s % 4, j)
        for n in range(N - 4, N):
            for j in range(U):
                step(n, n % 4, j)

    def place(s, j):
        return (U * s + j) % 4

    def later(n, s, j, d):
        q, jj = divmod(j + d, U)
        if isinstance(n, int) and n + q >= N:
            return None
        return n + q, (s + q) % 4, jj

    def cut_high(act, n, s, j):
        if j == 0:
            act.wait_ge(raw_loaded[s % 2], (n - s % 2) * 8 + 16)
        if not (isinstance(n, int) and n < R):
            act.wait_ge(down_done, (n - R) * U + (j + 1))
        nc.scalar.copy(hi[s % R][:, j, :], raw[s % 2][:, j, :]).then_inc(w_hi, 1)

    def cut_rest(dve, n, s, j):
        dve.wait_ge(w_hi, n * U + (j + 1))
        nc.vector.tensor_tensor(lo[s % R][:, j, :], raw[s % 2][:, j, :], hi[s % R][:, j, :].bitcast(F32),
                                ALU.subtract).then_inc(w_lo, 1)

    with nc.Block() as block:

        def spread_c(sp):
            sp.wait_ge(c_copied, 1)
            sp.dma_start(cscratch, cT[:, :]).then_inc(c_stored, 16)
            sp.wait_ge(c_stored, 16)
            for lo_e, hi_e, s in ((0, 4, c_first), (4, E, c_spread)):
                sp.dma_start(cb[:, lo_e:hi_e, :].rearrange("p e t -> p (e t)"),
                             cscratch[lo_e:hi_e].rearrange("e t -> (e t)").partition_broadcast(P)).then_inc(s, 16)

        @block.sync
        def _(sp):
            first_loads(sp)
            for n in range(2, N):
                if n == 4:
                    spread_c(sp)
                sp.wait_ge(w_lo, U * (n - 1))
                sp.dma_start(raw[n % 2][:, :, :].rearrange("p u w -> p (u w)"), wall[n]).then_inc(raw_loaded[n % 2], 16)
            if later_loads:
                later_loads(sp)

        @block.tensor
        def _(pe):
            norm_turn_pe(g, pe, k)
            pe.wait_ge(g.xnT_ready, TA * k)
            for s, n in gate_loaded:
                pe.wait_ge(s, n)
            for a in range(TA):
                for d in range(DC):
                    ins = nc.tensor.matmul(bank[:, 6, a * E:a * E + E], g.xnT[:, d, a * P:a * P + P], gate_w[:, d, :],
                                           start=d == 0, stop=d == DC - 1)
            ins.then_inc(z_ready, 1)
            pe.wait_ge(x_lo, 1)

            def down(n, s, j, last=False):
                u, r = n * U + j, rows[j]
                b = place(s, j)
                dn = 2 * DC * P
                pe.wait_ge(act_ready, u + 1)
                for a in range(TA):
                    for p, (l, w) in enumerate(((ahi, hi[s % R]), (alo, hi[s % R]), (ahi, lo[s % R]))):
                        ins = nc.tensor.matmul(bank[:, 4 + a, :], l[0:r, b, a * P:a * P + P], w[0:r, j, dn:dn + D],
                                               start=isinstance(n, int) and n == 0 and j == 0 and p == 0, stop=last and p == 2,
                                               skip_group_check=True)
                ins.then_inc(down_done, 1)

            def step(n, s, j):
                b, u, r = place(s, j), n * U + j, rows[j]
                pe.wait_ge(w_lo, u + 1)
                if not (isinstance(n, int) and u < 4):
                    pe.wait_ge(act_made, u - 3)
                for m in range(2):
                    for d in range(DC):
                        c = (m * DC + d) * P
                        for p, (w, xs) in enumerate(((hi[s % R], xhi), (hi[s % R], xlo), (lo[s % R], xhi))):
                            ins = nc.tensor.matmul(bank[0:r, b, m * T:m * T + T], w[:, j, c:c + r], xs[:, d, :],
                                                   start=d == 0 and p == 0, stop=d == DC - 1 and p == 2)
                ins.then_inc(gu_ready, 1)
                if j >= 2:
                    down(n, s, j - 2)
                elif not (isinstance(n, int) and n == 0):
                    down(n - 1, (s - 1) % 4, U - 2 + j)
                if isinstance(n, int) and n == 1 and j == U - 1:
                    pe.wait_ge(c_ready, 1)
                    for a in range(TA):
                        ins = nc.tensor.transpose(bank[0:E, 7, a * P:a * P + P], gates.c[:, a, :], g.ident[:, :])
                    ins.then_inc(c_turned, 1)

            over_units(pe, step)
            down(N - 1, (N - 1) % 4, U - 2)
            down(N - 1, (N - 1) % 4, U - 1, last=True)

        @block.scalar
        def _(act):
            for d in range(AHEAD):
                cut_high(act, *later(0, 0, 0, d))
            norm_act(g, act, k)
            norm_turn_act(g, act, k)
            act.wait_ge(g.xnT_ready, TA * k)
            nc.scalar.copy(xhi[:, :, :], g.xnT[:, :, :]).then_inc(x_hi, 1)
            if choose == "softmax":
                act.wait_ge(gate_in, 1)
                nc.scalar.activation(gates.s[:, :, :], gates.t[:, :, :], ACT.Exp).then_inc(gate_exp, 1)
            else:
                act.wait_ge(z_ready, 1)
                nc.scalar.activation(gates.s[:, :, :], bank[:, 6, 0:TA * E].rearrange("p (a e) -> p a e", a=TA), ACT.Exp,
                                     scale=-1.0).then_inc(gate_exp, 1)

            def step(n, s, j):
                b, u, r = place(s, j), n * U + j, rows[j]
                act.wait_ge(gu_ready, u + 1)
                if not (isinstance(n, int) and u < 4):
                    act.wait_ge(act_made, u - 3)
                nc.scalar.activation(silu[0:r, b, :], bank[0:r, b, 0:T], ACT.Silu).then_inc(silu_ready, 1)
                act.wait_ge(act_made, u + 1)
                if not (isinstance(n, int) and u < 4):
                    act.wait_ge(down_done, u - 3)
                nc.scalar.copy(ahi[0:r, b, :], acts[0:r, b % 2, :]).then_inc(act_hi, 1)
                if later(n, s, j, AHEAD):
                    cut_high(act, *later(n, s, j, AHEAD))

            over_units(act, step)

        @block.vector
        def _(dve):
            def link(ins):
                dve.wait_ge(g.dve_step.sem, g.dve_step.inc(ins))

            norm_dve(g, dve, k, link)
            dve.wait_ge(x_hi, 1)
            nc.vector.tensor_tensor(xlo[:, :, :], g.xnT[:, :, :], xhi[:, :, :].bitcast(F32), ALU.subtract).then_inc(x_lo, 1)
            for d in range(AHEAD - 1):
                cut_rest(dve, *later(0, 0, 0, d))
            G = gates

            def gate():
                dve.wait_ge(z_ready, 1)
                if choose == "softmax":
                    link(nc.vector.tensor_copy(G.z[:, :, :], bank[:, 6, 0:TA * E].rearrange("p (a e) -> p a e", a=TA)))
                    link(nc.vector.tensor_reduce(G.one[:, :, :], G.z[:, :, :], AX.X, ALU.max))
                    nc.vector.tensor_tensor(G.t[:, :, :], G.z[:, :, :], G.one[:, :, :].to_broadcast([P, TA, E]),
                                            ALU.subtract).then_inc(gate_in, 1)
                    dve.wait_ge(gate_exp, 1)
                    link(nc.vector.tensor_reduce(G.one[:, :, :], G.s[:, :, :], AX.X, ALU.add))
                    link(nc.vector.reciprocal(G.one[:, :, :], G.one[:, :, :]))
                    link(nc.vector.tensor_tensor(G.s[:, :, :], G.s[:, :, :], G.one[:, :, :].to_broadcast([P, TA, E]), ALU.mult))
                else:
                    dve.wait_ge(gate_exp, 1)
                    link(nc.vector.tensor_copy(G.z[:, :, :], bank[:, 6, 0:TA * E].rearrange("p (a e) -> p a e", a=TA)))
                    link(nc.vector.tensor_scalar(G.s[:, :, :], G.s[:, :, :], 1.0, None, ALU.add))
                    link(nc.vector.reciprocal(G.s[:, :, :], G.s[:, :, :]))

                def keep_top(out, val, n, top):
                    gt, eq, pre = G.gt[:, :, 0:n], G.eq[:, :, 0:n], G.pre[:, :, 0:n]
                    for a in range(TA):
                        link(nc.vector.max(G.m8[:, a, :], val[:, a, :]))
                    least = G.m8[:, :, top - 1:top].to_broadcast([P, TA, n])
                    nc.vector.tensor_tensor(gt, val[:, :, :], least, ALU.is_gt)
                    link(nc.vector.tensor_tensor(eq, val[:, :, :], least, ALU.is_equal))
                    link(nc.vector.tensor_reduce(G.one[:, :, :], gt, AX.X, ALU.add))
                    for a in range(TA):
                        link(nc.vector.tensor_tensor_scan(G.pre[:, a, 0:n], g.ones[:, 0:n], G.eq[:, a, 0:n], 0.0, ALU.mult, ALU.add))
                    link(nc.vector.tensor_tensor(pre, pre, G.one[:, :, :].to_broadcast([P, TA, n]), ALU.add))
                    link(nc.vector.tensor_scalar(pre, pre, top + 0.5, None, ALU.is_lt))
                    link(nc.vector.tensor_tensor(pre, pre, eq, ALU.mult))
                    link(nc.vector.tensor_tensor(out, pre, gt, ALU.add))

                if choose == "softmax":
                    keep_top(G.r[:, :, :], G.z, E, 2)
                    nc.vector.tensor_tensor(G.c[:, :, :], G.s[:, :, :], G.r[:, :, :], ALU.mult).then_inc(c_ready, 1)
                else:
                    link(nc.vector.tensor_reduce(G.g8[:, :, :], G.z[:, :, :].rearrange("p a (g e) -> p a g e", g=8), AX.X, ALU.max))
                    keep_top(G.m[:, :, :], G.g8, 8, 4)
                    z4 = G.z[:, :, :].rearrange("p a (g e) -> p a g e", g=8)
                    link(nc.vector.tensor_scalar(G.g8[:, :, :], G.m[:, :, :], 1.0, 1e30, ALU.subtract, ALU.mult))
                    for op, row in ((ALU.mult, G.m), (ALU.add, G.g8)):
                        for a in range(TA):
                            link(nc.vector.tensor_tensor(z4[:, a], z4[:, a], row[:, a, :].unsqueeze(2).to_broadcast([P, 8, 4]), op))
                    keep_top(G.r[:, :, :], G.z, E, 6)
                    link(nc.vector.tensor_tensor(G.c[:, :, :], G.s[:, :, :], G.r[:, :, :], ALU.mult))
                    link(nc.vector.tensor_reduce(G.one[:, :, :], G.c[:, :, :], AX.X, ALU.add))
                    link(nc.vector.reciprocal(G.one[:, :, :], G.one[:, :, :]))
                    link(nc.vector.tensor_tensor(G.c[:, :, :], G.c[:, :, :], G.one[:, :, :].to_broadcast([P, TA, E]), ALU.mult))
                    nc.vector.tensor_scalar(G.c[:, :, :], G.c[:, :, :], 2.5, None, ALU.mult).then_inc(c_ready, 1)

            gate()

            def step(n, s, j):
                b, u, r = place(s, j), n * U + j, rows[j]
                shared = isinstance(n, int) and n < 2
                dve.wait_ge(silu_ready, u + 1)
                if not shared:
                    c = cb[0:r, bass.ds(n - 2, 1), :].rearrange("p e t -> p (e t)")
                    nc.vector.tensor_tensor(silu[0:r, b, :], silu[0:r, b, :], c, ALU.mult).then_inc(weighted, 1)
                    dve.wait_ge(weighted, u - (2 * U - 1))
                if not (isinstance(n, int) and u < 2):
                    dve.wait_ge(act_hi, u - 1)
                nc.vector.tensor_tensor(acts[0:r, b % 2, :], silu[0:r, b, :], bank[0:r, b, T:2 * T], ALU.mult).then_inc(act_made, 1)
                if later(n, s, j, AHEAD - 1):
                    cut_rest(dve, *later(n, s, j, AHEAD - 1))
                dve.wait_ge(act_hi, u + 1)
                if not (isinstance(n, int) and u < 4):
                    dve.wait_ge(down_done, u - 3)
                nc.vector.tensor_tensor(alo[0:r, b, :], acts[0:r, b % 2, :], ahi[0:r, b, :].bitcast(F32),
                                        ALU.subtract).then_inc(act_ready, 1)
                if isinstance(n, int) and n == 1 and j == U - 1:
                    dve.wait_ge(c_turned, 1)
                    nc.vector.tensor_copy(cT[:, :], bank[0:E, 7, 0:T]).then_inc(c_copied, 1)
                    dve.wait_ge(c_first, 16)
                if isinstance(n, int) and n == 5 and j == U - 1:
                    dve.wait_ge(c_spread, 16)

            over_units(dve, step)
            dve.wait_ge(down_done, U * N)
            for a in range(TA):
                link(nc.vector.tensor_tensor(X[:, a, :], X[:, a, :], bank[:, 4 + a, :], ALU.add))


def cross_attention_1(g, k, ctxT, ctxT_loaded, ctx_chunks, mask, first_loads, later_loads):
    nc, sem, bank, X = g.nc, g.sem, g.bank, g.X
    at = g.area.at
    M = S2
    MC = M // 512
    MT = M // P
    pr = at(0, "pr", [P, TA, M])
    mb = at(32, "mb", [P, M])
    mask8 = at(48, "mask8", [P, M], mybir.dt.uint8)
    pT = at(52, "pT", [P, 4, 2, T])
    nat = [at(124 + 8 * c, f"nat{c}", [P, 4, D]) for c in range(6)]
    nat += [ctxT[0], ctxT[1]]
    pmx = at(172, "pmx", [P, TA, MC])
    nmx = at(172.25, "nmx", [P, TA])
    den = at(172.5, "cden", [P, TA])
    okay = at(172.75, "okay", [P, 1])
    SC = float(D) ** -0.5
    mask_loaded = sem("mask_loaded")
    nat_loaded = [sem(f"nat_loaded{c}") for c in range(MC)]
    s_ready = sem("x1_s_ready")
    s_masked = sem("x1_s_masked")
    maxed = sem("x1_maxed")
    exp_done = sem("x1_exp_done")
    p_turned = sem("x1_p_turned")
    pt_copied = [sem("x1_pt_copied0"), sem("x1_pt_copied1")]
    pv_done = sem("x1_pv_done")

    with nc.Block() as block:

        @block.sync
        def _(sp):
            sp.dma_start(mask8[:, :], mask.partition_broadcast(P)).then_inc(mask_loaded, 16)
            first_loads(sp)
            for c in range(MC):
                if c >= 6:
                    sp.wait_ge(s_ready, MC + c - 6 + 1)
                sp.dma_start(nat[c][:, :, :], ctx_chunks[c]).then_inc(nat_loaded[c], 16)
            sp.wait_ge(s_ready, 2 * MC)
            later_loads(sp)

        @block.tensor
        def _(pe):
            norm_turn_pe(g, pe, k)
            pe.wait_ge(g.xnT_ready, TA * k)
            for a in range(TA):
                for c in range(MC):
                    i = a * MC + c
                    if a == 0:
                        pe.wait_ge(ctxT_loaded[c], 16)
                    if i >= 4:
                        pe.wait_ge(s_masked, i - 3)
                    for d in range(DC):
                        ins = nc.tensor.matmul(bank[:, i % 4, :], g.xnT[:, d, a * P:a * P + P], ctxT[c][:, d, :],
                                               start=d == 0, stop=d == DC - 1)
                    ins.then_inc(s_ready, 1)

            def turn(i):
                if i >= 2:
                    pe.wait_ge(pt_copied[i % 2], i // 2)
                for t in range(2):
                    for a in range(TA):
                        ins = nc.tensor.transpose(bank[:, 4 + i % 2, t * T + a * P:t * T + a * P + P],
                                                  pr[:, a, (2 * i + t) * P:(2 * i + t + 1) * P], g.ident[:, :])
                ins.then_inc(p_turned, 1)

            def read(i):
                pe.wait_ge(pt_copied[i % 2], i // 2 + 1)
                if i % 2 == 0:
                    pe.wait_ge(nat_loaded[i // 2], 16)
                for t in range(2):
                    m = 2 * i + t
                    for a in range(TA):
                        ins = nc.tensor.matmul(bank[:, 6 + a, :], pT[:, i % 4, t, a * P:a * P + P], nat[m // 4][:, m % 4, :],
                                               start=m == 0, stop=m == MT - 1)
                ins.then_inc(pv_done, 1)

            pe.wait_ge(exp_done, TA)
            for i in range(MT // 2 + 1):
                if i < MT // 2:
                    turn(i)
                if i >= 1:
                    read(i - 1)

        @block.vector
        def _(dve):
            def link(ins):
                dve.wait_ge(g.dve_step.sem, g.dve_step.inc(ins))

            norm_dve(g, dve, k, link)
            dve.wait_ge(mask_loaded, 16)
            link(nc.vector.tensor_scalar(mb[:, :], mask8[:, :], 1.0, 1e30, ALU.subtract, ALU.mult))
            link(nc.vector.tensor_reduce(okay[:, :], mb[:, :], AX.X, ALU.max))
            link(nc.vector.tensor_scalar(okay[:, :], okay[:, :], -1.0, None, ALU.is_ge))
            for a in range(TA):
                for c in range(MC):
                    i = a * MC + c
                    dve.wait_ge(s_ready, i + 1)
                    nc.vector.tensor_tensor(pr[:, a, c * 512:c * 512 + 512], bank[:, i % 4, :], mb[:, c * 512:c * 512 + 512],
                                            ALU.add).then_inc(s_masked, 1)
                    dve.wait_ge(s_masked, i + 1)
                    n = nc.vector.tensor_reduce(pmx[:, a, c:c + 1], pr[:, a, c * 512:c * 512 + 512], AX.X, ALU.max)
                    if c == MC - 1:
                        link(n)
                link(nc.vector.tensor_reduce(nmx[:, a:a + 1], pmx[:, a, :], AX.X, ALU.max))
                nc.vector.tensor_scalar(nmx[:, a:a + 1], nmx[:, a:a + 1], -SC, None, ALU.mult).then_inc(maxed, 1)
            for i in range(1, MT // 2, 2):
                dve.wait_ge(p_turned, i + 1)
                if i >= 4:
                    dve.wait_ge(pv_done, i - 3)
                nc.vector.tensor_copy(pT[:, i % 4].rearrange("p t n -> p (t n)"), bank[:, 4 + i % 2, :]).then_inc(pt_copied[1], 1)
            link(nc.vector.reciprocal(den[:, :], den[:, :]))
            link(nc.vector.tensor_scalar(den[:, :], den[:, :], okay[:, 0:1], None, ALU.mult))
            dve.wait_ge(pv_done, MT // 2)
            for a in range(TA):
                link(nc.vector.scalar_tensor_tensor(out=X[:, a, :], in0=bank[:, 6 + a, :], scalar=den[:, a:a + 1],
                                                    in1=X[:, a, :], op0=ALU.mult, op1=ALU.add))

        @block.scalar
        def _(act):
            norm_act(g, act, k)
            norm_turn_act(g, act, k)
            for a in range(TA):
                act.wait_ge(maxed, a + 1)
                nc.scalar.activation(pr[:, a, :], pr[:, a, :], ACT.Exp, scale=SC, bias=nmx[:, a:a + 1],
                                     accum_out=den[:, a:a + 1]).then_inc(exp_done, 1)
            for i in range(0, MT // 2, 2):
                act.wait_ge(p_turned, i + 1)
                if i >= 4:
                    act.wait_ge(pv_done, i - 3)
                nc.scalar.copy(pT[:, i % 4].rearrange("p t n -> p (t n)"), bank[:, 4 + i % 2, :]).then_inc(pt_copied[0], 1)


H0, K0 = 16, 32
H1, K1, KV1 = 32, 64, 8
E0, I0 = 32, 256
E1, I1 = 8, 352
BIAS = 512 + 512 + 2048 + D


def perceiver(nc, ins, out):
    with ExitStack() as ctx:
        g = setup(nc, ctx)
        sem, at = g.sem, g.area.at

        def sb(name, shape, dt=F32):
            return ctx.enter_context(nc.sbuf_tensor(name, shape, dt))

        g.causal = sb("causal_mask", [P, 3 * P])
        g.ones = sb("ones_row", [P, E0])
        table0 = sb("rope0", [P, 2, TA, 2, K0])
        table1 = sb("rope1", [P, 2, TA, 2, K1])
        gate0 = sb("gate0_w", [P, DC, E0])
        gate1 = sb("gate1_w", [P, DC, E1])
        kw1 = sb("kw1_row", [P, H1])
        small_loaded = sem("small_loaded")
        w_attn0 = at(0, "w_attn0_sb", [P, 4, DC, D])
        w_attn0_loaded = sem("w_attn0_loaded")
        raw0 = [at(kib, f"raw0_{s}", [P, I0 // P, 2 * DC * P + D]) for s, kib in enumerate((156, 168))]
        raw0_loaded = [sem(f"raw0_loaded{s}") for s in range(2)]
        cb0 = at(0, "cb0", [P, E0, T])
        ctxT = [at(60 + 8 * c, f"ctxT{c}", [P, DC, 512]) for c in range(8)]
        ctxT_loaded = [sem(f"ctxT_loaded{c}") for c in range(8)]
        wq1 = at(76, "wq1_sb", [P, DC, 2048])
        wk1 = at(108, "wk1_sb", [P, DC, 512])
        wv1 = at(116, "wv1_sb", [P, DC, 512])
        wo1 = at(130, "wo1_sb", [P, 16, D])
        qkv1_loaded = sem("qkv1_loaded")
        wo1_loaded = sem("wo1_loaded")
        bias1_loaded = sem("bias1_loaded")
        bias1 = at(61, "bias1_row", [P, BIAS])
        raw1 = [at(kib, f"raw1_{s}", [P, -(-I1 // P), 2 * DC * P + D]) for s, kib in enumerate((162, 76))]
        raw1_loaded = [sem(f"raw1_loaded{s}") for s in range(2)]
        cb1 = at(0, "cb1", [P, E1, T])

        def loads_a(sp):
            for dst, src in ((g.causal[:, :], ins["causal"]), (g.ones[:, :], ins["ones"].partition_broadcast(P)),
                             (table0[:, :, :, :, :], ins["table0"]), (table1[:, :, :, :, :], ins["table1"]), (gate0[:, :, :], ins["gate0"]),
                             (gate1[:, :, :], ins["gate1"]), (kw1[:, :], ins["kw1"].partition_broadcast(P))):
                sp.dma_start(dst, src).then_inc(small_loaded, 16)
            sp.dma_start(w_attn0[:, :, :, :], ins["w_attn0"]).then_inc(w_attn0_loaded, 16)

        def loads_b(sp):
            for n in range(2):
                sp.dma_start(raw0[n][:, :, :].rearrange("p u w -> p (u w)"), ins["wall0"][n]).then_inc(raw0_loaded[n], 16)

        def first_d(sp):
            for c in range(8):
                sp.dma_start(ctxT[c][:, :, :], ins["ctxT"][c]).then_inc(ctxT_loaded[c], 16)

        def loads_d(sp):
            sp.dma_start(wk1[:, :, :], ins["wk1"]).then_inc(qkv1_loaded, 16)
            sp.dma_start(wv1[:, :, :], ins["wv1"]).then_inc(qkv1_loaded, 16)
            sp.dma_start(wq1[:, :, :], ins["wq1"]).then_inc(qkv1_loaded, 16)

        def load_raw1(sp, n):
            sp.dma_start(raw1[n][:, :, :].rearrange("p u w -> p (u w)"), ins["wall1"][n]).then_inc(raw1_loaded[n], 16)

        def loads_e(sp):
            sp.dma_start(bias1[:, :], ins["bias1"].partition_broadcast(P)).then_inc(bias1_loaded, 16)
            sp.dma_start(wo1[:, :, :], ins["wo1"]).then_inc(wo1_loaded, 16)
            load_raw1(sp, 0)

        def later_e(sp):
            load_raw1(sp, 1)

        smalls = (small_loaded, 16 * 7)
        cross_attention_0(g, ins["x"], ins["ctx_rows"], ins["ctx_vt"], loads_a)
        self_attention(g, 1, "a0", H0, K0, 4, lambda n: n // 4, lambda n: K0 * n, True,
                   {"q": w_attn0[:, 0], "k": w_attn0[:, 1], "v": w_attn0[:, 2], "o": w_attn0[:, 3]},
                   {"q": table0[:, 0], "k": table0[:, 1]}, None, None, lambda kib, n, s: at(32 + kib, n, s),
                   [smalls, (w_attn0_loaded, 16)], loads_b, None)
        experts(g, 2, "e0", E0, I0, "sigmoid", gate0, [smalls], raw0, raw0_loaded, ins["wall0"], cb0, 32,
                (57, 69, 81, 93), (105, 117, 129, 141), 4, lambda sp: None, None)
        cross_attention_1(g, 3, ctxT, ctxT_loaded, ins["ctx_chunks"], ins["mask"], first_d, loads_d)
        b = bias1[:, :]
        self_attention(g, 4, "a1", H1, K1, 16, lambda n: n // 8, lambda n: K1 * (2 * (n // 8) + n % 2), False,
                   {"q": wq1, "k": wk1, "v": wv1, "o": wo1}, {"q": table1[:, 0], "k": table1[:, 1]}, kw1,
                   {"k": b[:, 0:512], "v": b[:, 512:1024], "q": b[:, 1024:3072], "o": b[:, 3072:]},
                   lambda kib, n, s: at(kib, n, s), [smalls, (bias1_loaded, 16), (qkv1_loaded, 48), (wo1_loaded, 16)], loads_e, later_e)
        experts(g, 5, "e1", E1, I1, "softmax", gate1, [smalls], raw1, raw1_loaded, ins["wall1"], cb1, 8,
                (33, 51), (94, 112), 3, lambda sp: None, None)
        out_stored = sem("out_stored")
        with nc.Block() as block:
            @block.sync
            def _(sp):
                sp.dma_start(out.rearrange("(a p) d -> p a d", p=P), g.X[:, :, :]).then_inc(out_stored, 16)
                sp.wait_ge(out_stored, 16)


def kernel(**inputs):
    import numpy as np
    import concourse.bacc as bacc
    from concourse.bass_utils import run_bass_kernel_spmd

    nc = bacc.Bacc("TRN2", target_bir_lowering=False, num_devices=1)
    c = np.ascontiguousarray
    v = {n: c(a) for n, a in inputs.items()}

    def inner_first(wT, n):
        s = wT.shape
        return c(np.moveaxis(wT.reshape(s[:-2] + (n, P, s[-1])), -3, -2))

    def rope(dim, base, repeat, scale):
        f32 = np.float32
        i = np.arange(dim // 2)
        inv = (base ** (-2.0 * i / dim)).astype(f32) if repeat else (1.0 / (base ** (2.0 * i / dim)).astype(f32)).astype(f32)
        ang = (np.arange(T, dtype=f32)[:, None] * inv[None, :]).astype(np.float64)
        cos, sin = np.cos(ang), np.sin(ang)
        if repeat:
            cs, sn = np.repeat(cos, 2, axis=-1), np.stack([-sin, sin], axis=-1).reshape(T, dim)
        else:
            cs, sn = np.concatenate([cos, cos], -1), np.concatenate([-sin, sin], -1)
        t = np.stack([cs, sn], 1)
        t = np.stack([t * scale, t], 0).astype(f32)
        return c(t.reshape(2, TA, P, 2, dim).transpose(2, 0, 1, 3, 4))

    def all_experts(gate, up, down, width):
        n, U = gate.shape[0], -(-width // P)
        out = np.zeros((n, P, U, 2 * DC * P + D), down.dtype)
        for m, w in enumerate((gate, up)):
            wide = np.zeros((n, D, U * P), w.dtype)
            wide[:, :, :width] = w
            out[..., m * DC * P:(m + 1) * DC * P] = wide.reshape(n, DC, P, U, P).transpose(0, 2, 3, 1, 4).reshape(n, P, U, DC * P)
        deep = np.zeros((n, U * P, D), down.dtype)
        deep[:, :width] = down
        out[..., 2 * DC * P:] = deep.reshape(n, U, P, D).transpose(0, 2, 1, 3)
        return c(out.reshape(n, P, -1))

    halves = lambda w: w.reshape(D, 2, -1).transpose(1, 0, 2)
    order = [4 * (2 * p + r) + m for p in range(KV1 // 2) for m in range(4) for r in range(2)]
    ctx = v["ctx_2048"]
    tri = np.where(np.tril(np.ones((P, P), bool)), np.float32(0), np.float32(-1e30)).astype(np.float32)
    Wq = v["L1_attn_Wq"].reshape(H1, K1, D)[order].reshape(H1 * K1, D)
    Wo = v["L1_attn_Wo"].reshape(D, H1, K1)[:, order].reshape(D, H1 * K1)
    arrays = {
        "x": v["x"].reshape(T, D),
        "ctx_rows": ctx.reshape(XH, P, 1024),
        "ctx_vt": c(ctx.reshape(XH, XC, XT, P).transpose(0, 3, 2, 1)),
        "ctxT": c(ctx.reshape(8, 512, DC, P).transpose(0, 3, 2, 1)),
        "ctx_chunks": c(ctx.reshape(8, 4, P, D).transpose(0, 2, 1, 3)),
        "mask": v["mask_BxS2_bk0"].reshape(S2),
        "causal": np.concatenate([tri, np.zeros((P, P), np.float32), tri], axis=1),
        "ones": np.ones(E0, np.float32),
        "table0": rope(K0, 10000.0, True, float(K0) ** -0.5),
        "table1": rope(K1, 10000.0, False, float(K1) ** -0.5),
        "gate0": inner_first(v["L0_ffn_gate_w"].T, DC),
        "gate1": inner_first(v["L1_ffn_gate_w"], DC),
        "kw1": c(v["L1_attn_key_weights"][order]),
        "bias1": c(np.concatenate([v["L1_attn_bk"], v["L1_attn_bv"], v["L1_attn_bq"].reshape(H1, K1)[order].reshape(-1),
                                   v["L1_attn_bo"]])),
        "w_attn0": c(np.stack([inner_first(v["L0_attn_" + n].T, DC) for n in ("wq", "wk", "wv", "wo")], axis=1)),
        "wk1": inner_first(v["L1_attn_Wk"].T, DC),
        "wv1": inner_first(v["L1_attn_Wv"].T, DC),
        "wq1": inner_first(Wq.T, DC),
        "wo1": inner_first(Wo.T, 16),
        "wall0": all_experts(np.concatenate([halves(v["L0_ffn_sw1"].T), v["L0_ffn_w11"].transpose(0, 2, 1)]),
                             np.concatenate([halves(v["L0_ffn_sw3"].T), v["L0_ffn_w33"].transpose(0, 2, 1)]),
                             np.concatenate([v["L0_ffn_sw2"].T.reshape(2, I0, D), v["L0_ffn_w22"].transpose(0, 2, 1)]), I0),
        "wall1": all_experts(np.concatenate([halves(v["L1_ffn_sw_gate"]), v["L1_ffn_w_gate"]]),
                             np.concatenate([halves(v["L1_ffn_sw_up"]), v["L1_ffn_w_up"]]),
                             np.concatenate([v["L1_ffn_sw_down"].reshape(2, I1, D), v["L1_ffn_w_down"]]), I1),
    }
    ins = {n: nc.dram_tensor(n, a.shape, mybir.dt.from_np(a.dtype), kind="ExternalInput").ap() for n, a in arrays.items()}
    out = nc.dram_tensor("out", (T, D), F32, kind="ExternalOutput").ap()
    perceiver(nc, ins, out)
    r = run_bass_kernel_spmd(nc, [arrays], core_ids=[0])
    return r.results[0]["out"].reshape(1, T, D)
```

```python
from contextlib import ExitStack

import concourse.bass as bass
from concourse import mybir

F32 = mybir.dt.float32
BF16 = mybir.dt.bfloat16
F32R = mybir.dt.float32r
ALU = mybir.AluOpType
ACT = mybir.ActivationFunctionType
AX = mybir.AxisListType

P = 128
T = 256
TA = T // P
D = 512
DC = D // P
S2 = 4096
EPS = 1e-5
HIGHEST = 3.4e38
SR = 3

XH = 16
XC = T // XH
XS = S2 * D // T
XT = XS // P
XHA = P // XC
XSCALE = 0.25
TERMS = [0, 1, 0, 1, 2, 0]
QTERMS = [0, 0, 1, 1, 0, 2]
KR = 6 * XC
PVS = 3
LAG = 8
XG = XT // 4
PR = 8
TURN = [n if n < XT - 4 else n + 1 for n in range(XT)]
MAX_TURN = XT - 4
S_BANKS = [4, 5, 7]


class Count:

    def __init__(self, sem):
        self.sem, self.n = sem, 0

    def inc(self, ins, by=1):
        ins.then_inc(self.sem, by)
        self.n += by
        return self.n




def size(dt):
    return 2 if dt == BF16 else 1 if dt == mybir.dt.uint8 else 4


class Area:

    def __init__(self, nc, lo, hi):
        self.nc, self.base, self.hi = nc, lo, hi

    def at(self, kib, name, shape, dt=F32):
        n = size(dt)
        for d in shape[1:]:
            n *= d
        assert self.base + kib * 1024 + n <= self.hi, (name, kib, n)
        self.end = kib + n / 1024
        return self.nc.alloc_sbuf_tensor_at(name, shape, dt, offset=self.base + int(kib * 1024))


class Shared:
    pass


class Gates:
    pass


def setup(nc, ctx):
    g = Shared()
    g.nc = nc

    def sb(name, shape, dt=F32):
        return ctx.enter_context(nc.sbuf_tensor(name, shape, dt))

    def sem(name):
        return ctx.enter_context(nc.semaphore(name))

    g.sem = sem
    g.bank = ctx.enter_context(nc.psum_tensor("bank", [P, 8, 512], F32))
    g.ident = sb("ident", [P, P])
    g.identb = sb("identb", [P, P], BF16)
    g.X = sb("X", [P, TA, D])
    g.xn = sb("xn", [P, TA, D])
    g.xnT = sb("xnT", [P, DC, T])
    g.stats = sb("stats", [P, TA, 6])
    g.mv = sb("mv", [P, TA, 2])
    g.rstd = sb("rstd", [P, TA, 1])
    g.var = sb("var", [P, TA, 1])
    g.std = sb("std", [P, TA, 1])
    g.small = sb("head_sums", [P, 4, 2])
    g.rden = sb("head_rden", [P, 2, 2])
    g.warm = sb("warm", [P, 1])
    g.arena_size = 184 * 1024
    slab = ctx.enter_context(nc.sbuf_tensor("slab", [P, g.arena_size // 4], F32))
    g.slab = slab
    base = nc.sbuf_base - g.arena_size
    g.area = Area(nc, base, base + g.arena_size)
    g.ident_ready = sem("ident_ready")
    g.dve_step = Count(sem("dve_step"))
    g.var_ready = sem("var_ready")
    g.std_ready = sem("std_ready")
    g.xn_ready = sem("xn_ready")
    g.xn_turned = sem("xn_turned")
    g.xnT_ready = sem("xnT_ready")
    g.stage = 0
    return g


def norm_dve(g, dve, k, link):
    nc = g.nc
    for a in range(TA):
        ins = nc.vector.bn_stats(g.stats[:, a, :], g.X[:, a, :])
    link(ins)
    for a in range(TA):
        ins = nc.vector.bn_aggr(g.mv[:, a, :], g.stats[:, a, :])
    link(ins)
    nc.vector.tensor_scalar(g.var[:, :, :], g.mv[:, :, 1:2], EPS, None, ALU.add).then_inc(g.var_ready, 1)
    dve.wait_ge(g.std_ready, k + 1)
    link(nc.vector.reciprocal(g.rstd[:, :, :], g.std[:, :, :]))
    link(nc.vector.tensor_tensor(g.std[:, :, :], g.rstd[:, :, :], g.rstd[:, :, :], ALU.mult))
    link(nc.vector.scalar_tensor_tensor(out=g.std[:, :, :], in0=g.std[:, :, :], scalar=-0.5, in1=g.var[:, :, :],
                                        op0=ALU.mult, op1=ALU.mult))
    link(nc.vector.scalar_tensor_tensor(out=g.rstd[:, :, :], in0=g.std[:, :, :], scalar=1.5, in1=g.rstd[:, :, :],
                                        op0=ALU.add, op1=ALU.mult))
    for a in range(TA):
        nc.vector.tensor_scalar(g.xn[:, a, :], g.X[:, a, :], g.mv[:, a, 0:1], g.rstd[:, a, :],
                                ALU.subtract, ALU.mult).then_inc(g.xn_ready, 1)


def norm_act(g, act, k):
    act.wait_ge(g.ident_ready, 4)
    g.nc.scalar.activation(g.warm[:, :], g.ident[:, 0:1], ACT.Sqrt)
    act.wait_ge(g.var_ready, k + 1)
    g.nc.scalar.activation(g.std[:, :, :], g.var[:, :, :], ACT.Sqrt).then_inc(g.std_ready, 1)


def norm_turn_act(g, act, k):
    for a in range(TA):
        act.wait_ge(g.xn_turned, TA * (k - 1) + a + 1)
        g.nc.scalar.copy(g.xnT[:, :, a * P:a * P + P],
                         g.bank[:, 6 + a, :].rearrange("p (d t) -> p d t", d=DC)).then_inc(g.xnT_ready, 1)


def norm_turn_pe(g, pe, k):
    for a in range(TA):
        pe.wait_ge(g.xn_ready, TA * k + a + 1)
        for d in range(DC):
            ins = g.nc.tensor.transpose(g.bank[:, 6 + a, d * P:d * P + P], g.xn[:, a, d * P:d * P + P], g.ident[:, :])
        ins.then_inc(g.xn_turned, 1)


def cross_attention_0(g, x, ctx_rows, ctx_vt, first_loads):
    nc, sem, bank, ident, identb, X, xn = g.nc, g.sem, g.bank, g.ident, g.identb, g.X, g.xn
    dve_step = g.dve_step
    at = g.area.at
    kraw = at(32, "kraw", [P, 2, 1024])
    kres = at(40, "kres", [P, 1024])
    ksplit = at(44, "ksplit", [P, 3, 1024], BF16)
    kstack = at(50, "kstack", [P, 2, XS], BF16)
    qsplit = at(82, "qsplit", [P, 3, TA, D], BF16)
    qstack = at(88, "qstack", [P, XH, D], BF16)
    vraw = at(104, "vraw", [P, 2, XT, XC])
    vext = at(112, "vext", [P, 2, XT, 2 * XC])
    probs = at(128, "probs", [P, PR, 512])
    osb = at(144, "osb", [P, 2, D])
    nd = at(148, "nd", [P, TA, 4, 2, D])
    pm = at(180, "pm", [P, 2, 4, 8])
    negmax = at(180.25, "negmax", [P, 2, 4])
    nres = at(180.5, "nres", [P, 4])
    nsplit = at(180.75, "nsplit", [P, 4, 3], BF16)
    kscratch = nc.dram_tensor("kscratch", [XH, 3, P, 1024], BF16, kind="Internal").ap()
    qscratch = nc.dram_tensor("qscratch", [3, T, D], BF16, kind="Internal").ap()
    oscratch = nc.dram_tensor("oscratch", [XH, P, D], F32, kind="Internal").ap()
    x_loaded = sem("x_loaded")
    kraw_loaded = [sem("kraw_loaded0"), sem("kraw_loaded1")]
    vraw_loaded = [sem("vraw_loaded0"), sem("vraw_loaded1")]
    split_step = sem("split_step")
    split_stored = sem("split_stored")
    stack_lo = [sem("stack_lo0"), sem("stack_lo1")]
    stack_hi = [sem("stack_hi0"), sem("stack_hi1")]
    const_ready = sem("const_ready")
    v_ready = sem("v_ready")
    qsplit_ready = sem("qsplit_ready")
    qsplit_stored = [sem(f"qsplit_stored{part}") for part in range(3)]
    q_stacked = sem("q_stacked")
    pre_scores = sem("pre_scores")
    pre_reduced = sem("pre_reduced")
    negmax_ready = sem("negmax_ready")
    nsplit_step = sem("nsplit_step")
    negmax_turned = sem("negmax_turned")
    negmax_stacked = sem("negmax_stacked")
    scores = sem("scores")
    probs_ready = sem("probs_ready")
    pv_done = sem("pv_done")
    o_copied = sem("o_copied")
    o_stored = [sem("o_stored0"), sem("o_stored1")]
    nd_loaded = [sem("nd_loaded0"), sem("nd_loaded1")]
    x_final = sem("x_final")

    def s_bank(n):
        return S_BANKS[TURN[n] % 3]

    with nc.Block() as block:

        def over_heads(eng, phase):
            phase(0, 0, True, False)
            phase(1, 1, False, False)
            with eng.Fori(1, XH // 2 - 1) as i:
                phase(i * 2, 0, False, False)
                phase(i * 2 + 1, 1, False, False)
            phase(XH - 2, 0, False, False)
            phase(XH - 1, 1, False, True)

        @block.sync
        def _(sp):
            def load_raw(h, b):
                sp.dma_start(kraw[:, b, :], ctx_rows[bass.ds(h, 1)].rearrange("h p n -> (h p) n")).then_inc(kraw_loaded[b], 16)

            def load_v(h, b):
                sp.dma_start(vraw[:, b], ctx_vt[bass.ds(h, 1)].rearrange("h p t c -> (h p) t c")).then_inc(vraw_loaded[b], 16)

            def store_split(h):
                sp.wait_ge(split_step, 4 * h + 4)
                sp.dma_start(kscratch[bass.ds(h, 1)].rearrange("h k p n -> (h p) k n") if isinstance(h, int) else
                             kscratch[bass.ds(h, 1)].rearrange("h k p n -> p (h k) n"), ksplit[:, :, :]).then_inc(split_stored, 16)

            def load_stack(h, b, half, reused):
                if half == 0:
                    sp.wait_ge(split_stored, 16 * h + 16)
                if reused:
                    sp.wait_ge(scores, XT * (h - 2) + XT // 2 * (half + 1))
                lo = half * XS // 2
                for j, part in enumerate(TERMS):
                    src = kscratch[bass.ds(h, 1), part].rearrange("h (c s) n -> (h c) (s n)", c=XC)
                    sp.dma_start(kstack[XC * j:XC * j + XC, b, lo:lo + XS // 2],
                                 src[:, lo:lo + XS // 2]).then_inc([stack_lo, stack_hi][half][b], 16)

            load_raw(0, 0)
            sp.dma_start(X[:, :, :], x.rearrange("(a p) d -> p a d", p=P)).then_inc(x_loaded, 16)
            load_raw(1, 1)
            load_v(0, 0)
            load_v(1, 1)
            store_split(0)
            load_stack(0, 0, 0, False)
            for part in range(3):
                sp.wait_ge(qsplit_ready, part + 1)
                sp.dma_start(qscratch[part].rearrange("(a p) t -> p a t", p=P), qsplit[:, part]).then_inc(qsplit_stored[part], 16)
            for part in range(3):
                sp.wait_ge(qsplit_stored[part], 16)
                for j in range(6):
                    if QTERMS[j] == part:
                        sp.dma_start(qstack[XC * j:XC * j + XC, :, :],
                                     qscratch[part].rearrange("(h c) t -> c h t", c=XC)).then_inc(q_stacked, 16)
            load_stack(0, 0, 1, False)
            first_loads(sp)

            def phase(h, b, first, last):
                if not last:
                    store_split(h + 1)
                    load_stack(h + 1, 1 - b, 0, not first)
                    load_stack(h + 1, 1 - b, 1, not first)
                if not first:
                    sp.wait_ge(o_copied, h)
                    sp.dma_start(oscratch[bass.ds(h - 1, 1)].rearrange("h p t -> (h p) t"), osb[:, 1 - b, :]).then_inc(o_stored[1 - b], 16)
                if not last and not (isinstance(h, int) and h == XH - 2):
                    sp.wait_ge(split_step, 4 * h + 4)
                    load_raw(h + 2, b)
                    sp.wait_ge(v_ready, h + 1)
                    load_v(h + 2, b)

            over_heads(sp, phase)

            def load_nd(h):
                r = XC * (h % XHA)
                sp.dma_start(nd[r:r + XC, h // XHA].rearrange("c g k t -> c (g k) t"),
                             oscratch[h].rearrange("(q c) t -> c q t", c=XC)).then_inc(nd_loaded[h // XHA], 16)

            sp.wait_ge(o_stored[0], 16 * XH // 2)
            sp.wait_ge(o_stored[1], 16 * (XH // 2 - 1))
            for h in range(XH - 1):
                load_nd(h)
            sp.wait_ge(o_copied, XH)
            sp.dma_start(oscratch[XH - 1], osb[:, 1, :]).then_inc(o_stored[1], 16)
            sp.wait_ge(o_stored[1], 16 * XH // 2)
            load_nd(XH - 1)

        @block.gpsimd
        def _(pool):
            nc.gpsimd.memset(ident[:, :], 0.0).then_inc(g.ident_ready, 1)
            nc.gpsimd.memset(identb[:, :], 0.0).then_inc(g.ident_ready, 1)
            pool.wait_ge(g.ident_ready, 2)
            for m in (ident, identb):
                nc.gpsimd.affine_select(out=m[:, :], in_=m[:, :], compare_op=ALU.not_equal, fill=1.0, base=0,
                                        pattern=[[-1, P]], channel_multiplier=1).then_inc(g.ident_ready, 1)

            def split(h, b):
                pool.wait_ge(kraw_loaded[b], (h - b) * 8 + 16)
                pool.wait_ge(split_stored, 16 * h)
                nc.gpsimd.tensor_copy(ksplit[:, 0, :], kraw[:, b, :]).then_inc(split_step, 1)
                pool.wait_ge(split_step, 4 * h + 1)
                nc.gpsimd.tensor_tensor(kres[:, :], kraw[:, b, :], ksplit[:, 0, :], ALU.subtract).then_inc(split_step, 1)
                pool.wait_ge(split_step, 4 * h + 2)
                nc.gpsimd.tensor_copy(ksplit[:, 1, :], kres[:, :]).then_inc(split_step, 1)
                pool.wait_ge(split_step, 4 * h + 3)
                nc.gpsimd.tensor_tensor(ksplit[:, 2, :], kres[:, :], ksplit[:, 1, :], ALU.subtract).then_inc(split_step, 1)

            def values(h, b, reused):
                pool.wait_ge(vraw_loaded[b], (h - b) * 8 + 16)
                if reused:
                    pool.wait_ge(pv_done, XG * (h - 1))
                nc.gpsimd.tensor_copy(vext[:, b, :, 0:XC], vraw[:, b]).then_inc(v_ready, 1)

            split(1, 1)
            values(0, 0, False)
            nc.gpsimd.memset(vext[:, :, :, XC:], 1.0).then_inc(const_ready, 1)
            pool.wait_ge(const_ready, 1)
            nc.gpsimd.memset(kstack[96:99, :, :], 1.0).then_inc(const_ready, 1)
            pool.wait_ge(const_ready, 2)

            def phase(h, b, first, last):
                pool.wait_ge(negmax_ready, h + 1)
                if not first:
                    pool.wait_ge(negmax_turned, h)
                nc.gpsimd.tensor_copy(nsplit[:, :, 0], negmax[:, b, :]).then_inc(nsplit_step, 1)
                pool.wait_ge(nsplit_step, 4 * h + 1)
                nc.gpsimd.tensor_tensor(nres[:, :], negmax[:, b, :], nsplit[:, :, 0], ALU.subtract).then_inc(nsplit_step, 1)
                pool.wait_ge(nsplit_step, 4 * h + 2)
                nc.gpsimd.tensor_copy(nsplit[:, :, 1], nres[:, :]).then_inc(nsplit_step, 1)
                pool.wait_ge(nsplit_step, 4 * h + 3)
                nc.gpsimd.tensor_tensor(nsplit[:, :, 2], nres[:, :], nsplit[:, :, 1], ALU.subtract).then_inc(nsplit_step, 1)
                if not last:
                    values(h + 1, 1 - b, not first)
                if not last and not (isinstance(h, int) and h == XH - 2):
                    split(h + 2, b)

            for h in range(XH):
                phase(h, h % 2, h == 0, h == XH - 1)

        @block.vector
        def _(dve):
            def link(ins):
                dve.wait_ge(dve_step.sem, dve_step.inc(ins))

            dve.wait_ge(split_step, 1)
            nc.vector.tensor_tensor(kres[:, :], kraw[:, 0, :], ksplit[:, 0, :], ALU.subtract).then_inc(split_step, 1)
            dve.wait_ge(x_loaded, 16)
            norm_dve(g, dve, 0, link)
            dve.wait_ge(split_step, 3)
            nc.vector.tensor_tensor(ksplit[:, 2, :], kres[:, :], ksplit[:, 1, :], ALU.subtract).then_inc(split_step, 1)
            dve.wait_ge(g.xn_ready, TA)
            nc.vector.tensor_copy(qsplit[:, 0], xn[:, :, :]).then_inc(qsplit_ready, 1)
            dve.wait_ge(qsplit_ready, 1)
            link(nc.vector.tensor_tensor(xn[:, :, :], xn[:, :, :], qsplit[:, 0], ALU.subtract))
            nc.vector.tensor_copy(qsplit[:, 1], xn[:, :, :]).then_inc(qsplit_ready, 1)
            dve.wait_ge(qsplit_ready, 2)
            nc.vector.tensor_tensor(qsplit[:, 2], xn[:, :, :], qsplit[:, 1], ALU.subtract).then_inc(qsplit_ready, 1)

            def reduces(h, b, rs):
                for r in rs:
                    dve.wait_ge(pre_scores, 32 * h + r + 1)
                    nc.vector.tensor_reduce(pm[:, b, r % 4, r // 4:r // 4 + 1], bank[:, 2 * (r % 2):2 * (r % 2) + 2, :],
                                            AX.XY, ALU.max).then_inc(pre_reduced, 1)

            reduces(0, 0, range(32))

            def phase(h, b, first, last):
                dve.wait_ge(pre_reduced, 32 * h + 32)
                nc.vector.tensor_reduce(negmax[:, b, :], pm[:, b], AX.X, ALU.max, negate=True).then_inc(negmax_ready, 1)
                if not last:
                    reduces(h + 1, 1 - b, range(32))

            over_heads(dve, phase)
            for a in range(TA):
                dve.wait_ge(nd_loaded[a], 16 * XHA)
                for q in range(1, 4):
                    link(nc.vector.tensor_tensor(nd[:, a, 0], nd[:, a, 0], nd[:, a, q], ALU.add))
                link(nc.vector.reciprocal(nd[:, a, 1, 1, :], nd[:, a, 0, 1, :]))
                link(nc.vector.tensor_tensor(nd[:, a, 0, 0, :], nd[:, a, 0, 0, :], nd[:, a, 1, 1, :], ALU.mult))
                nc.vector.tensor_tensor(X[:, a, :], X[:, a, :], nd[:, a, 0, 0, :], ALU.add).then_inc(x_final, 1)
            dve.wait_ge(x_final, TA)

        @block.scalar
        def _(act):
            def exps(h, b, n, first):
                m = XT * b + n
                act.wait_ge(scores, XT * h + n + 1)
                if n % 4 == 0 and not (first and n < PR):
                    act.wait_ge(pv_done, XG * h + n // 4 + 1 - PR // 4)
                nc.scalar.activation(probs[:, m % PR, :], bank[:, s_bank(n), :], ACT.Exp, scale=XSCALE).then_inc(probs_ready, 1)

            def stack_negmax(h):
                act.wait_ge(negmax_turned, h + 1)
                nc.scalar.copy(qstack[96:99, bass.ds(h, 1), :], bank[96:99, S_BANKS[MAX_TURN % 3]:S_BANKS[MAX_TURN % 3] + 1, :]).then_inc(negmax_stacked, 1)

            def copy_o(h, b, first):
                act.wait_ge(pv_done, XG * h + XG)
                if not first:
                    act.wait_ge(o_stored[b], (h - b) * 8)
                nc.scalar.copy(osb[:, b, :], bank[:, 6, :]).then_inc(o_copied, 1)

            def phase(h, b, first, last):
                for n in range(XT):
                    if n == 0 and first:
                        stack_negmax(h)
                    exps(h, b, n, first)
                    if n == XT - 4 and not last:
                        stack_negmax(h + 1)
                    if n == 3 and not first:
                        copy_o(h - 1, 1 - b, isinstance(h, int) and h <= 2)

            act.wait_ge(kraw_loaded[0], 16)
            nc.scalar.copy(ksplit[:, 0, :], kraw[:, 0, :]).then_inc(split_step, 1)
            act.wait_ge(split_step, 2)
            nc.scalar.copy(ksplit[:, 1, :], kres[:, :]).then_inc(split_step, 1)
            norm_act(g, act, 0)
            over_heads(act, phase)
            copy_o(XH - 1, 1, False)

        @block.tensor
        def _(pe):
            def pre(h, b, n):
                r = n // 2
                c, tt = r // 4, r % 4
                if n % 2 == 0 and not (isinstance(h, int) and h == 0 and r < 2):
                    pe.wait_ge(pre_reduced, 32 * h + r - 1)
                if n == 0:
                    pe.wait_ge(stack_lo[b], (h - b) * 48 + 96)
                if n == 32:
                    pe.wait_ge(stack_hi[b], (h - b) * 48 + 96)
                k = c * 1024 + 512 * (n % 2)
                ins = nc.tensor.matmul(bank[:, 2 * (r % 2) + n % 2, :], qof(h, slice(0, KR))[:, tt * P:tt * P + P],
                                       kstack[0:KR, b, k:k + 512], start=True, stop=True)
                if n % 2:
                    ins.then_inc(pre_scores, 1)

            def qof(h, rows):
                if isinstance(h, int):
                    return qstack[rows, h, :]
                return qstack[rows, bass.ds(h, 1), :].rearrange("p h t -> p (h t)")

            def score(h, b, n, first):
                if n == 0:
                    pe.wait_ge(negmax_stacked, h + 1)
                if n == XT - 2:
                    if not (isinstance(h, int) and h == XH - 1):
                        pe.wait_ge(negmax_stacked, h + 2)
                elif n != 2 and not (first and n < 3):
                    back = 2 if n in (0, 1, XT - 4, XT - 3) else 3
                    pe.wait_ge(probs_ready, XT * h + n + 1 - back)
                nc.tensor.matmul(bank[:, s_bank(n), :], kstack[0:KR + 3, b, n * P:n * P + P], qof(h, slice(0, KR + 3)),
                                 start=True, stop=True).then_inc(scores, 1)

            def pv(h, b, q, first):
                pe.wait_ge(probs_ready, XT * h + 4 * q + 4)
                if q == 0:
                    pe.wait_ge(v_ready, h + 1)
                    if not first:
                        pe.wait_ge(o_copied, h)
                for e in range(4):
                    ins = nc.tensor.matmul(bank[32 * e:32 * e + 32, 6, :], vext[:, b, 4 * q + e, :],
                                           probs[:, (XT * b + 4 * q + e) % PR, :], start=q == 0, stop=q == XG - 1)
                ins.then_inc(pv_done, 1)

            pe.wait_ge(q_stacked, 96)
            for n in range(64):
                pre(0, 0, n)

            def main_step(h, b, s, first):
                if s >= LAG:
                    score(h, b, s - LAG, first)
                elif not first:
                    score(h - 1, 1 - b, XT + s - LAG, False)
                if s % 4 == PVS:
                    q = (s - LAG - PVS) // 4 - 1
                    if q >= 0:
                        pv(h, b, q, first)
                    elif not first:
                        pv(h - 1, 1 - b, XG + q, False)

            def phase(h, b, first, last):
                for s in range(XT):
                    if s == 4:
                        pe.wait_ge(nsplit_step, 4 * h + 4)
                        if not first:
                            pe.wait_ge(probs_ready, XT * (h - 1) + MAX_TURN - 2)
                        for tt in range(4):
                            ins = nc.tensor.matmul(bank[96:99, S_BANKS[MAX_TURN % 3], tt * P:tt * P + P], nsplit[:, tt, :], identb[:, :],
                                                   start=True, stop=True)
                        ins.then_inc(negmax_turned, 1)
                    if not last:
                        pre(h + 1, 1 - b, s)
                    main_step(h, b, s, first)

            pe.wait_ge(const_ready, 2)
            pe.wait_ge(g.ident_ready, 4)
            over_heads(pe, phase)
            for s in range(LAG):
                main_step(XH, 0, s, False)
            pv(XH - 1, 1, XG - 1, False)



def self_attention(g, k, name, heads, dk, q_tiles, kv_tile_of, v_col_of, pairs, w, wo_high, wo_rest, table, kw, bias, area_at,
                   loaded, wo_loaded, first_loads, later_loads):
    nc, sem, bank, X = g.nc, g.sem, g.bank, g.X
    per = P // dk
    NQ = q_tiles * P
    jobs = [("k", 0, a) for a in range(TA)] + [("v", 0, a) for a in range(TA)]
    jobs += [("q", c, a) for c in range(NQ // 512) for a in range(TA)]

    at = lambda kib, what, shape: area_at(kib, f"{name}_{what}", shape)
    qtok = at(0, "qtok", [P, TA, NQ])
    kib = TA * NQ * 4 / 1024
    ktok = at(kib, "ktok", [P, TA, 512])
    vtok = at(kib + 4, "vtok", [P, TA, 512])
    rot = at(kib + 8, "rot", [P, 3, 2, 512])
    qT = at(kib + 20, "qT", [P, q_tiles, T])
    kT = at(2 * kib + 20, "kT", [P, 4, T])
    soft = at(2 * kib + 24, "soft", [P, SR, 3 * P])
    turned_sb = rot[:, 0:2].rearrange("p a b n -> p (a b n)")[:, 0:2 * 3 * P].rearrange("p (r n) -> p r n", r=2)
    aohi = area_at(0, f"{name}_aohi", [P, q_tiles, T], F32R)
    aolo = area_at(kib + 20, f"{name}_aolo", [P, q_tiles, T], F32R)
    OC = q_tiles // 4
    small = g.small
    nmax = small[:, 0:2]
    denom = small[:, 2:4]
    rden = g.rden

    proj_done = sem(name + "_proj_done")
    rot_step = Count(sem(name + "_rot_step"))
    rotated = sem(name + "_rotated")
    v_copied = sem(name + "_v_copied")
    turned = sem(name + "_turned")
    turn_copied = sem(name + "_turn_copied")
    s_ready = sem(name + "_s_ready")
    maxed = sem(name + "_maxed")
    exp_done = sem(name + "_exp_done")
    inverted = sem(name + "_inverted")
    normed = sem(name + "_normed")
    p_turned = sem(name + "_p_turned")
    pt_copied = sem(name + "_pt_copied")
    pv_done = sem(name + "_pv_done")
    ao_hi = sem(name + "_ao_hi")
    ao_lo = sem(name + "_ao_lo")
    wo_hi = sem(name + "_wo_hi")
    wo_lo = sem(name + "_wo_lo")
    out_done = sem(name + "_out_done")

    rot_jobs = [j for j, (kind, c, a) in enumerate(jobs) if kind != "v"]
    v_jobs = [j for j, (kind, c, a) in enumerate(jobs) if kind == "v"]

    with nc.Block() as block:

        @block.sync
        def _(sp):
            first_loads(sp)
            if later_loads:
                sp.wait_ge(proj_done, len(jobs))
                later_loads(sp)

        @block.tensor
        def _(pe):
            norm_turn_pe(g, pe, k)
            pe.wait_ge(g.xnT_ready, TA * k)
            for s, n in loaded:
                pe.wait_ge(s, n)

            def project(j):
                kind, c, a = jobs[j]
                if j >= 4:
                    if jobs[j - 4][0] == "v":
                        pe.wait_ge(v_copied, v_jobs.index(j - 4) + 1)
                    else:
                        pe.wait_ge(rotated, rot_jobs.index(j - 4) + 1)
                for d in range(DC):
                    ins = nc.tensor.matmul(bank[:, j % 4, :], g.xnT[:, d, a * P:a * P + P],
                                           w[kind][:, d, 512 * c:512 * c + 512], start=d == 0, stop=d == DC - 1)
                ins.then_inc(proj_done, 1)

            def turn(r):
                kind, c, a = jobs[rot_jobs[r]]
                pe.wait_ge(rotated, r + 1)
                if r >= 2:
                    pe.wait_ge(turn_copied, r - 1)
                src = (ktok if kind == "k" else qtok)[:, a, 512 * c:512 * c + 512]
                for f in range(4):
                    ins = nc.tensor.transpose(bank[:, 4 + r % 2, f * P:f * P + P], src[:, f * P:f * P + P], g.ident[:, :])
                ins.then_inc(turned, 1)

            r = 0
            for j in range(len(jobs)):
                project(j)
                while r < len(rot_jobs) and rot_jobs[r] <= j - 2:
                    turn(r)
                    r += 1
            for r in range(r, len(rot_jobs)):
                turn(r)
            pe.wait_ge(turn_copied, len(rot_jobs))
            pe.wait_ge(v_copied, TA)

            def scores(n):
                if n >= 2:
                    pe.wait_ge(maxed, 2 * n - 2)
                b, r0, q, kt = bank[:, n % 2, :], dk * (n % per), n // per, kv_tile_of(n)
                nc.tensor.matmul(b[:, 0:P], qT[r0:r0 + dk, q, 0:P], kT[r0:r0 + dk, kt, 0:P], start=True, stop=True)
                nc.tensor.matmul(b[:, P:3 * P], qT[r0:r0 + dk, q, P:T], kT[r0:r0 + dk, kt, :],
                                 start=True, stop=True).then_inc(s_ready, 1)

            def turn_probs(n):
                pe.wait_ge(normed, n + 1)
                if n >= 2:
                    pe.wait_ge(pt_copied, n - 1)
                for f in range(3):
                    ins = nc.tensor.transpose(bank[:, 2 + n % 2, f * P:f * P + P], soft[:, n % SR, f * P:f * P + P], g.ident[:, :])
                ins.then_inc(p_turned, 1)

            def values(n):
                pe.wait_ge(pt_copied, n + 1)
                q, r0, v0 = n // per, dk * (n % per), v_col_of(n)
                if n % per == 0 and q >= 2:
                    pe.wait_ge(ao_lo, q - 1)
                b = bank[r0:r0 + dk, 4 + q % 2, :]
                nc.tensor.matmul(b[:, 0:T], vtok[:, 0, v0:v0 + dk], turned_sb[:, n % 2, 0:T], start=True, stop=False)
                nc.tensor.matmul(b[:, P:T], vtok[:, 1, v0:v0 + dk], turned_sb[:, n % 2, T:3 * P],
                                 start=False, stop=True).then_inc(pv_done, 1)

            for n in range(heads + SR):
                if n < heads:
                    scores(n)
                if 0 <= n - SR + 1 < heads:
                    turn_probs(n - SR + 1)
                if 0 <= n - SR < heads:
                    values(n - SR)
            pe.wait_ge(wo_lo, OC)
            for a in range(TA):
                for q in range(q_tiles):
                    if a == 0 and q in (0, q_tiles - 1):
                        pe.wait_ge(ao_lo, q_tiles if q else q_tiles - 1)
                    cols = slice(a * P, a * P + P)
                    for n, (l, r) in enumerate(((aohi, wo_high), (aolo, wo_high), (aohi, wo_rest))):
                        ins = nc.tensor.matmul(bank[:, 6 + a, :], l[:, q, cols], r[:, q, :],
                                               start=q == 0 and n == 0, stop=q == q_tiles - 1 and n == 2)
                ins.then_inc(out_done, 1)

        @block.vector
        def _(dve):
            def link(ins):
                dve.wait_ge(g.dve_step.sem, g.dve_step.inc(ins))

            norm_dve(g, dve, k, link)

            def rotate(r):
                kind, c, a = jobs[rot_jobs[r]]
                j = rot_jobs[r]
                dve.wait_ge(proj_done, j + 1)
                src = bank[:, j % 4, :]
                if bias is not None:
                    row = bias[kind][:, 512 * c:512 * c + 512]
                    dve.wait_ge(rot_step.sem, rot_step.inc(nc.vector.tensor_tensor(rot[:, 2, r % 2, :], src, row, ALU.add)))
                    src = rot[:, 2, r % 2, :]
                tab = table[kind]
                cos = tab[:, a, 0, :].unsqueeze(1).to_broadcast([P, 512 // dk, dk])
                fold = "p (h i two) -> p h i two" if pairs else "p (h two i) -> p h i two"
                tfold = "p (i two) -> p i two" if pairs else "p (two i) -> p i two"
                sin = tab[:, a, 1, :].rearrange(tfold, two=2)
                x4 = src.rearrange(fold, i=dk // 2, two=2)
                o4 = rot[:, 1, r % 2, :].rearrange(fold, i=dk // 2, two=2)
                rot_step.inc(nc.vector.tensor_tensor(rot[:, 0, r % 2, :].rearrange("p (h i) -> p h i", i=dk),
                                                     src.rearrange("p (h i) -> p h i", i=dk), cos, ALU.mult))
                for t in range(2):
                    s1 = sin[:, :, t].unsqueeze(1).to_broadcast([P, 512 // dk, dk // 2])
                    n = rot_step.inc(nc.vector.tensor_tensor(o4[:, :, :, t], x4[:, :, :, 1 - t], s1, ALU.mult))
                dve.wait_ge(rot_step.sem, n)
                dst = (ktok if kind == "k" else qtok)[:, a, 512 * c:512 * c + 512]
                if kind == "q" and kw is not None:
                    n = rot_step.inc(nc.vector.tensor_tensor(rot[:, 0, r % 2, :], rot[:, 0, r % 2, :], rot[:, 1, r % 2, :], ALU.add))
                    dve.wait_ge(rot_step.sem, n)
                    f = kw[:, 512 // dk * c:512 // dk * (c + 1)].unsqueeze(2).to_broadcast([P, 512 // dk, dk])
                    nc.vector.tensor_tensor(dst.rearrange("p (h i) -> p h i", i=dk),
                                            rot[:, 0, r % 2, :].rearrange("p (h i) -> p h i", i=dk), f, ALU.mult).then_inc(rotated, 1)
                else:
                    nc.vector.tensor_tensor(dst, rot[:, 0, r % 2, :], rot[:, 1, r % 2, :], ALU.add).then_inc(rotated, 1)

            for s, n in loaded:
                dve.wait_ge(s, n)
            for r in range(len(rot_jobs)):
                rotate(r)
                if r == 1:
                    for a in range(TA):
                        j = v_jobs[a]
                        dve.wait_ge(proj_done, j + 1)
                        if bias is not None:
                            nc.vector.tensor_tensor(vtok[:, a, :], bank[:, j % 4, :], bias["v"], ALU.add).then_inc(v_copied, 1)
                        else:
                            nc.vector.tensor_copy(vtok[:, a, :], bank[:, j % 4, :]).then_inc(v_copied, 1)

            def mask_max(n):
                dve.wait_ge(s_ready, n + 1)
                if n >= SR:
                    dve.wait_ge(p_turned, n - SR + 1)
                if n >= 2:
                    dve.wait_ge(exp_done, 2 * n - 2)
                for a, cols in enumerate((slice(0, P), slice(P, 3 * P))):
                    nc.vector.tensor_tensor_reduce(soft[:, n % SR, cols], bank[:, n % 2, cols], g.causal[:, cols], -1.0, HIGHEST,
                                                   ALU.add, ALU.min, nmax[:, n % 2, a:a + 1]).then_inc(maxed, 1)

            def invert(n):
                dve.wait_ge(exp_done, 2 * n + 2)
                nc.vector.reciprocal(rden[:, n % 2, :], denom[:, n % 2, :]).then_inc(inverted, 1)
                dve.wait_ge(inverted, n + 1)
                nc.vector.tensor_scalar(soft[:, n % SR, 0:P], soft[:, n % SR, 0:P], rden[:, n % 2, 0:1], None, ALU.mult)
                nc.vector.tensor_scalar(soft[:, n % SR, P:3 * P], soft[:, n % SR, P:3 * P], rden[:, n % 2, 1:2], None,
                                        ALU.mult).then_inc(normed, 1)

            def rest_ao(q):
                dve.wait_ge(ao_hi, q + 1)
                nc.vector.tensor_tensor(aolo[:, q, :], bank[:, 4 + q % 2, 0:T], aohi[:, q, :].bitcast(F32),
                                        ALU.subtract).then_inc(ao_lo, 1)

            for n in range(heads + SR + 2):
                if n < heads:
                    mask_max(n)
                if 0 <= n - 1 < heads:
                    invert(n - 1)
                if 0 <= n - SR - 1 < heads and (n - SR - 1) % per == per - 1:
                    rest_ao((n - SR - 1) // per)
            if bias is not None:
                for a in range(TA):
                    link(nc.vector.tensor_tensor(X[:, a, :], X[:, a, :], bias["o"], ALU.add))
            for a in range(TA):
                dve.wait_ge(out_done, a + 1)
                link(nc.vector.tensor_tensor(X[:, a, :], X[:, a, :], bank[:, 6 + a, :], ALU.add))

        @block.gpsimd
        def _(pool):
            for s, n in wo_loaded:
                pool.wait_ge(s, n)
            pool.wait_ge(proj_done, len(jobs))
            for c in range(OC):
                part = slice(4 * c, 4 * c + 4)
                nc.gpsimd.tensor_copy(wo_high[:, part, :], w["o"][:, part, :]).then_inc(wo_hi, 1)
                pool.wait_ge(wo_hi, c + 1)
                nc.gpsimd.tensor_tensor(wo_rest[:, part, :], w["o"][:, part, :], wo_high[:, part, :].bitcast(F32),
                                        ALU.subtract).then_inc(wo_lo, 1)

        @block.scalar
        def _(act):
            norm_act(g, act, k)
            norm_turn_act(g, act, k)
            for r in range(len(rot_jobs)):
                kind, c, a = jobs[rot_jobs[r]]
                act.wait_ge(turned, r + 1)
                dst = kT if kind == "k" else qT
                nc.scalar.copy(dst[:, 4 * c:4 * c + 4, a * P:a * P + P],
                               bank[:, 4 + r % 2, :].rearrange("p (f t) -> p f t", f=4)).then_inc(turn_copied, 1)

            def exps(n):
                act.wait_ge(maxed, 2 * n + 2)
                if n >= 2:
                    act.wait_ge(inverted, n - 1)
                for a, cols in enumerate((slice(0, P), slice(P, 3 * P))):
                    nc.scalar.activation(soft[:, n % SR, cols], soft[:, n % SR, cols], ACT.Exp, scale=-1.0, bias=nmax[:, n % 2, a:a + 1],
                                         accum_out=denom[:, n % 2, a:a + 1]).then_inc(exp_done, 1)

            def copy_turned(n):
                act.wait_ge(p_turned, n + 1)
                if n >= 2:
                    act.wait_ge(pv_done, n - 1)
                nc.scalar.copy(turned_sb[:, n % 2, :], bank[:, 2 + n % 2, 0:3 * P]).then_inc(pt_copied, 1)

            def high_ao(q):
                act.wait_ge(pv_done, per * q + per)
                nc.scalar.copy(aohi[:, q, :], bank[:, 4 + q % 2, 0:T]).then_inc(ao_hi, 1)

            for n in range(heads + SR + 1):
                if n < heads:
                    exps(n)
                if 0 <= n - SR + 1 < heads:
                    copy_turned(n - SR + 1)
                if 0 <= n - SR < heads and (n - SR) % per == per - 1:
                    high_ao((n - SR) // per)


def experts(g, k, name, E, width, choose, gate_w, gate_loaded, raw, raw_loaded, wall, cb, parts_at, hi_at, lo_at, AHEAD,
            first_loads, later_loads):
    nc, sem, bank, X = g.nc, g.sem, g.bank, g.X
    rows = [min(P, width - u * P) for u in range(-(-width // P))]
    U = len(rows)
    N = E + 2
    WU = 2 * DC * P + D

    at = lambda kib, what, shape, dt=F32: g.area.at(kib, f"{name}_{what}", shape, dt)
    hi = [at(s, f"hi{n}", [P, U, WU], F32R) for n, s in enumerate(hi_at)]
    lo = [at(s, f"lo{n}", [P, U, WU], F32R) for n, s in enumerate(lo_at)]
    R = len(hi)
    silu = at(parts_at, "silu", [P, 4, T])
    acts = at(parts_at + 4, "acts", [P, 2, T])
    ahi = at(parts_at + 6, "ahi", [P, 4, T], F32R)
    alo = at(parts_at + 10, "alo", [P, 4, T], F32R)
    xhi = at(parts_at + 14, "xhi", [P, DC, T], F32R)
    xlo = at(parts_at + 18, "xlo", [P, DC, T], F32R)
    gates = Gates()
    gates.z = at(parts_at + 22, "z", [P, TA, E])
    gates.s = at(parts_at + 22.25, "s", [P, TA, E])
    gates.c = at(parts_at + 22.5, "c", [P, TA, E])
    gates.t = at(parts_at + 22.75, "t", [P, TA, E])
    gates.r = at(parts_at + 23, "r", [P, TA, E])
    gates.g8 = at(parts_at + 23.25, "g8", [P, TA, 8])
    gates.m = at(parts_at + 23.375, "m", [P, TA, 8])
    gates.one = at(parts_at + 23.5, "one", [P, TA, 1])
    gates.gt = at(0, "gt", [P, TA, E])
    gates.eq = at(0.25, "eq", [P, TA, E])
    gates.pre = at(0.5, "pre", [P, TA, E])
    gates.m8 = at(0.75, "m8", [P, TA, 8])
    cT = at(parts_at + 23.625, "cT", [E, T])
    cscratch = nc.dram_tensor(name + "_cscratch", [E, T], F32, kind="Internal").ap()

    z_ready = sem(name + "_z_ready")
    gate_exp = sem(name + "_gate_exp")
    gate_in = sem(name + "_gate_in")
    c_ready = sem(name + "_c_ready")
    c_turned = sem(name + "_c_turned")
    c_copied = sem(name + "_c_copied")
    c_stored = sem(name + "_c_stored")
    c_first = sem(name + "_c_first")
    c_spread = sem(name + "_c_spread")
    x_hi = sem(name + "_x_hi")
    x_lo = sem(name + "_x_lo")
    w_hi = sem(name + "_w_hi")
    w_lo = sem(name + "_w_lo")
    gu_ready = sem(name + "_gu_ready")
    silu_ready = sem(name + "_silu_ready")
    weighted = sem(name + "_weighted")
    act_made = sem(name + "_act_made")
    act_hi = sem(name + "_act_hi")
    act_ready = sem(name + "_act_ready")
    down_done = sem(name + "_down_done")

    def over_units(eng, step):
        for n in range(2):
            for j in range(U):
                step(n, n, j)
        for n in range(2, 6):
            for j in range(U):
                step(n, n % 4, j)
        if E > 8:
            with eng.Fori(1, E // 4 - 1) as i:
                for s in range(2, 6):
                    for j in range(U):
                        step(i * 4 + s, s % 4, j)
        for n in range(N - 4, N):
            for j in range(U):
                step(n, n % 4, j)

    def place(s, j):
        return (U * s + j) % 4

    def later(n, s, j, d):
        q, jj = divmod(j + d, U)
        if isinstance(n, int) and n + q >= N:
            return None
        return n + q, (s + q) % 4, jj

    def cut_high(act, n, s, j):
        if j == 0:
            act.wait_ge(raw_loaded[s % 2], (n - s % 2) * 8 + 16)
        if not (isinstance(n, int) and n < R):
            act.wait_ge(down_done, (n - R) * U + (j + 1))
        nc.scalar.copy(hi[s % R][:, j, :], raw[s % 2][:, j, :]).then_inc(w_hi, 1)

    def cut_rest(dve, n, s, j):
        dve.wait_ge(w_hi, n * U + (j + 1))
        nc.vector.tensor_tensor(lo[s % R][:, j, :], raw[s % 2][:, j, :], hi[s % R][:, j, :].bitcast(F32),
                                ALU.subtract).then_inc(w_lo, 1)

    with nc.Block() as block:

        def spread_c(sp):
            sp.wait_ge(c_copied, 1)
            sp.dma_start(cscratch, cT[:, :]).then_inc(c_stored, 16)
            sp.wait_ge(c_stored, 16)
            for lo_e, hi_e, s in ((0, 4, c_first), (4, E, c_spread)):
                sp.dma_start(cb[:, lo_e:hi_e, :].rearrange("p e t -> p (e t)"),
                             cscratch[lo_e:hi_e].rearrange("e t -> (e t)").partition_broadcast(P)).then_inc(s, 16)

        @block.sync
        def _(sp):
            first_loads(sp)
            for n in range(2, N):
                if n == 4:
                    spread_c(sp)
                sp.wait_ge(w_lo, U * (n - 1))
                sp.dma_start(raw[n % 2][:, :, :].rearrange("p u w -> p (u w)"), wall[n]).then_inc(raw_loaded[n % 2], 16)
            if later_loads:
                later_loads(sp)

        @block.tensor
        def _(pe):
            norm_turn_pe(g, pe, k)
            pe.wait_ge(g.xnT_ready, TA * k)
            for s, n in gate_loaded:
                pe.wait_ge(s, n)
            for a in range(TA):
                for d in range(DC):
                    ins = nc.tensor.matmul(bank[:, 6, a * E:a * E + E], g.xnT[:, d, a * P:a * P + P], gate_w[:, d, :],
                                           start=d == 0, stop=d == DC - 1)
            ins.then_inc(z_ready, 1)
            pe.wait_ge(x_lo, 1)

            def down(n, s, j, last=False):
                u, r = n * U + j, rows[j]
                b = place(s, j)
                dn = 2 * DC * P
                pe.wait_ge(act_ready, u + 1)
                for a in range(TA):
                    for p, (l, w) in enumerate(((ahi, hi[s % R]), (alo, hi[s % R]), (ahi, lo[s % R]))):
                        ins = nc.tensor.matmul(bank[:, 4 + a, :], l[0:r, b, a * P:a * P + P], w[0:r, j, dn:dn + D],
                                               start=isinstance(n, int) and n == 0 and j == 0 and p == 0, stop=last and p == 2,
                                               skip_group_check=True)
                ins.then_inc(down_done, 1)

            def step(n, s, j):
                b, u, r = place(s, j), n * U + j, rows[j]
                pe.wait_ge(w_lo, u + 1)
                if not (isinstance(n, int) and u < 4):
                    pe.wait_ge(act_made, u - 3)
                for m in range(2):
                    for d in range(DC):
                        c = (m * DC + d) * P
                        for p, (w, xs) in enumerate(((hi[s % R], xhi), (hi[s % R], xlo), (lo[s % R], xhi))):
                            ins = nc.tensor.matmul(bank[0:r, b, m * T:m * T + T], w[:, j, c:c + r], xs[:, d, :],
                                                   start=d == 0 and p == 0, stop=d == DC - 1 and p == 2)
                ins.then_inc(gu_ready, 1)
                if isinstance(n, int) and u == AHEAD - 2:
                    pe.wait_ge(c_ready, 1)
                    for a in range(TA):
                        ins = nc.tensor.transpose(bank[0:E, 7, a * P:a * P + P], gates.c[:, a, :], g.ident[:, :])
                    ins.then_inc(c_turned, 1)
                if j >= 2:
                    down(n, s, j - 2)
                elif not (isinstance(n, int) and n == 0):
                    down(n - 1, (s - 1) % 4, U - 2 + j)

            over_units(pe, step)
            down(N - 1, (N - 1) % 4, U - 2)
            down(N - 1, (N - 1) % 4, U - 1, last=True)

        @block.scalar
        def _(act):
            for d in range(AHEAD):
                cut_high(act, *later(0, 0, 0, d))
            norm_act(g, act, k)
            norm_turn_act(g, act, k)
            act.wait_ge(g.xnT_ready, TA * k)
            nc.scalar.copy(xhi[:, :, :], g.xnT[:, :, :]).then_inc(x_hi, 1)
            if choose == "softmax":
                act.wait_ge(gate_in, 1)
                nc.scalar.activation(gates.s[:, :, :], gates.t[:, :, :], ACT.Exp).then_inc(gate_exp, 1)
            else:
                act.wait_ge(z_ready, 1)
                nc.scalar.activation(gates.s[:, :, :], bank[:, 6, 0:TA * E].rearrange("p (a e) -> p a e", a=TA), ACT.Exp,
                                     scale=-1.0).then_inc(gate_exp, 1)

            def step(n, s, j):
                b, u, r = place(s, j), n * U + j, rows[j]
                act.wait_ge(gu_ready, u + 1)
                if not (isinstance(n, int) and u < 4):
                    act.wait_ge(act_made, u - 3)
                nc.scalar.activation(silu[0:r, b, :], bank[0:r, b, 0:T], ACT.Silu).then_inc(silu_ready, 1)
                act.wait_ge(act_made, u + 1)
                if not (isinstance(n, int) and u < 4):
                    act.wait_ge(down_done, u - 3)
                nc.scalar.copy(ahi[0:r, b, :], acts[0:r, b % 2, :]).then_inc(act_hi, 1)
                if later(n, s, j, AHEAD):
                    cut_high(act, *later(n, s, j, AHEAD))

            over_units(act, step)

        @block.vector
        def _(dve):
            def link(ins):
                dve.wait_ge(g.dve_step.sem, g.dve_step.inc(ins))

            norm_dve(g, dve, k, link)
            dve.wait_ge(x_hi, 1)
            nc.vector.tensor_tensor(xlo[:, :, :], g.xnT[:, :, :], xhi[:, :, :].bitcast(F32), ALU.subtract).then_inc(x_lo, 1)
            for d in range(AHEAD - 1):
                cut_rest(dve, *later(0, 0, 0, d))
            G = gates

            def gate():
                dve.wait_ge(z_ready, 1)
                if choose == "softmax":
                    link(nc.vector.tensor_copy(G.z[:, :, :], bank[:, 6, 0:TA * E].rearrange("p (a e) -> p a e", a=TA)))
                    link(nc.vector.tensor_reduce(G.one[:, :, :], G.z[:, :, :], AX.X, ALU.max))
                    nc.vector.tensor_tensor(G.t[:, :, :], G.z[:, :, :], G.one[:, :, :].to_broadcast([P, TA, E]),
                                            ALU.subtract).then_inc(gate_in, 1)
                    dve.wait_ge(gate_exp, 1)
                    link(nc.vector.tensor_reduce(G.one[:, :, :], G.s[:, :, :], AX.X, ALU.add))
                    link(nc.vector.reciprocal(G.one[:, :, :], G.one[:, :, :]))
                    link(nc.vector.tensor_tensor(G.s[:, :, :], G.s[:, :, :], G.one[:, :, :].to_broadcast([P, TA, E]), ALU.mult))
                else:
                    dve.wait_ge(gate_exp, 1)
                    link(nc.vector.tensor_copy(G.z[:, :, :], bank[:, 6, 0:TA * E].rearrange("p (a e) -> p a e", a=TA)))
                    link(nc.vector.tensor_scalar(G.s[:, :, :], G.s[:, :, :], 1.0, None, ALU.add))
                    link(nc.vector.reciprocal(G.s[:, :, :], G.s[:, :, :]))

                def keep_top(out, val, n, top):
                    gt, eq, pre = G.gt[:, :, 0:n], G.eq[:, :, 0:n], G.pre[:, :, 0:n]
                    for a in range(TA):
                        link(nc.vector.max(G.m8[:, a, :], val[:, a, :]))
                    least = G.m8[:, :, top - 1:top].to_broadcast([P, TA, n])
                    nc.vector.tensor_tensor(gt, val[:, :, :], least, ALU.is_gt)
                    link(nc.vector.tensor_tensor(eq, val[:, :, :], least, ALU.is_equal))
                    link(nc.vector.tensor_reduce(G.one[:, :, :], gt, AX.X, ALU.add))
                    for a in range(TA):
                        link(nc.vector.tensor_tensor_scan(G.pre[:, a, 0:n], g.ones[:, 0:n], G.eq[:, a, 0:n], 0.0, ALU.mult, ALU.add))
                    link(nc.vector.tensor_tensor(pre, pre, G.one[:, :, :].to_broadcast([P, TA, n]), ALU.add))
                    link(nc.vector.tensor_scalar(pre, pre, top + 0.5, None, ALU.is_lt))
                    link(nc.vector.tensor_tensor(pre, pre, eq, ALU.mult))
                    link(nc.vector.tensor_tensor(out, pre, gt, ALU.add))

                if choose == "softmax":
                    keep_top(G.r[:, :, :], G.z, E, 2)
                    nc.vector.tensor_tensor(G.c[:, :, :], G.s[:, :, :], G.r[:, :, :], ALU.mult).then_inc(c_ready, 1)
                else:
                    link(nc.vector.tensor_reduce(G.g8[:, :, :], G.z[:, :, :].rearrange("p a (g e) -> p a g e", g=8), AX.X, ALU.max))
                    keep_top(G.m[:, :, :], G.g8, 8, 4)
                    z4 = G.z[:, :, :].rearrange("p a (g e) -> p a g e", g=8)
                    link(nc.vector.tensor_scalar(G.g8[:, :, :], G.m[:, :, :], 1.0, 1e30, ALU.subtract, ALU.mult))
                    for op, row in ((ALU.mult, G.m), (ALU.add, G.g8)):
                        for a in range(TA):
                            link(nc.vector.tensor_tensor(z4[:, a], z4[:, a], row[:, a, :].unsqueeze(2).to_broadcast([P, 8, 4]), op))
                    keep_top(G.r[:, :, :], G.z, E, 6)
                    link(nc.vector.tensor_tensor(G.c[:, :, :], G.s[:, :, :], G.r[:, :, :], ALU.mult))
                    link(nc.vector.tensor_reduce(G.one[:, :, :], G.c[:, :, :], AX.X, ALU.add))
                    link(nc.vector.reciprocal(G.one[:, :, :], G.one[:, :, :]))
                    link(nc.vector.tensor_tensor(G.c[:, :, :], G.c[:, :, :], G.one[:, :, :].to_broadcast([P, TA, E]), ALU.mult))
                    nc.vector.tensor_scalar(G.c[:, :, :], G.c[:, :, :], 2.5, None, ALU.mult).then_inc(c_ready, 1)

            gate()
            dve.wait_ge(c_turned, 1)
            nc.vector.tensor_copy(cT[:, :], bank[0:E, 7, 0:T]).then_inc(c_copied, 1)

            def step(n, s, j):
                b, u, r = place(s, j), n * U + j, rows[j]
                shared = isinstance(n, int) and n < 2
                dve.wait_ge(silu_ready, u + 1)
                if not shared:
                    c = cb[0:r, bass.ds(n - 2, 1), :].rearrange("p e t -> p (e t)")
                    nc.vector.tensor_tensor(silu[0:r, b, :], silu[0:r, b, :], c, ALU.mult).then_inc(weighted, 1)
                    dve.wait_ge(weighted, u - (2 * U - 1))
                if not (isinstance(n, int) and u < 2):
                    dve.wait_ge(act_hi, u - 1)
                nc.vector.tensor_tensor(acts[0:r, b % 2, :], silu[0:r, b, :], bank[0:r, b, T:2 * T], ALU.mult).then_inc(act_made, 1)
                if later(n, s, j, AHEAD - 1):
                    cut_rest(dve, *later(n, s, j, AHEAD - 1))
                dve.wait_ge(act_hi, u + 1)
                if not (isinstance(n, int) and u < 4):
                    dve.wait_ge(down_done, u - 3)
                nc.vector.tensor_tensor(alo[0:r, b, :], acts[0:r, b % 2, :], ahi[0:r, b, :].bitcast(F32),
                                        ALU.subtract).then_inc(act_ready, 1)
                if isinstance(n, int) and n == 1 and j == U - 1:
                    dve.wait_ge(c_first, 16)
                if isinstance(n, int) and n == 5 and j == U - 1:
                    dve.wait_ge(c_spread, 16)

            over_units(dve, step)
            dve.wait_ge(down_done, U * N)
            for a in range(TA):
                link(nc.vector.tensor_tensor(X[:, a, :], X[:, a, :], bank[:, 4 + a, :], ALU.add))


def cross_attention_1(g, k, ctxT, ctxT_loaded, ctx_chunks, mask, first_loads, later_loads):
    nc, sem, bank, X = g.nc, g.sem, g.bank, g.X
    at = g.area.at
    M = S2
    MC = M // 512
    MI = M // T
    MP = 4
    pr = at(0, "pr", [P, TA, M])
    mb = at(32, "mb", [P, M])
    mask8 = at(48, "mask8", [P, M], mybir.dt.uint8)
    xhi = at(52, "x1_xhi", [P, DC, T], F32R)
    xlo = at(56, "x1_xlo", [P, DC, T], F32R)
    phi = at(52, "x1_phi", [P, 4, 2, T], F32R)
    plo = at(173, "x1_plo", [P, 4, 2, T], F32R)
    whi = [at(156 + 8 * s, f"x1_whi{s}", [P, 4, 512], F32R) for s in range(2)]
    nat = [at(124 + 8 * c, f"nat{c}", [P, 4, D]) for c in range(4)]
    nat += [ctxT[0], ctxT[1]]
    nat += [at(32 + 8 * c, f"nat{6 + c}", [P, 4, D]) for c in range(2)]
    rest_t = [at(60 + 8 * c, f"x1_rest_t{c}", [P, 4, 512], F32R) for c in range(MC)]
    rest_n = [at(124 + 8 * c, f"x1_rest_n{c}", [P, 4, 512], F32R) for c in range(4)] + rest_t[0:2]
    rest_n += [at(32 + 8 * c, f"x1_rest_n{6 + c}", [P, 4, 512], F32R) for c in range(2)]
    pmx = at(172, "pmx", [P, TA, MC])
    nmx = at(172.25, "nmx", [P, TA])
    sums = at(172.375, "x1_sums", [P, TA, MP])
    den = at(172.5, "cden", [P, TA])
    okay = at(172.75, "okay", [P, 1])
    SC = float(D) ** -0.5
    mask_loaded = sem("mask_loaded")
    nat_loaded = [sem(f"nat_loaded{c}") for c in range(MC)]
    x_hi = sem("x1_x_hi")
    x_lo = sem("x1_x_lo")
    w_hi = sem("x1_w_hi")
    w_lo = sem("x1_w_lo")
    s_ready = sem("x1_s_ready")
    s_masked = sem("x1_s_masked")
    maxed = sem("x1_maxed")
    exp_done = sem("x1_exp_done")
    p_turned = sem("x1_p_turned")
    p_hi = sem("x1_p_hi")
    p_lo = sem("x1_p_lo")
    pv_done = sem("x1_pv_done")

    def chunk(c):
        return (ctxT[c], rest_t[c], ctxT_loaded[c]) if c < MC else (nat[c - MC], rest_n[c - MC], nat_loaded[c - MC])

    with nc.Block() as block:

        @block.sync
        def _(sp):
            sp.dma_start(mask8[:, :], mask.partition_broadcast(P)).then_inc(mask_loaded, 16)
            first_loads(sp)
            for c in range(MC):
                if c in (4, 5):
                    sp.wait_ge(s_ready, TA * (c - 4) + TA)
                if c == 6:
                    sp.wait_ge(s_masked, TA * MC)
                sp.dma_start(nat[c][:, :, :], ctx_chunks[c]).then_inc(nat_loaded[c], 16)
            later_loads(sp)

        @block.tensor
        def _(pe):
            norm_turn_pe(g, pe, k)
            pe.wait_ge(x_lo, 1)
            for c in range(MC):
                pe.wait_ge(w_lo, c + 1)
                for a in range(TA):
                    i = TA * c + a
                    if i >= 4:
                        pe.wait_ge(s_masked, i - 3)
                    for d in range(DC):
                        for n, (l, w) in enumerate(((xhi, whi[c % 2]), (xlo, whi[c % 2]), (xhi, rest_t[c]))):
                            ins = nc.tensor.matmul(bank[:, i % 4, :], l[:, d, a * P:a * P + P], w[:, d, :],
                                                   start=d == 0 and n == 0, stop=d == DC - 1 and n == 2)
                    ins.then_inc(s_ready, 1)

            def turn(i):
                pe.wait_ge(exp_done, TA * (i * MP // MI) + TA)
                if i >= 2:
                    pe.wait_ge(p_lo, i - 1)
                for t in range(2):
                    for a in range(TA):
                        ins = nc.tensor.transpose(bank[:, 4 + i % 2, t * T + a * P:t * T + a * P + P],
                                                  pr[:, a, (2 * i + t) * P:(2 * i + t + 1) * P], g.ident[:, :])
                ins.then_inc(p_turned, 1)

            def read(i):
                c = i // 2
                pe.wait_ge(p_lo, i + 1)
                if i % 2 == 0:
                    pe.wait_ge(w_lo, MC + c + 1)
                for t in range(2):
                    m = 2 * i + t
                    for a in range(TA):
                        cols = slice(a * P, a * P + P)
                        for n, (l, w) in enumerate(((phi, whi[c % 2]), (plo, whi[c % 2]), (phi, rest_n[c]))):
                            ins = nc.tensor.matmul(bank[:, 6 + a, :], l[:, i % 4, t, cols], w[:, m % 4, :],
                                                   start=m == 0 and n == 0, stop=m == 2 * MI - 1 and n == 2)
                ins.then_inc(pv_done, 1)

            for i in range(MI + 1):
                if i < MI:
                    turn(i)
                if i >= 1:
                    read(i - 1)

        @block.vector
        def _(dve):
            def link(ins):
                dve.wait_ge(g.dve_step.sem, g.dve_step.inc(ins))

            def cut_rest(c):
                x, rest, _ = chunk(c)
                dve.wait_ge(w_hi, c + 1)
                nc.vector.tensor_tensor(rest[:, :, :], x[:, :, :], whi[c % 2][:, :, :].bitcast(F32),
                                        ALU.subtract).then_inc(w_lo, 1)

            norm_dve(g, dve, k, link)
            cut_rest(0)
            dve.wait_ge(x_hi, 1)
            nc.vector.tensor_tensor(xlo[:, :, :], g.xnT[:, :, :], xhi[:, :, :].bitcast(F32), ALU.subtract).then_inc(x_lo, 1)
            dve.wait_ge(mask_loaded, 16)
            link(nc.vector.tensor_scalar(mb[:, :], mask8[:, :], 1.0, 1e30, ALU.subtract, ALU.mult))
            cut_rest(1)
            for c in range(MC):
                for a in range(TA):
                    i = TA * c + a
                    dve.wait_ge(s_ready, i + 1)
                    nc.vector.tensor_tensor_reduce(pr[:, a, c * 512:c * 512 + 512], bank[:, i % 4, :], mb[:, c * 512:c * 512 + 512],
                                                   1.0, -HIGHEST, ALU.add, ALU.max, pmx[:, a, c:c + 1]).then_inc(s_masked, 1)
                if c == 3:
                    link(nc.vector.tensor_reduce(okay[:, :], mb[:, :], AX.X, ALU.max))
                    link(nc.vector.tensor_scalar(okay[:, :], okay[:, :], -1.0, None, ALU.is_ge))
                if c < MC - 1:
                    cut_rest(c + 2)
            dve.wait_ge(s_masked, TA * MC)
            link(nc.vector.tensor_reduce(nmx[:, :], pmx[:, :, :], AX.X, ALU.max))
            nc.vector.tensor_scalar(nmx[:, :], nmx[:, :], -SC, None, ALU.mult).then_inc(maxed, 1)
            for i in range(MI):
                dve.wait_ge(p_hi, i + 1)
                nc.vector.tensor_tensor(plo[:, i % 4].rearrange("p t n -> p (t n)"), bank[:, 4 + i % 2, :],
                                        phi[:, i % 4].rearrange("p t n -> p (t n)").bitcast(F32), ALU.subtract).then_inc(p_lo, 1)
                if i == 0:
                    cut_rest(MC + 1)
                elif i % 2 and 3 <= i < MI - 1:
                    cut_rest(MC + (i + 1) // 2)
            link(nc.vector.tensor_reduce(den[:, :], sums[:, :, :], AX.X, ALU.add))
            link(nc.vector.reciprocal(den[:, :], den[:, :]))
            link(nc.vector.tensor_scalar(den[:, :], den[:, :], okay[:, 0:1], None, ALU.mult))
            dve.wait_ge(pv_done, MI)
            for a in range(TA):
                link(nc.vector.scalar_tensor_tensor(out=X[:, a, :], in0=bank[:, 6 + a, :], scalar=den[:, a:a + 1],
                                                    in1=X[:, a, :], op0=ALU.mult, op1=ALU.add))

        @block.scalar
        def _(act):
            def cut_high(c):
                x, _, loaded = chunk(c)
                act.wait_ge(loaded, 16)
                if 2 <= c < MC + 2:
                    act.wait_ge(s_ready, TA * (c - 1))
                elif c >= MC + 2:
                    act.wait_ge(pv_done, 2 * (c - MC - 1))
                nc.scalar.copy(whi[c % 2][:, :, :], x[:, :, :]).then_inc(w_hi, 1)

            def exps(q):
                for a in range(TA):
                    cols = slice(q * M // MP, (q + 1) * M // MP)
                    nc.scalar.activation(pr[:, a, cols], pr[:, a, cols], ACT.Exp, scale=SC, bias=nmx[:, a:a + 1],
                                         accum_out=sums[:, a, q:q + 1]).then_inc(exp_done, 1)

            norm_act(g, act, k)
            cut_high(0)
            norm_turn_act(g, act, k)
            act.wait_ge(g.xnT_ready, TA * k)
            nc.scalar.copy(xhi[:, :, :], g.xnT[:, :, :]).then_inc(x_hi, 1)
            for c in range(1, MC + 1):
                cut_high(c)
            act.wait_ge(maxed, 1)
            exps(0)
            for i in range(MI):
                act.wait_ge(p_turned, i + 1)
                if i >= 4:
                    act.wait_ge(pv_done, i - 3)
                nc.scalar.copy(phi[:, i % 4].rearrange("p t n -> p (t n)"), bank[:, 4 + i % 2, :]).then_inc(p_hi, 1)
                if i == 0:
                    cut_high(MC + 1)
                    exps(1)
                elif i % 2 and 3 <= i < MI - 1:
                    cut_high(MC + (i + 1) // 2)
                if i in (3, 6):
                    exps(2 + i // 6)


H0, K0 = 16, 32
H1, K1, KV1 = 32, 64, 8
E0, I0 = 32, 256
E1, I1 = 8, 352
BIAS = 512 + 512 + 2048 + D


def perceiver(nc, ins, out):
    with ExitStack() as ctx:
        g = setup(nc, ctx)
        sem, at = g.sem, g.area.at

        def sb(name, shape, dt=F32):
            return ctx.enter_context(nc.sbuf_tensor(name, shape, dt))

        g.causal = sb("causal_mask", [P, 3 * P])
        g.ones = sb("ones_row", [P, E0])
        table0 = sb("rope0", [P, 2, TA, 2, K0])
        table1 = sb("rope1", [P, 2, TA, 2, K1])
        gate0 = sb("gate0_w", [P, DC, E0])
        gate1 = sb("gate1_w", [P, DC, E1])
        kw1 = sb("kw1_row", [P, H1])
        small_loaded = sem("small_loaded")
        w_attn0 = at(0, "w_attn0_sb", [P, 4, DC, D])
        w_attn0_loaded = sem("w_attn0_loaded")
        raw0 = [at(kib, f"raw0_{s}", [P, I0 // P, 2 * DC * P + D]) for s, kib in enumerate((156, 168))]
        raw0_loaded = [sem(f"raw0_loaded{s}") for s in range(2)]
        cb0 = at(0, "cb0", [P, E0, T])
        ctxT = [at(60 + 8 * c, f"ctxT{c}", [P, DC, 512]) for c in range(8)]
        ctxT_loaded = [sem(f"ctxT_loaded{c}") for c in range(8)]
        wq1 = at(76, "wq1_sb", [P, DC, 2048])
        wk1 = at(108, "wk1_sb", [P, DC, 512])
        wv1 = at(116, "wv1_sb", [P, DC, 512])
        wo1 = at(130, "wo1_sb", [P, 16, D])
        qkv1_loaded = sem("qkv1_loaded")
        wo1_loaded = sem("wo1_loaded")
        bias1_loaded = sem("bias1_loaded")
        bias1 = at(62, "bias1_row", [P, BIAS])
        raw1 = [at(kib, f"raw1_{s}", [P, -(-I1 // P), 2 * DC * P + D]) for s, kib in enumerate((162, 76))]
        raw1_loaded = [sem(f"raw1_loaded{s}") for s in range(2)]
        cb1 = at(0, "cb1", [P, E1, T])

        def loads_a(sp):
            for dst, src in ((g.causal[:, :], ins["causal"]), (g.ones[:, :], ins["ones"].partition_broadcast(P)),
                             (table0[:, :, :, :, :], ins["table0"]), (table1[:, :, :, :, :], ins["table1"]), (gate0[:, :, :], ins["gate0"]),
                             (gate1[:, :, :], ins["gate1"]), (kw1[:, :], ins["kw1"].partition_broadcast(P))):
                sp.dma_start(dst, src).then_inc(small_loaded, 16)
            sp.dma_start(w_attn0[:, :, :, :], ins["w_attn0"]).then_inc(w_attn0_loaded, 16)

        def loads_b(sp):
            for n in range(2):
                sp.dma_start(raw0[n][:, :, :].rearrange("p u w -> p (u w)"), ins["wall0"][n]).then_inc(raw0_loaded[n], 16)

        def first_d(sp):
            for c in range(8):
                sp.dma_start(ctxT[c][:, :, :], ins["ctxT"][c]).then_inc(ctxT_loaded[c], 16)

        def loads_d(sp):
            sp.dma_start(wk1[:, :, :], ins["wk1"]).then_inc(qkv1_loaded, 16)
            sp.dma_start(wv1[:, :, :], ins["wv1"]).then_inc(qkv1_loaded, 16)
            sp.dma_start(wq1[:, :, :], ins["wq1"]).then_inc(qkv1_loaded, 16)

        def load_raw1(sp, n):
            sp.dma_start(raw1[n][:, :, :].rearrange("p u w -> p (u w)"), ins["wall1"][n]).then_inc(raw1_loaded[n], 16)

        def loads_e(sp):
            sp.dma_start(bias1[:, :], ins["bias1"].partition_broadcast(P)).then_inc(bias1_loaded, 16)
            sp.dma_start(wo1[:, :, :], ins["wo1"]).then_inc(wo1_loaded, 16)
            load_raw1(sp, 0)

        def later_e(sp):
            load_raw1(sp, 1)

        smalls = (small_loaded, 16 * 7)
        cross_attention_0(g, ins["x"], ins["ctx_rows"], ins["ctx_vt"], loads_a)
        self_attention(g, 1, "a0", H0, K0, 4, lambda n: n // 4, lambda n: K0 * n, True,
                   {"q": w_attn0[:, 0], "k": w_attn0[:, 1], "v": w_attn0[:, 2], "o": w_attn0[:, 3]},
                   at(0, "wo0_high", [P, 4, D], F32R), at(24, "wo0_rest", [P, 4, D], F32R),
                   {"q": table0[:, 0], "k": table0[:, 1]}, None, None, lambda kib, n, s, dt=F32: at(32 + kib, n, s, dt),
                   [smalls, (w_attn0_loaded, 16)], [(w_attn0_loaded, 16)], loads_b, None)
        experts(g, 2, "e0", E0, I0, "sigmoid", gate0, [smalls], raw0, raw0_loaded, ins["wall0"], cb0, 32,
                (57, 69, 81, 93), (105, 117, 129, 141), 4, lambda sp: None, None)
        cross_attention_1(g, 3, ctxT, ctxT_loaded, ins["ctx_chunks"], ins["mask"], first_d, loads_d)
        b = bias1[:, :]
        self_attention(g, 4, "a1", H1, K1, 16, lambda n: n // 8, lambda n: K1 * (2 * (n // 8) + n % 2), False,
                   {"q": wq1, "k": wk1, "v": wv1, "o": wo1},
                   at(94, "wo1_high", [P, 16, D], F32R), at(130, "wo1_rest", [P, 16, D], F32R), {"q": table1[:, 0], "k": table1[:, 1]}, kw1,
                   {"k": b[:, 0:512], "v": b[:, 512:1024], "q": b[:, 1024:3072], "o": b[:, 3072:]},
                   lambda kib, n, s, dt=F32: at(kib, n, s, dt), [smalls, (bias1_loaded, 16), (qkv1_loaded, 48)],
                   [(wo1_loaded, 16)], loads_e, later_e)
        experts(g, 5, "e1", E1, I1, "softmax", gate1, [smalls], raw1, raw1_loaded, ins["wall1"], cb1, 8,
                (33, 51), (94, 112), 3, lambda sp: None, None)
        out_stored = sem("out_stored")
        with nc.Block() as block:
            @block.sync
            def _(sp):
                sp.dma_start(out.rearrange("(a p) d -> p a d", p=P), g.X[:, :, :]).then_inc(out_stored, 16)
                sp.wait_ge(out_stored, 16)


def kernel(**inputs):
    import numpy as np
    import concourse.bacc as bacc
    from concourse.bass_utils import run_bass_kernel_spmd

    nc = bacc.Bacc("TRN2", target_bir_lowering=False, num_devices=1)
    c = np.ascontiguousarray
    v = {n: c(a) for n, a in inputs.items()}

    def inner_first(wT, n):
        s = wT.shape
        return c(np.moveaxis(wT.reshape(s[:-2] + (n, P, s[-1])), -3, -2))

    def rope(dim, base, repeat, scale):
        f32 = np.float32
        i = np.arange(dim // 2)
        inv = (base ** (-2.0 * i / dim)).astype(f32) if repeat else (1.0 / (base ** (2.0 * i / dim)).astype(f32)).astype(f32)
        ang = (np.arange(T, dtype=f32)[:, None] * inv[None, :]).astype(np.float64)
        cos, sin = np.cos(ang), np.sin(ang)
        if repeat:
            cs, sn = np.repeat(cos, 2, axis=-1), np.stack([-sin, sin], axis=-1).reshape(T, dim)
        else:
            cs, sn = np.concatenate([cos, cos], -1), np.concatenate([-sin, sin], -1)
        t = np.stack([cs, sn], 1)
        t = np.stack([t * scale, t], 0).astype(f32)
        return c(t.reshape(2, TA, P, 2, dim).transpose(2, 0, 1, 3, 4))

    def all_experts(gate, up, down, width):
        n, U = gate.shape[0], -(-width // P)
        out = np.zeros((n, P, U, 2 * DC * P + D), down.dtype)
        for m, w in enumerate((gate, up)):
            wide = np.zeros((n, D, U * P), w.dtype)
            wide[:, :, :width] = w
            out[..., m * DC * P:(m + 1) * DC * P] = wide.reshape(n, DC, P, U, P).transpose(0, 2, 3, 1, 4).reshape(n, P, U, DC * P)
        deep = np.zeros((n, U * P, D), down.dtype)
        deep[:, :width] = down
        out[..., 2 * DC * P:] = deep.reshape(n, U, P, D).transpose(0, 2, 1, 3)
        return c(out.reshape(n, P, -1))

    halves = lambda w: w.reshape(D, 2, -1).transpose(1, 0, 2)
    order = [4 * (2 * p + r) + m for p in range(KV1 // 2) for m in range(4) for r in range(2)]
    ctx = v["ctx_2048"]
    tri = np.where(np.tril(np.ones((P, P), bool)), np.float32(0), np.float32(-1e30)).astype(np.float32)
    Wq = v["L1_attn_Wq"].reshape(H1, K1, D)[order].reshape(H1 * K1, D)
    Wo = v["L1_attn_Wo"].reshape(D, H1, K1)[:, order].reshape(D, H1 * K1)
    arrays = {
        "x": v["x"].reshape(T, D),
        "ctx_rows": ctx.reshape(XH, P, 1024),
        "ctx_vt": c(ctx.reshape(XH, XC, XT, P).transpose(0, 3, 2, 1)),
        "ctxT": c(ctx.reshape(8, 512, DC, P).transpose(0, 3, 2, 1)),
        "ctx_chunks": c(ctx.reshape(8, 4, P, D).transpose(0, 2, 1, 3)),
        "mask": v["mask_BxS2_bk0"].reshape(S2),
        "causal": np.concatenate([tri, np.zeros((P, P), np.float32), tri], axis=1),
        "ones": np.ones(E0, np.float32),
        "table0": rope(K0, 10000.0, True, float(K0) ** -0.5),
        "table1": rope(K1, 10000.0, False, float(K1) ** -0.5),
        "gate0": inner_first(v["L0_ffn_gate_w"].T, DC),
        "gate1": inner_first(v["L1_ffn_gate_w"], DC),
        "kw1": c(v["L1_attn_key_weights"][order]),
        "bias1": c(np.concatenate([v["L1_attn_bk"], v["L1_attn_bv"], v["L1_attn_bq"].reshape(H1, K1)[order].reshape(-1),
                                   v["L1_attn_bo"]])),
        "w_attn0": c(np.stack([inner_first(v["L0_attn_" + n].T, DC) for n in ("wq", "wk", "wv", "wo")], axis=1)),
        "wk1": inner_first(v["L1_attn_Wk"].T, DC),
        "wv1": inner_first(v["L1_attn_Wv"].T, DC),
        "wq1": inner_first(Wq.T, DC),
        "wo1": inner_first(Wo.T, 16),
        "wall0": all_experts(np.concatenate([halves(v["L0_ffn_sw1"].T), v["L0_ffn_w11"].transpose(0, 2, 1)]),
                             np.concatenate([halves(v["L0_ffn_sw3"].T), v["L0_ffn_w33"].transpose(0, 2, 1)]),
                             np.concatenate([v["L0_ffn_sw2"].T.reshape(2, I0, D), v["L0_ffn_w22"].transpose(0, 2, 1)]), I0),
        "wall1": all_experts(np.concatenate([halves(v["L1_ffn_sw_gate"]), v["L1_ffn_w_gate"]]),
                             np.concatenate([halves(v["L1_ffn_sw_up"]), v["L1_ffn_w_up"]]),
                             np.concatenate([v["L1_ffn_sw_down"].reshape(2, I1, D), v["L1_ffn_w_down"]]), I1),
    }
    ins = {n: nc.dram_tensor(n, a.shape, mybir.dt.from_np(a.dtype), kind="ExternalInput").ap() for n, a in arrays.items()}
    out = nc.dram_tensor("out", (T, D), F32, kind="ExternalOutput").ap()
    perceiver(nc, ins, out)
    r = run_bass_kernel_spmd(nc, [arrays], core_ids=[0])
    return r.results[0]["out"].reshape(1, T, D)
```
